# Optimizing a Trainium2 kernel written in Bass

```python
import numpy as np
import jax
import jax.numpy as jnp

def _softmax(x, axis=-1):
    return jax.nn.softmax(x, axis=axis)

def _gelu(x):
    return jax.nn.gelu(x, approximate=True)

def _silu(x):
    return jax.nn.silu(x)

def _sigmoid(x):
    return jax.nn.sigmoid(x)

def _layernorm(x, axis=-1, eps=1e-05):
    m = jnp.mean(x, axis=axis, keepdims=True)
    v = jnp.var(x, axis=axis, keepdims=True)
    return (x - m) / jnp.sqrt(v + eps)

def _scatter_add(tgt, idx, src, axis=0):
    return tgt.at[idx].add(src)

def _segment_sum(src, seg, n):
    return jax.ops.segment_sum(src, seg, n)
kernel_name = 'mk_seq_postln_d4_jaxref_r8_89b6f9'

def setup_inputs(seed: int=0):
    np.random.seed(seed)
    _w = jnp.asarray

    def _L0_attn_setup():
        import jax, jax.numpy as jnp
        import numpy as np
        N_EMBD = 128
        N_HEAD = 16
        HORIZON = 64
        HS = N_EMBD // N_HEAD
        BD = max(HS // 4, 16)

        def _windows(t, delta):
            B, nh, T, D = t.shape
            padded = jnp.pad(t, ((0, 0), (0, 0), (delta - 1, 0), (0, 0)))
            idx = jnp.arange(T)[:, None] + jnp.arange(delta)[None, :]
            return padded[:, :, idx]
        key = jax.random.key(seed)
        ks = jax.random.split(key, 12)
        s = 0.02
        B, T = (2, 128)
        return {'x': jax.random.normal(ks[0], (B, T, N_EMBD), jnp.float32), 'W_disp': jax.random.normal(ks[1], (N_EMBD, N_HEAD * BD), jnp.float32) * s, 'W_val': jax.random.normal(ks[2], (N_EMBD, N_EMBD), jnp.float32) * s, 'rel_pos_emb': jax.random.normal(ks[3], (HORIZON, BD), jnp.float32) * s, 'W_strain': jax.random.normal(ks[4], (BD, BD), jnp.float32) * s, 'W_pos': jax.random.normal(ks[5], (BD, BD), jnp.float32) * s, 'W_bond': jax.random.normal(ks[6], (BD, 1), jnp.float32) * s, 'W_dmg': jax.random.normal(ks[7], (BD, BD), jnp.float32) * s, 'b_dmg': jnp.zeros((BD,), jnp.float32), 'W_dmg_out': jax.random.normal(ks[8], (BD, 1), jnp.float32) * s, 'b_dmg_out': jnp.full((1,), -3.0, jnp.float32), 'W_cproj': jax.random.normal(ks[9], (N_EMBD, N_EMBD), jnp.float32) * s}
    _L0_attn_in = _L0_attn_setup()

    def _L0_ffn_setup():
        import jax, jax.numpy as jnp
        import numpy as np
        B, S, D = (2, 128, 128)
        E, K, F, FS = (8, 2, 64, 128)
        key = jax.random.key(seed)
        ks = jax.random.split(key, 9)
        s = lambda k, shape, fan: jax.random.normal(k, shape, jnp.float32) * fan ** (-0.5)
        return {'x': jax.random.normal(ks[0], (B, S, D), jnp.float32), 'Wr': s(ks[1], (D, E), D), 'Wg': s(ks[2], (E, D, F), D), 'Wu': s(ks[3], (E, D, F), D), 'Wd': s(ks[4], (E, F, D), F), 'Sg': s(ks[5], (D, FS), D), 'Su': s(ks[6], (D, FS), D), 'Sd': s(ks[7], (FS, D), FS), 'expert_bias': jnp.zeros((E,), jnp.float32)}
    _L0_ffn_in = _L0_ffn_setup()

    def _L1_attn_setup():
        import jax, jax.numpy as jnp
        import numpy as np
        D_MODEL = 128
        N_HEADS = 16
        key = jax.random.key(seed)
        k1, k2, k3, k4 = jax.random.split(key, 4)
        B, T, D = (4, 256, D_MODEL)
        x = jax.random.normal(k1, (B, T, D), dtype=jnp.float32)
        w_qkv = jax.random.normal(k2, (D, 3 * D), dtype=jnp.float32) / np.sqrt(D)
        w_out = jax.random.normal(k3, (D, D), dtype=jnp.float32) / np.sqrt(D)
        b_out = jax.random.normal(k4, (D,), dtype=jnp.float32) * 0.01
        return {'x': x, 'w_qkv': w_qkv, 'w_out': w_out, 'b_out': b_out}
    _L1_attn_in = _L1_attn_setup()

    def _L1_ffn_setup():
        import jax, jax.numpy as jnp
        import numpy as np
        HIDDEN_SIZE = 128
        NUM_EXPERTS = 8
        MOE_INTERMEDIATE_SIZE = 176
        NUM_EXPERTS_PER_TOK = 2
        SHARED_EXPERT_INTERMEDIATE_SIZE = 352
        B, T = (2, 128)
        W_SCALE = 0.02
        key = jax.random.key(seed)
        ks = jax.random.split(key, 8)
        H, E, I, SI = (HIDDEN_SIZE, NUM_EXPERTS, MOE_INTERMEDIATE_SIZE, SHARED_EXPERT_INTERMEDIATE_SIZE)
        return {'x': jax.random.normal(ks[0], (B, T, H), jnp.float32), 'gate_w': jax.random.normal(ks[1], (E, H), jnp.float32) * W_SCALE, 'experts_gate_up': jax.random.normal(ks[2], (E, 2 * I, H), jnp.float32) * W_SCALE, 'experts_down': jax.random.normal(ks[3], (E, H, I), jnp.float32) * W_SCALE, 'shared_gate_w': jax.random.normal(ks[4], (SI, H), jnp.float32) * W_SCALE, 'shared_up_w': jax.random.normal(ks[5], (SI, H), jnp.float32) * W_SCALE, 'shared_down_w': jax.random.normal(ks[6], (H, SI), jnp.float32) * W_SCALE, 'shared_expert_gate_w': jax.random.normal(ks[7], (1, H), jnp.float32) * W_SCALE}
    _L1_ffn_in = _L1_ffn_setup()

    def _L2_attn_setup():
        import jax, jax.numpy as jnp
        import numpy as np
        EPS = 1e-12

        def _l2norm(t):
            n = jnp.linalg.norm(t, axis=-1, keepdims=True)
            return t / jnp.maximum(n, EPS)
        key = jax.random.key(seed)
        kx, kq, kk, kv = jax.random.split(key, 4)
        B, N, D = (8, 512, 128)
        s = 1.0 / np.sqrt(D)
        return {'x': jax.random.normal(kx, (B, N, D), dtype=jnp.float32), 'W_q': jax.random.normal(kq, (D, D), dtype=jnp.float32) * s, 'W_k': jax.random.normal(kk, (D, D), dtype=jnp.float32) * s, 'W_v': jax.random.normal(kv, (D, D), dtype=jnp.float32) * s}
    _L2_attn_in = _L2_attn_setup()

    def _L2_ffn_setup():
        import jax, jax.numpy as jnp
        import numpy as np
        E = 32
        K = 4
        H = 128
        I = 96
        ROUTED_SCALING_FACTOR = 1.0
        key = jax.random.key(seed)
        k0, k1, k2, k3, k4, k5 = jax.random.split(key, 6)
        return {'hidden_states': jax.random.normal(k0, (1, 256, H), jnp.float32), 'gate_w': jax.random.normal(k1, (E, H), jnp.float32) * 0.02, 'w1': jax.random.normal(k2, (E, H, I), jnp.float32) * 0.02, 'w3': jax.random.normal(k3, (E, H, I), jnp.float32) * 0.02, 'w2': jax.random.normal(k4, (E, I, H), jnp.float32) * 0.02, 'e_bias': jax.random.normal(k5, (E,), jnp.float32) * 0.02}
    _L2_ffn_in = _L2_ffn_setup()

    def _L3_attn_setup():
        import jax, jax.numpy as jnp
        import numpy as np
        import math
        EMBED_DIM = 128
        NUM_HEADS = 16
        NUM_KV_HEADS = 16
        DEPTH = 12
        HEAD_DIM = EMBED_DIM // NUM_HEADS // 2
        LAMBDA_INIT = 0.8 - 0.6 * math.exp(-0.3 * DEPTH)
        EPS = 1e-05
        THETA = 0.0001

        def rope(q):
            b, s, h, d = q.shape
            pos = jnp.arange(s, dtype=jnp.float32)[:, None]
            freq = 1.0 / THETA ** (2.0 * jnp.arange(d // 2, dtype=jnp.float32) / d)
            ang = pos * freq
            cos = jnp.cos(ang)[None, :, None, :].astype(q.dtype)
            sin = jnp.sin(ang)[None, :, None, :].astype(q.dtype)
            qr = q.reshape(b, s, h, d // 2, 2)
            q0, q1 = (qr[..., 0], qr[..., 1])
            out = jnp.stack([q0 * cos - q1 * sin, q0 * sin + q1 * cos], axis=-1)
            return out.reshape(q.shape)
        key = jax.random.key(seed)
        ks = jax.random.split(key, 10)
        d = EMBED_DIM
        sd = 1.0 / math.sqrt(d)
        return {'x': jax.random.normal(ks[0], (1, 256, d), dtype=jnp.float32), 'Wq': jax.random.normal(ks[1], (d, d), dtype=jnp.float32) * sd, 'Wk': jax.random.normal(ks[2], (d, d), dtype=jnp.float32) * sd, 'Wv': jax.random.normal(ks[3], (d, d), dtype=jnp.float32) * sd, 'Wo': jax.random.normal(ks[4], (d, d), dtype=jnp.float32) * sd, 'lambda_q1': jax.random.normal(ks[5], (HEAD_DIM,), dtype=jnp.float32) * 0.1, 'lambda_k1': jax.random.normal(ks[6], (HEAD_DIM,), dtype=jnp.float32) * 0.1, 'lambda_q2': jax.random.normal(ks[7], (HEAD_DIM,), dtype=jnp.float32) * 0.1, 'lambda_k2': jax.random.normal(ks[8], (HEAD_DIM,), dtype=jnp.float32) * 0.1, 'subln_g': jnp.ones((2 * HEAD_DIM,), dtype=jnp.float32)}
    _L3_attn_in = _L3_attn_setup()

    def _L3_ffn_setup():
        import jax, jax.numpy as jnp
        import numpy as np
        DIM = 128
        DEPTH = 2
        HEADS = 8
        DIM_HEAD = 64
        WINDOW = 64
        INNER = HEADS * DIM_HEAD
        HID = int(DIM * 4 * 2 / 3)
        B, N = (2, 1024)
        QK_SCALE = 8.0

        def shift_token(t):
            t1, t2 = jnp.split(t, 2, axis=-1)
            t2 = jnp.pad(t2, ((0, 0), (1, 0), (0, 0)))[:, :-1]
            return jnp.concatenate([t1, t2], axis=-1)

        def l2norm(t):
            return t / jnp.clip(jnp.linalg.norm(t, axis=-1, keepdims=True), 1e-12)

        def rotate_half(x):
            x1, x2 = jnp.split(x, 2, axis=-1)
            return jnp.concatenate([-x2, x1], axis=-1)

        def rotary_xpos(q, k):
            n = q.shape[-2]
            half_idx = jnp.arange(0, DIM_HEAD, 2, dtype=jnp.float32)
            inv_freq = 1.0 / 10000.0 ** (half_idx / DIM_HEAD)
            t = jnp.arange(n, dtype=jnp.float32)
            freqs = t[:, None] * inv_freq[None, :]
            freqs = jnp.concatenate([freqs, freqs], axis=-1)
            base = (half_idx + 0.4 * DIM_HEAD) / (1.4 * DIM_HEAD)
            power = (t - n // 2) / float(WINDOW // 2)
            scale = base[None, :] ** power[:, None]
            scale = jnp.concatenate([scale, scale], axis=-1)
            cos, sin = (jnp.cos(freqs), jnp.sin(freqs))
            q = q * cos * scale + rotate_half(q) * sin * scale
            k = k * cos / scale + rotate_half(k) * sin / scale
            return (q, k)

        def local_attention(q, k, v):
            b, h, n, d = q.shape
            w = n // WINDOW
            bq = q.reshape(b, h, w, WINDOW, d) * QK_SCALE
            bk = k.reshape(b, h, w, WINDOW, d)
            bv = v.reshape(b, h, w, WINDOW, d)

            def look_around(t):
                p = jnp.pad(t, ((0, 0), (0, 0), (1, 0), (0, 0), (0, 0)))
                return jnp.concatenate([p[:, :, :w], p[:, :, 1:]], axis=3)
            bk, bv = (look_around(bk), look_around(bv))
            bt = jnp.arange(n).reshape(w, WINDOW)
            btp = jnp.pad(bt, ((1, 0), (0, 0)), constant_values=-1)
            btk = jnp.concatenate([btp[:w], btp[1:]], axis=1)
            sim = jnp.einsum('bhwid,bhwjd->bhwij', bq, bk)
            i = bt[:, :, None]
            j = btk[:, None, :]
            mask = (i < j) | (i > j + WINDOW) | (j == -1)
            sim = jnp.where(mask, -jnp.finfo(sim.dtype).max, sim)
            attn = jax.nn.softmax(sim, axis=-1)
            out = jnp.einsum('bhwij,bhwjd->bhwid', attn, bv)
            return out.reshape(b, h, n, d)

        def _layer(x, wqkv, qs, ksc, wo, lg, lb, w1, b1, w2, b2):
            b, n, _ = x.shape
            h = shift_token(x)
            qkv = h @ wqkv
            q, k, v = jnp.split(qkv, 3, axis=-1)
            to_heads = lambda t: t.reshape(b, n, HEADS, DIM_HEAD).transpose(0, 2, 1, 3)
            q, k, v = (to_heads(q), to_heads(k), to_heads(v))
            q = l2norm(q) * qs
            k = l2norm(k) * ksc
            q, k = rotary_xpos(q, k)
            o = local_attention(q, k, v)
            o = o.transpose(0, 2, 1, 3).reshape(b, n, INNER)
            x = x + o @ wo
            h = shift_token(x)
            mu = h.mean(-1, keepdims=True)
            var = h.var(-1, keepdims=True)
            h = (h - mu) / jnp.sqrt(var + 1e-05) * lg + lb
            h = h @ w1 + b1
            a, g = jnp.split(h, 2, axis=-1)
            h = a * jax.nn.gelu(g, approximate=False)
            x = x + h @ w2 + b2
            return x
        key = jax.random.key(seed)
        ks = jax.random.split(key, 6)
        return {'x': jax.random.normal(ks[0], (B, N, DIM), jnp.float32), 'wqkv': jax.random.normal(ks[1], (DEPTH, DIM, 3 * INNER), jnp.float32) * 0.02, 'q_scale': jnp.ones((DEPTH, DIM_HEAD), jnp.float32), 'k_scale': jnp.ones((DEPTH, DIM_HEAD), jnp.float32), 'wo': jax.random.normal(ks[2], (DEPTH, INNER, DIM), jnp.float32) * 0.02, 'ln_g': jnp.ones((DEPTH, DIM), jnp.float32), 'ln_b': jnp.zeros((DEPTH, DIM), jnp.float32), 'w1': jax.random.normal(ks[3], (DEPTH, DIM, 2 * HID), jnp.float32) * 0.02, 'b1': jnp.zeros((DEPTH, 2 * HID), jnp.float32), 'w2': jax.random.normal(ks[4], (DEPTH, HID, DIM), jnp.float32) * 0.02, 'b2': jnp.zeros((DEPTH, DIM), jnp.float32)}
    _L3_ffn_in = _L3_ffn_setup()
    _d = {'L0_attn_x': _L0_attn_in['x'], 'L0_attn_W_disp': _L0_attn_in['W_disp'], 'L0_attn_W_val': _L0_attn_in['W_val'], 'L0_attn_rel_pos_emb': _L0_attn_in['rel_pos_emb'], 'L0_attn_W_strain': _L0_attn_in['W_strain'], 'L0_attn_W_pos': _L0_attn_in['W_pos'], 'L0_attn_W_bond': _L0_attn_in['W_bond'], 'L0_attn_W_dmg': _L0_attn_in['W_dmg'], 'L0_attn_b_dmg': _L0_attn_in['b_dmg'], 'L0_attn_W_dmg_out': _L0_attn_in['W_dmg_out'], 'L0_attn_b_dmg_out': _L0_attn_in['b_dmg_out'], 'L0_attn_W_cproj': _L0_attn_in['W_cproj'], 'L0_ffn_Wr': _L0_ffn_in['Wr'], 'L0_ffn_Wg': _L0_ffn_in['Wg'], 'L0_ffn_Wu': _L0_ffn_in['Wu'], 'L0_ffn_Wd': _L0_ffn_in['Wd'], 'L0_ffn_Sg': _L0_ffn_in['Sg'], 'L0_ffn_Su': _L0_ffn_in['Su'], 'L0_ffn_Sd': _L0_ffn_in['Sd'], 'L0_ffn_expert_bias': _L0_ffn_in['expert_bias'], 'L1_attn_w_qkv': _L1_attn_in['w_qkv'], 'L1_attn_w_out': _L1_attn_in['w_out'], 'L1_attn_b_out': _L1_attn_in['b_out'], 'L1_ffn_gate_w': _L1_ffn_in['gate_w'], 'L1_ffn_experts_gate_up': _L1_ffn_in['experts_gate_up'], 'L1_ffn_experts_down': _L1_ffn_in['experts_down'], 'L1_ffn_shared_gate_w': _L1_ffn_in['shared_gate_w'], 'L1_ffn_shared_up_w': _L1_ffn_in['shared_up_w'], 'L1_ffn_shared_down_w': _L1_ffn_in['shared_down_w'], 'L1_ffn_shared_expert_gate_w': _L1_ffn_in['shared_expert_gate_w'], 'L2_attn_W_q': _L2_attn_in['W_q'], 'L2_attn_W_k': _L2_attn_in['W_k'], 'L2_attn_W_v': _L2_attn_in['W_v'], 'L2_ffn_gate_w': _L2_ffn_in['gate_w'], 'L2_ffn_w1': _L2_ffn_in['w1'], 'L2_ffn_w3': _L2_ffn_in['w3'], 'L2_ffn_w2': _L2_ffn_in['w2'], 'L2_ffn_e_bias': _L2_ffn_in['e_bias'], 'L3_attn_Wq': _L3_attn_in['Wq'], 'L3_attn_Wk': _L3_attn_in['Wk'], 'L3_attn_Wv': _L3_attn_in['Wv'], 'L3_attn_Wo': _L3_attn_in['Wo'], 'L3_attn_lambda_q1': _L3_attn_in['lambda_q1'], 'L3_attn_lambda_k1': _L3_attn_in['lambda_k1'], 'L3_attn_lambda_q2': _L3_attn_in['lambda_q2'], 'L3_attn_lambda_k2': _L3_attn_in['lambda_k2'], 'L3_attn_subln_g': _L3_attn_in['subln_g'], 'L3_ffn_wqkv': _L3_ffn_in['wqkv'], 'L3_ffn_q_scale': _L3_ffn_in['q_scale'], 'L3_ffn_k_scale': _L3_ffn_in['k_scale'], 'L3_ffn_wo': _L3_ffn_in['wo'], 'L3_ffn_ln_g': _L3_ffn_in['ln_g'], 'L3_ffn_ln_b': _L3_ffn_in['ln_b'], 'L3_ffn_w1': _L3_ffn_in['w1'], 'L3_ffn_b1': _L3_ffn_in['b1'], 'L3_ffn_w2': _L3_ffn_in['w2'], 'L3_ffn_b2': _L3_ffn_in['b2']}
    _x0 = _d['L0_attn_x']
    _d['L0_attn_x'] = jax.random.normal(jax.random.fold_in(jax.random.key(seed), 1), (8, 512, 128), dtype=_x0.dtype)
    del _x0
    return _d

def reference(L0_attn_x, L0_attn_W_disp, L0_attn_W_val, L0_attn_rel_pos_emb, L0_attn_W_strain, L0_attn_W_pos, L0_attn_W_bond, L0_attn_W_dmg, L0_attn_b_dmg, L0_attn_W_dmg_out, L0_attn_b_dmg_out, L0_attn_W_cproj, L0_ffn_Wr, L0_ffn_Wg, L0_ffn_Wu, L0_ffn_Wd, L0_ffn_Sg, L0_ffn_Su, L0_ffn_Sd, L0_ffn_expert_bias, L1_attn_w_qkv, L1_attn_w_out, L1_attn_b_out, L1_ffn_gate_w, L1_ffn_experts_gate_up, L1_ffn_experts_down, L1_ffn_shared_gate_w, L1_ffn_shared_up_w, L1_ffn_shared_down_w, L1_ffn_shared_expert_gate_w, L2_attn_W_q, L2_attn_W_k, L2_attn_W_v, L2_ffn_gate_w, L2_ffn_w1, L2_ffn_w3, L2_ffn_w2, L2_ffn_e_bias, L3_attn_Wq, L3_attn_Wk, L3_attn_Wv, L3_attn_Wo, L3_attn_lambda_q1, L3_attn_lambda_k1, L3_attn_lambda_q2, L3_attn_lambda_k2, L3_attn_subln_g, L3_ffn_wqkv, L3_ffn_q_scale, L3_ffn_k_scale, L3_ffn_wo, L3_ffn_ln_g, L3_ffn_ln_b, L3_ffn_w1, L3_ffn_b1, L3_ffn_w2, L3_ffn_b2):

    def _L0_attn_ref(x, W_disp, W_val, rel_pos_emb, W_strain, W_pos, W_bond, W_dmg, b_dmg, W_dmg_out, b_dmg_out, W_cproj):
        import jax, jax.numpy as jnp
        import numpy as np
        N_EMBD = 128
        N_HEAD = 16
        HORIZON = 64
        HS = N_EMBD // N_HEAD
        BD = max(HS // 4, 16)

        def _windows(t, delta):
            B, nh, T, D = t.shape
            padded = jnp.pad(t, ((0, 0), (0, 0), (delta - 1, 0), (0, 0)))
            idx = jnp.arange(T)[:, None] + jnp.arange(delta)[None, :]
            return padded[:, :, idx]
        B, T, C = x.shape
        nh, bd, hs = (N_HEAD, BD, HS)
        delta = min(HORIZON, T)
        disp = (x @ W_disp).reshape(B, T, nh, bd).transpose(0, 2, 1, 3)
        val = (x @ W_val).reshape(B, T, nh, hs).transpose(0, 2, 1, 3)
        disp_win = _windows(disp, delta)
        val_win = _windows(val, delta)
        cmask = jnp.arange(T)[:, None] - delta + 1 + jnp.arange(delta)[None, :] >= 0
        strain = disp_win - disp[:, :, :, None, :]
        rel_emb = rel_pos_emb[:delta]
        bond_act = jax.nn.gelu(strain @ W_strain + rel_emb @ W_pos, approximate=False)
        bond_logits = (bond_act @ W_bond)[..., 0]
        damage_act = jax.nn.gelu(strain @ W_dmg + b_dmg, approximate=False)
        damage = jax.nn.sigmoid((damage_act @ W_dmg_out)[..., 0] + b_dmg_out[0])
        logits = bond_logits - 10.0 * damage
        logits = jnp.where(cmask[None, None], logits, -jnp.inf)
        weights = jax.nn.softmax(logits, axis=-1)
        out = jnp.einsum('bntd,bntde->bnte', weights, val_win)
        out = out.transpose(0, 2, 1, 3).reshape(B, T, C)
        return out @ W_cproj

    def _L0_ffn_ref(x, Wr, Wg, Wu, Wd, Sg, Su, Sd, expert_bias):
        import jax, jax.numpy as jnp
        import numpy as np
        B, S, D = (2, 128, 128)
        E, K, F, FS = (8, 2, 64, 128)
        b, s, d = x.shape
        xf = x.reshape(-1, d)
        T = xf.shape[0]
        logits = xf @ Wr + expert_bias
        top_v, top_i = jax.lax.top_k(logits, K)
        probs = jax.nn.softmax(top_v, axis=-1)
        rw = jnp.zeros_like(logits).at[jnp.arange(T)[:, None], top_i].set(probs)
        gate = jnp.einsum('td,edf->tef', xf, Wg)
        up = jnp.einsum('td,edf->tef', xf, Wu)
        h = jax.nn.silu(gate) * up
        eo = jnp.einsum('tef,efd->ted', h, Wd)
        out = jnp.einsum('te,ted->td', rw, eo)
        out = out + jax.nn.silu(xf @ Sg) * (xf @ Su) @ Sd
        return out.reshape(b, s, d)

    def _L1_attn_ref(x, w_qkv, w_out, b_out):
        import jax, jax.numpy as jnp
        import numpy as np
        D_MODEL = 128
        N_HEADS = 16
        B, T, D = x.shape
        h = N_HEADS
        Hd = D // h
        qkv = jnp.einsum('btd,de->bte', x, w_qkv).reshape(B, T, 3, h, Hd)
        q = jnp.transpose(qkv[:, :, 0], (0, 2, 1, 3))
        k = jnp.transpose(qkv[:, :, 1], (0, 2, 1, 3))
        v = jnp.transpose(qkv[:, :, 2], (0, 2, 1, 3))
        scale = 1.0 / jnp.sqrt(jnp.array(Hd, dtype=x.dtype))
        logits = jnp.einsum('bhqd,bhkd->bhqk', q, k) * scale
        mask = jnp.tril(jnp.ones((T, T), dtype=x.dtype))
        big_neg = jnp.array(-10000000000.0, dtype=x.dtype)
        logits = logits + (1.0 - mask)[None, None, :, :] * big_neg
        attn = jax.nn.softmax(logits, axis=-1)
        out = jnp.einsum('bhqk,bhkd->bhqd', attn, v)
        out = jnp.transpose(out, (0, 2, 1, 3)).reshape(B, T, D)
        return jnp.einsum('btd,de->bte', out, w_out) + b_out

    def _L1_ffn_ref(x, gate_w, experts_gate_up, experts_down, shared_gate_w, shared_up_w, shared_down_w, shared_expert_gate_w):
        import jax, jax.numpy as jnp
        import numpy as np
        HIDDEN_SIZE = 128
        NUM_EXPERTS = 8
        MOE_INTERMEDIATE_SIZE = 176
        NUM_EXPERTS_PER_TOK = 2
        SHARED_EXPERT_INTERMEDIATE_SIZE = 352
        B, T = (2, 128)
        W_SCALE = 0.02
        Bx, Tx, H = x.shape
        E = gate_w.shape[0]
        I = experts_down.shape[2]
        x_flat = x.reshape(Bx * Tx, H)
        logits = x_flat @ gate_w.T
        scores = jax.nn.softmax(logits, axis=-1)
        _, topk_ids = jax.lax.top_k(scores, NUM_EXPERTS_PER_TOK)
        in_topk = jax.nn.one_hot(topk_ids, E, dtype=x.dtype).sum(axis=1)
        w = scores * in_topk
        gu = jnp.einsum('nh,eih->nei', x_flat, experts_gate_up)
        g, u = (gu[..., :I], gu[..., I:])
        h = jax.nn.silu(g) * u
        expert_out = jnp.einsum('nei,ehi->neh', h, experts_down)
        out = jnp.einsum('neh,ne->nh', expert_out, w)
        shared = jax.nn.silu(x_flat @ shared_gate_w.T) * (x_flat @ shared_up_w.T) @ shared_down_w.T
        shared_weight = jax.nn.sigmoid(x_flat @ shared_expert_gate_w.T)
        out = out + shared_weight * shared
        return out.reshape(Bx, Tx, H)

    def _L2_attn_ref(x, W_q, W_k, W_v):
        import jax, jax.numpy as jnp
        import numpy as np
        EPS = 1e-12

        def _l2norm(t):
            n = jnp.linalg.norm(t, axis=-1, keepdims=True)
            return t / jnp.maximum(n, EPS)
        Q = _l2norm(jnp.einsum('bnd,ed->bne', x, W_q))
        K = _l2norm(jnp.einsum('bnd,ed->bne', x, W_k))
        V = jnp.einsum('bnd,ed->bne', x, W_v)
        C = x.shape[1]
        global_feat = jnp.sum(K * V, axis=1, keepdims=True) / C
        return Q * global_feat

    def _L2_ffn_ref(hidden_states, gate_w, w1, w3, w2, e_bias):
        import jax, jax.numpy as jnp
        import numpy as np
        E = 32
        K = 4
        H = 128
        I = 96
        ROUTED_SCALING_FACTOR = 1.0
        orig_shape = hidden_states.shape
        x = hidden_states.reshape(-1, orig_shape[-1])
        T = x.shape[0]
        router_logits = x @ gate_w.T
        scores = jax.nn.sigmoid(router_logits.astype(jnp.float32))
        _, topk_ids = jax.lax.top_k(scores + e_bias[None, :], K)
        topk_w = jnp.take_along_axis(scores, topk_ids, axis=1)
        topk_w = topk_w / jnp.sum(topk_w, axis=1, keepdims=True)
        combine = jnp.zeros((T, E), jnp.float32).at[jnp.arange(T)[:, None], topk_ids].add(topk_w)
        g = jnp.einsum('th,ehi->tei', x, w1)
        u = jnp.einsum('th,ehi->tei', x, w3)
        a = jax.nn.silu(g) * u * combine[:, :, None].astype(x.dtype)
        out = jnp.einsum('tei,eih->th', a, w2)
        out = out * ROUTED_SCALING_FACTOR
        return out.reshape(orig_shape)

    def _L3_attn_ref(x, Wq, Wk, Wv, Wo, lambda_q1, lambda_k1, lambda_q2, lambda_k2, subln_g):
        import jax, jax.numpy as jnp
        import numpy as np
        import math
        EMBED_DIM = 128
        NUM_HEADS = 16
        NUM_KV_HEADS = 16
        DEPTH = 12
        HEAD_DIM = EMBED_DIM // NUM_HEADS // 2
        LAMBDA_INIT = 0.8 - 0.6 * math.exp(-0.3 * DEPTH)
        EPS = 1e-05
        THETA = 0.0001

        def rope(q):
            b, s, h, d = q.shape
            pos = jnp.arange(s, dtype=jnp.float32)[:, None]
            freq = 1.0 / THETA ** (2.0 * jnp.arange(d // 2, dtype=jnp.float32) / d)
            ang = pos * freq
            cos = jnp.cos(ang)[None, :, None, :].astype(q.dtype)
            sin = jnp.sin(ang)[None, :, None, :].astype(q.dtype)
            qr = q.reshape(b, s, h, d // 2, 2)
            q0, q1 = (qr[..., 0], qr[..., 1])
            out = jnp.stack([q0 * cos - q1 * sin, q0 * sin + q1 * cos], axis=-1)
            return out.reshape(q.shape)
        b, s, d = x.shape
        H, hd = (NUM_HEADS, HEAD_DIM)
        scaling = hd ** (-0.5)
        q = (x @ Wq).reshape(b, s, 2 * H, hd)
        k = (x @ Wk).reshape(b, s, 2 * NUM_KV_HEADS, hd)
        v = (x @ Wv).reshape(b, s, NUM_KV_HEADS, 2 * hd)
        q = rope(q).transpose(0, 2, 1, 3) * scaling
        k = rope(k).transpose(0, 2, 1, 3)
        v = v.transpose(0, 2, 1, 3)
        scores = jnp.einsum('bhqd,bhkd->bhqk', q, k)
        probs = jax.nn.softmax(scores.astype(jnp.float32), axis=-1).astype(scores.dtype)
        lam1 = jnp.exp(jnp.sum(lambda_q1 * lambda_k1))
        lam2 = jnp.exp(jnp.sum(lambda_q2 * lambda_k2))
        lam = (lam1 - lam2 + LAMBDA_INIT).astype(q.dtype)
        probs = probs.reshape(b, H, 2, s, s)
        w = probs[:, :, 0] - lam * probs[:, :, 1]
        attn = jnp.einsum('bhqk,bhkd->bhqd', w, v)
        rms = jax.lax.rsqrt(jnp.mean(attn * attn, axis=-1, keepdims=True) + EPS)
        attn = attn * rms * subln_g
        attn = attn * (1.0 - LAMBDA_INIT)
        attn = attn.transpose(0, 2, 1, 3).reshape(b, s, H * 2 * hd)
        return attn @ Wo

    def _L3_ffn_ref(x, wqkv, q_scale, k_scale, wo, ln_g, ln_b, w1, b1, w2, b2):
        import jax, jax.numpy as jnp
        import numpy as np
        DIM = 128
        DEPTH = 2
        HEADS = 8
        DIM_HEAD = 64
        WINDOW = 64
        INNER = HEADS * DIM_HEAD
        HID = int(DIM * 4 * 2 / 3)
        B, N = (2, 1024)
        QK_SCALE = 8.0

        def shift_token(t):
            t1, t2 = jnp.split(t, 2, axis=-1)
            t2 = jnp.pad(t2, ((0, 0), (1, 0), (0, 0)))[:, :-1]
            return jnp.concatenate([t1, t2], axis=-1)

        def l2norm(t):
            return t / jnp.clip(jnp.linalg.norm(t, axis=-1, keepdims=True), 1e-12)

        def rotate_half(x):
            x1, x2 = jnp.split(x, 2, axis=-1)
            return jnp.concatenate([-x2, x1], axis=-1)

        def rotary_xpos(q, k):
            n = q.shape[-2]
            half_idx = jnp.arange(0, DIM_HEAD, 2, dtype=jnp.float32)
            inv_freq = 1.0 / 10000.0 ** (half_idx / DIM_HEAD)
            t = jnp.arange(n, dtype=jnp.float32)
            freqs = t[:, None] * inv_freq[None, :]
            freqs = jnp.concatenate([freqs, freqs], axis=-1)
            base = (half_idx + 0.4 * DIM_HEAD) / (1.4 * DIM_HEAD)
            power = (t - n // 2) / float(WINDOW // 2)
            scale = base[None, :] ** power[:, None]
            scale = jnp.concatenate([scale, scale], axis=-1)
            cos, sin = (jnp.cos(freqs), jnp.sin(freqs))
            q = q * cos * scale + rotate_half(q) * sin * scale
            k = k * cos / scale + rotate_half(k) * sin / scale
            return (q, k)

        def local_attention(q, k, v):
            b, h, n, d = q.shape
            w = n // WINDOW
            bq = q.reshape(b, h, w, WINDOW, d) * QK_SCALE
            bk = k.reshape(b, h, w, WINDOW, d)
            bv = v.reshape(b, h, w, WINDOW, d)

            def look_around(t):
                p = jnp.pad(t, ((0, 0), (0, 0), (1, 0), (0, 0), (0, 0)))
                return jnp.concatenate([p[:, :, :w], p[:, :, 1:]], axis=3)
            bk, bv = (look_around(bk), look_around(bv))
            bt = jnp.arange(n).reshape(w, WINDOW)
            btp = jnp.pad(bt, ((1, 0), (0, 0)), constant_values=-1)
            btk = jnp.concatenate([btp[:w], btp[1:]], axis=1)
            sim = jnp.einsum('bhwid,bhwjd->bhwij', bq, bk)
            i = bt[:, :, None]
            j = btk[:, None, :]
            mask = (i < j) | (i > j + WINDOW) | (j == -1)
            sim = jnp.where(mask, -jnp.finfo(sim.dtype).max, sim)
            attn = jax.nn.softmax(sim, axis=-1)
            out = jnp.einsum('bhwij,bhwjd->bhwid', attn, bv)
            return out.reshape(b, h, n, d)

        def _layer(x, wqkv, qs, ksc, wo, lg, lb, w1, b1, w2, b2):
            b, n, _ = x.shape
            h = shift_token(x)
            qkv = h @ wqkv
            q, k, v = jnp.split(qkv, 3, axis=-1)
            to_heads = lambda t: t.reshape(b, n, HEADS, DIM_HEAD).transpose(0, 2, 1, 3)
            q, k, v = (to_heads(q), to_heads(k), to_heads(v))
            q = l2norm(q) * qs
            k = l2norm(k) * ksc
            q, k = rotary_xpos(q, k)
            o = local_attention(q, k, v)
            o = o.transpose(0, 2, 1, 3).reshape(b, n, INNER)
            x = x + o @ wo
            h = shift_token(x)
            mu = h.mean(-1, keepdims=True)
            var = h.var(-1, keepdims=True)
            h = (h - mu) / jnp.sqrt(var + 1e-05) * lg + lb
            h = h @ w1 + b1
            a, g = jnp.split(h, 2, axis=-1)
            h = a * jax.nn.gelu(g, approximate=False)
            x = x + h @ w2 + b2
            return x
        for l in range(DEPTH):
            x = _layer(x, wqkv[l], q_scale[l], k_scale[l], wo[l], ln_g[l], ln_b[l], w1[l], b1[l], w2[l], b2[l])
        return x
    x = L0_attn_x
    x = _layernorm(x + _L0_attn_ref(x, L0_attn_W_disp, L0_attn_W_val, L0_attn_rel_pos_emb, L0_attn_W_strain, L0_attn_W_pos, L0_attn_W_bond, L0_attn_W_dmg, L0_attn_b_dmg, L0_attn_W_dmg_out, L0_attn_b_dmg_out, L0_attn_W_cproj), axis=-1)
    x = _layernorm(x + _L0_ffn_ref(x, L0_ffn_Wr, L0_ffn_Wg, L0_ffn_Wu, L0_ffn_Wd, L0_ffn_Sg, L0_ffn_Su, L0_ffn_Sd, L0_ffn_expert_bias), axis=-1)
    x = _layernorm(x + _L1_attn_ref(x, L1_attn_w_qkv, L1_attn_w_out, L1_attn_b_out), axis=-1)
    x = _layernorm(x + _L1_ffn_ref(x, L1_ffn_gate_w, L1_ffn_experts_gate_up, L1_ffn_experts_down, L1_ffn_shared_gate_w, L1_ffn_shared_up_w, L1_ffn_shared_down_w, L1_ffn_shared_expert_gate_w), axis=-1)
    x = _layernorm(x + _L2_attn_ref(x, L2_attn_W_q, L2_attn_W_k, L2_attn_W_v), axis=-1)
    x = _layernorm(x + _L2_ffn_ref(x, L2_ffn_gate_w, L2_ffn_w1, L2_ffn_w3, L2_ffn_w2, L2_ffn_e_bias), axis=-1)
    x = _layernorm(x + _L3_attn_ref(x, L3_attn_Wq, L3_attn_Wk, L3_attn_Wv, L3_attn_Wo, L3_attn_lambda_q1, L3_attn_lambda_k1, L3_attn_lambda_q2, L3_attn_lambda_k2, L3_attn_subln_g), axis=-1)
    x = _layernorm(x + _L3_ffn_ref(x, L3_ffn_wqkv, L3_ffn_q_scale, L3_ffn_k_scale, L3_ffn_wo, L3_ffn_ln_g, L3_ffn_ln_b, L3_ffn_w1, L3_ffn_b1, L3_ffn_w2, L3_ffn_b2), axis=-1)
    return x

_drawn_inputs = setup_inputs


def setup_inputs(seed=0):
    import zlib

    import numpy as np

    out = dict(_drawn_inputs(seed))
    spreads = {'L0_attn_b_dmg': (0.0, 0.8),
     'L0_ffn_expert_bias': (0.0, 0.1),
     'L3_attn_subln_g': (1.0, 0.2),
     'L3_ffn_q_scale': (1.0, 0.6),
     'L3_ffn_k_scale': (1.0, 0.6),
     'L3_ffn_ln_g': (1.0, 0.6),
     'L3_ffn_ln_b': (0.0, 0.8),
     'L3_ffn_b1': (0.0, 0.8),
     'L3_ffn_b2': (0.0, 0.467)}
    factors = {'L0_attn_W_disp': 8.0,
     'L0_attn_rel_pos_emb': 8.0,
     'L0_attn_W_strain': 8.0,
     'L0_attn_W_pos': 8.0,
     'L0_attn_W_bond': 8.0,
     'L0_attn_W_dmg': 8.0,
     'L0_attn_W_dmg_out': 8.0,
     'L1_attn_b_out': 4.358,
     'L1_ffn_gate_w': 8.0,
     'L1_ffn_experts_gate_up': 8.0,
     'L1_ffn_experts_down': 8.0,
     'L1_ffn_shared_gate_w': 8.0,
     'L1_ffn_shared_up_w': 8.0,
     'L1_ffn_shared_down_w': 8.0,
     'L1_ffn_shared_expert_gate_w': 8.0,
     'L2_attn_W_q': 8.0,
     'L2_attn_W_k': 8.0,
     'L2_attn_W_v': 8.0,
     'L2_ffn_gate_w': 8.0,
     'L2_ffn_w1': 8.0,
     'L2_ffn_w3': 8.0,
     'L2_ffn_w2': 8.0,
     'L2_ffn_e_bias': 8.0,
     'L3_attn_lambda_q1': 8.0,
     'L3_attn_lambda_k1': 8.0,
     'L3_attn_lambda_q2': 7.664,
     'L3_attn_lambda_k2': 7.664,
     'L3_ffn_wqkv': 3.209,
     'L3_ffn_wo': 3.231,
     'L3_ffn_w1': 6.318,
     'L3_ffn_w2': 6.184}
    for name, (base, spread) in spreads.items():
        noise = np.random.default_rng([zlib.crc32(name.encode()), seed]).standard_normal(out[name].shape)
        drawn = base * np.exp(spread * noise) if base else spread * noise
        out[name] = jnp.asarray(drawn.astype(out[name].dtype))
    for name, factor in factors.items():
        out[name] = (out[name] * factor).astype(out[name].dtype)
    return out
```

```python
import math
from contextlib import ExitStack

import numpy as np

import concourse.bass as bass
from concourse import mybir

F32 = mybir.dt.float32
BF16 = mybir.dt.bfloat16
ALU = mybir.AluOpType
ACT = mybir.ActivationFunctionType
AX = mybir.AxisListType.X

P = 128
NB = 8
T = 512
TT = T // P
NTOK = NB * T // P
BIG = 1e30
LAMBDA_INIT = 0.8 - 0.6 * math.exp(-0.3 * 12)

STAGES = (0, 7)


class Signals:

    def __init__(self, sem, per):
        self.sem, self.per = sem, per

    def wait(self, eng, turn, n):
        eng.wait_ge(self.sem, turn * self.per + n)


class Stage:

    def __init__(self, nc, ctx):
        self.nc, self.ctx, self.sems = nc, ctx, []
        ctx.callback(self.clear)

    CLEARED = []

    def clear(self):
        for sem in Stage.CLEARED:
            self.nc.release_semaphore(sem)
        Stage.CLEARED = list(self.sems)
        for sem in self.sems:
            self.nc.gpsimd.sem_clear(sem)

    def sb(self, name, shape, dt=F32):
        return self.ctx.enter_context(self.nc.sbuf_tensor(name, shape, dt))

    def sem(self, name):
        self.sems.append(self.nc.alloc_semaphore(name))
        return self.sems[-1]

    def sig(self, name, per):
        return Signals(self.sem(name), per)


def layernorm(nc, tag, X, Y, PS, C):
    with ExitStack() as ctx:
        s = Stage(nc, ctx)
        std = s.sb(f"{tag}_std", [P, NTOK])
        rstd = s.sb(f"{tag}_rstd", [P, NTOK])
        mean_ready = s.sem(f"{tag}_mean_ready")
        centred = s.sem(f"{tag}_centred")
        squared = s.sem(f"{tag}_squared")
        var_ready = s.sem(f"{tag}_var_ready")
        eps_added = s.sem(f"{tag}_eps_added")
        std_ready = s.sem(f"{tag}_std_ready")
        rstd_ready = s.sem(f"{tag}_rstd_ready")
        spread = s.sem(f"{tag}_spread")
        block = ctx.enter_context(nc.Block())

        @block.tensor
        def _(pe):
            with pe.Fori(0, NB) as b:
                pe.matmul(PS[:, b, :], C["inv_d"], Y[:, b, :], start=True, stop=True).then_inc(mean_ready, 1)
            for n in range(NTOK):
                if n % TT == 0:
                    pe.wait_ge(squared, n // TT + 1)
                mm = pe.matmul(PS[:, 0, n:n + 1], X[:, n // TT, bass.ts(n % TT, P)], C["inv_d"][:, 0:1],
                               start=True, stop=True)
            mm.then_inc(var_ready, 1)
            pe.wait_ge(rstd_ready, 1)
            for n in range(NTOK):
                mm = pe.matmul(PS[:, n // TT, bass.ts(n % TT, P)], rstd[:, n:n + 1].to_broadcast([P, P]),
                               C["ident"], start=True, stop=True)
                if n % TT == TT - 1:
                    mm.then_inc(spread, 1)

        @block.vector
        def _(dve):
            with dve.Fori(0, NB) as b:
                dve.wait_ge(mean_ready, b + 1)
                dve.tensor_tensor(Y[:, b, :], Y[:, b, :], PS[:, b, :], ALU.subtract).then_inc(centred, 1)
            dve.wait_ge(var_ready, 1)
            dve.tensor_scalar(std[:, :], PS[:, 0, 0:NTOK], 1e-5, None, ALU.add).then_inc(eps_added, 1)
            dve.wait_ge(std_ready, 1)
            dve.reciprocal(rstd[:, :], std[:, :]).then_inc(rstd_ready, 1)
            with dve.Fori(0, NB) as b:
                dve.wait_ge(spread, b + 1)
                dve.tensor_tensor(X[:, b, :], Y[:, b, :], PS[:, b, :], ALU.mult)

        @block.scalar
        def _(act):
            with act.Fori(0, NB) as b:
                act.wait_ge(centred, b + 1)
                act.activation(X[:, b, :], Y[:, b, :], ACT.Square).then_inc(squared, 1)
            act.wait_ge(eps_added, 1)
            act.activation(std[:, :], std[:, :], ACT.Sqrt).then_inc(std_ready, 1)


def moe(nc, tag, X, Y, PS, C, W, kind, E, K, NT):
    EW = E + (1 if kind in ("top_softmax", "softmax_top") else 0)
    NV = E + 8 - K
    NR = W["router"].shape[1]
    SENT, PICKED = -3e38, 3e38
    with ExitStack() as ctx:
        s = Stage(nc, ctx)
        vals = s.sb(f"{tag}_vals", [P, NTOK, NV])
        top = s.sb(f"{tag}_top", [P, NTOK, 8])
        marked = s.sb(f"{tag}_marked", [P, NTOK, NV])
        score = s.sb(f"{tag}_score", [P, NTOK, NR])
        wt = s.sb(f"{tag}_wt", [P, NTOK, EW])
        tot = s.sb(f"{tag}_tot", [P, NTOK])
        rtot = s.sb(f"{tag}_rtot", [P, NTOK])
        parts = s.sb(f"{tag}_parts", [P, NTOK, 96], BF16)
        partsT = s.sb(f"{tag}_partsT", [96, NB, T], BF16)
        silu = s.sb(f"{tag}_silu", [P, 3, T])
        prod = s.sb(f"{tag}_prod", [P, T])
        hid = s.sb(f"{tag}_hid", [P, 3, T])
        logits_ready = s.sem(f"{tag}_logits_ready")
        step = s.sem(f"{tag}_router_step")
        exp_in = s.sem(f"{tag}_exp_in")
        exp_out = s.sem(f"{tag}_exp_out")
        cleared = s.sem(f"{tag}_cleared")
        parts_ready = s.sem(f"{tag}_parts_ready")
        turned = s.sem(f"{tag}_turned")
        turned_kept = s.sem(f"{tag}_turned_kept")
        gate_ready = s.sig(f"{tag}_gate_ready", NT)
        up_ready = s.sig(f"{tag}_up_ready", NT)
        silu_ready = s.sig(f"{tag}_silu_ready", NT)
        prod_ready = s.sig(f"{tag}_prod_ready", NT)
        hid_ready = s.sig(f"{tag}_hid_ready", NT)
        hid_used = s.sig(f"{tag}_hid_used", NT)
        out_kept = s.sig(f"{tag}_out_kept", 1)
        block = ctx.enter_context(nc.Block())
        LOG = PS[:, 0:2, :].rearrange("p a b -> p (a b)")[:, 0:NTOK * 32].rearrange("p (n e) -> p n e", e=32)

        @block.sync
        def _(sp):
            C["load"](sp, tag)

        @block.gpsimd
        def _(pool):
            pool.memset(parts[:, :, :], 0.0).then_inc(cleared, 1)
            pool.memset(vals[:, :, E:NV], SENT).then_inc(cleared, 1)

        @block.tensor
        def _(pe):
            C["weights"](pe, tag)
            for n in range(NTOK):
                mm = pe.matmul(LOG[:, n, 0:NR], X[:, n // TT, bass.ts(n % TT, P)], W["router"],
                               start=True, stop=True)
            mm.then_inc(logits_ready, 1)
            pe.wait_ge(parts_ready, 1)
            for b in range(NB):
                TP = PS[:, b, 0:T // 2].bitcast(BF16)
                for t in range(TT):
                    mm = pe.transpose(TP[0:96, bass.ts(t, P)], parts[:, b * TT + t, :], C["ident_bf"])
                mm.then_inc(turned, 1)
            pe.wait_ge(turned_kept, NB)

            def down(b, f):
                hid_ready.wait(pe, b, f + 1)
                if f == 0:
                    out_kept.wait(pe, b, 0)
                pe.matmul(PS[:, 6, :], W["down"][:, bass.ts(f, P)], hid[:, f % 3, :],
                          start=(f == 0), stop=(f == NT - 1)).then_inc(hid_used.sem, 1)

            with pe.Fori(0, NB) as b:
                for f in range(NT):
                    if f >= 2:
                        silu_ready.wait(pe, b, f - 1)
                        hid_ready.wait(pe, b, f - 1)
                    else:
                        hid_ready.wait(pe, b, 0)
                    pe.matmul(PS[:, f % 2, :], W["gate"][:, bass.ts(f, P)], X[:, b, :],
                              start=True, stop=True).then_inc(gate_ready.sem, 1)
                    pe.matmul(PS[:, 2 + f % 2, :], W["up"][:, bass.ts(f, P)], X[:, b, :], start=True, stop=True)
                    pe.matmul(PS[:, 4 + f % 2, :], W["sel"][:, bass.ts(f, P)], partsT[:, b, :],
                              start=True, stop=True).then_inc(up_ready.sem, 1)
                    if f >= 2:
                        down(b, f - 2)
                down(b, NT - 2)
                down(b, NT - 1)

        @block.scalar
        def _(act):
            if kind == "top_softmax":
                act.wait_ge(exp_in, 1)
                act.activation(score[:, :, :], score[:, :, :], ACT.Exp).then_inc(exp_out, 1)
            elif kind == "softmax_top":
                act.wait_ge(exp_in, 1)
                act.activation(score[:, :, :], score[:, :, :], ACT.Exp).then_inc(exp_out, 1)
            else:
                act.wait_ge(logits_ready, 1)
                act.activation(score[:, 0:NTOK // 2, :], LOG[:, 0:NTOK // 2, 0:NR], ACT.Sigmoid)
                act.activation(score[:, NTOK // 2:, :], LOG[:, NTOK // 2:, 0:NR], ACT.Sigmoid).then_inc(exp_out, 1)
            with act.Fori(0, NB) as b:
                for f in range(NT):
                    gate_ready.wait(act, b, f + 1)
                    if f >= 3:
                        prod_ready.wait(act, b, f - 2)
                    else:
                        prod_ready.wait(act, b, 0)
                    act.activation(silu[:, f % 3, :], PS[:, f % 2, :], ACT.Silu).then_inc(silu_ready.sem, 1)

        @block.vector
        def _(dve):
            chain = [0]

            def then(ins):
                chain[0] += 1
                ins.then_inc(step, 1)
                dve.wait_ge(step, chain[0])

            def over(a, n):
                return a.rearrange("p (n o) -> p n o", o=1).to_broadcast([P, NTOK, n])

            C["weights"](dve, tag)
            dve.wait_ge(logits_ready, 1)
            if kind == "top_softmax":
                bias = W["bias"].rearrange("p (o e) -> p o e", o=1).to_broadcast([P, NTOK, E])
                dve.wait_ge(cleared, 2)
                then(dve.tensor_tensor(vals[:, :, 0:E], LOG[:, :, 0:E], bias, ALU.add))
                pick_from = vals
            elif kind == "softmax_top":
                then(dve.tensor_reduce(tot[:, :], LOG[:, :, 0:E], AX, ALU.max))
                then(dve.tensor_tensor(score[:, :, 0:E], LOG[:, :, 0:E], over(tot[:, :], E), ALU.subtract))
                dve.tensor_scalar(score[:, :, E:E + 1], LOG[:, :, E:E + 1], -1.0, None, ALU.mult).then_inc(exp_in, 1)
                dve.wait_ge(exp_out, 1)
                then(dve.tensor_reduce(tot[:, :], score[:, :, 0:E], AX, ALU.add))
                then(dve.reciprocal(rtot[:, :], tot[:, :]))
                dve.wait_ge(cleared, 2)
                then(dve.tensor_tensor(vals[:, :, 0:E], score[:, :, 0:E], over(rtot[:, :], E), ALU.mult))
            else:
                bias = W["bias"].rearrange("p (o e) -> p o e", o=1).to_broadcast([P, NTOK, E])
                dve.wait_ge(exp_out, 1)
                dve.wait_ge(cleared, 2)
                then(dve.tensor_tensor(vals[:, :, 0:E], score[:, :, 0:E], bias, ALU.add))
            for n in range(NTOK):
                m = dve.max(top[:, n, :], vals[:, n, 0:E])
            then(m)
            then(dve.memset(top[:, :, K:8], SENT))
            for n in range(NTOK):
                m = dve.match_replace(marked[:, n, :], top[:, n, :], vals[:, n, :], PICKED)
            then(m)
            then(dve.tensor_scalar(marked[:, :, 0:E], marked[:, :, 0:E], 1e38, None, ALU.is_ge))
            if kind == "top_softmax":
                best = top[:, :, 0:1].to_broadcast([P, NTOK, E])
                dve.tensor_tensor(score[:, :, :], vals[:, :, 0:E], best, ALU.subtract).then_inc(exp_in, 1)
                dve.wait_ge(exp_out, 1)
                source = score
            elif kind == "softmax_top":
                source = vals
            else:
                source = score
            then(dve.tensor_tensor(wt[:, :, 0:E], source[:, :, 0:E], marked[:, :, 0:E], ALU.mult))
            if kind != "softmax_top":
                then(dve.tensor_reduce(tot[:, :], wt[:, :, 0:E], AX, ALU.add))
                then(dve.reciprocal(rtot[:, :], tot[:, :]))
                then(dve.tensor_tensor(wt[:, :, 0:E], wt[:, :, 0:E], over(rtot[:, :], E), ALU.mult))
            if kind == "top_softmax":
                then(dve.memset(wt[:, :, E:EW], 1.0))
            elif kind == "softmax_top":
                then(dve.tensor_scalar(score[:, :, E:EW], score[:, :, E:EW], 1.0, None, ALU.add))
                then(dve.reciprocal(wt[:, :, E:EW], score[:, :, E:EW]))
            then(dve.tensor_copy(parts[:, :, 0:EW], wt[:, :, :]))
            then(dve.tensor_tensor(wt[:, :, :], wt[:, :, :], parts[:, :, 0:EW], ALU.subtract))
            then(dve.tensor_copy(parts[:, :, 32:32 + EW], wt[:, :, :]))
            then(dve.tensor_tensor(wt[:, :, :], wt[:, :, :], parts[:, :, 32:32 + EW], ALU.subtract))
            dve.tensor_copy(parts[:, :, 64:64 + EW], wt[:, :, :]).then_inc(parts_ready, 1)
            for b in range(NB):
                dve.wait_ge(turned, b + 1)
                dve.tensor_copy(partsT[:, b, :], PS[:, b, 0:T // 2].bitcast(BF16)[0:96, :]).then_inc(turned_kept, 1)

            with dve.Fori(0, NB) as b:
                for f in range(NT):
                    silu_ready.wait(dve, b, f + 1)
                    up_ready.wait(dve, b, f + 1)
                    if f >= 1:
                        hid_ready.wait(dve, b, f)
                    else:
                        hid_ready.wait(dve, b, 0)
                    dve.tensor_tensor(prod[:, :], silu[:, f % 3, :], PS[:, 2 + f % 2, :], ALU.mult)\
                       .then_inc(prod_ready.sem, 1)
                    prod_ready.wait(dve, b, f + 1)
                    if f >= 3:
                        hid_used.wait(dve, b, f - 2)
                    else:
                        hid_used.wait(dve, b, 0)
                    dve.tensor_tensor(hid[:, f % 3, :], prod[:, :], PS[:, 4 + f % 2, :], ALU.mult)\
                       .then_inc(hid_ready.sem, 1)
                hid_used.wait(dve, b, NT)
                dve.tensor_tensor(Y[:, b, :], X[:, b, :], PS[:, 6, :], ALU.add).then_inc(out_kept.sem, 1)


TERMS = [(0, 0), (0, 1), (1, 0), (0, 2), (2, 0), (1, 1)]


def attn(nc, tag, X, Y, PS, C, W, causal):
    D = 8 if causal else 4
    SW = 64 if causal else 32
    HG = P // SW
    NG = 8
    NO = NG * HG // 4
    MR = 6 * D
    NU = TT * HG
    NPR = HG // 2
    STEPS = NG * TT
    with ExitStack() as ctx:
        s = Stage(nc, ctx)
        xs = s.sb(f"{tag}_xs", [P, T])
        qk = s.sb(f"{tag}_qk", [P, 2, T])
        rot = s.sb(f"{tag}_rot", [P, 2, T])
        qk_parts = s.sb(f"{tag}_qk_parts", [P, 3, 2, T], BF16)
        q_str = s.sb(f"{tag}_q_str", [P, NG, T], BF16)
        k_str = s.sb(f"{tag}_k_str", [P, NG, T], BF16)
        q_max = s.sb(f"{tag}_q_max", [P, 2, T], BF16)
        v_aug = s.sb(f"{tag}_v_aug", [P, TT, 16, 32])
        mx = s.sb(f"{tag}_mx", [P, 2, TT, HG])
        mx_rest = s.sb(f"{tag}_mx_rest", [P, TT, HG])
        neg_max = s.sb(f"{tag}_neg_max", [P, 2, TT, P], BF16)
        probs = s.sb(f"{tag}_probs", [P, 3, HG, T])
        o_raw = s.sb(f"{tag}_o_raw", [P, NO, T])
        rsum = s.sb(f"{tag}_rsum", [P, 2, T])
        oc = s.sb(f"{tag}_oc", [P, 2, T])
        sq = s.sb(f"{tag}_sq", [P, T])
        lam = s.sb(f"{tag}_lam", [P, 8])
        set_up = s.sem(f"{tag}_set_up")
        lam_in = s.sem(f"{tag}_lam_in")
        lam_exp = s.sem(f"{tag}_lam_exp")
        lam_step = s.sem(f"{tag}_lam_step")
        xs_ready = s.sig(f"{tag}_xs_ready", 1)
        qk_ready = s.sig(f"{tag}_qk_ready", 1)
        v_ready = s.sig(f"{tag}_v_ready", 1)
        v_kept = s.sig(f"{tag}_v_kept", 1)
        split_step = s.sig(f"{tag}_split_step", 6 if not causal else 5)
        parts_ready = s.sig(f"{tag}_parts_ready", 1)
        spread = s.sig(f"{tag}_spread", 2 * NG)
        q_kept = s.sig(f"{tag}_q_kept", NG)
        k_kept = s.sig(f"{tag}_k_kept", NG)
        scored = s.sig(f"{tag}_scored", NG * NU)
        maxed = s.sig(f"{tag}_maxed", NG * NU)
        max_step = s.sig(f"{tag}_max_step", 3 * NG)
        neg_ready = s.sig(f"{tag}_neg_ready", NG)
        neg_turned = s.sig(f"{tag}_neg_turned", NG)
        q_max_ready = s.sig(f"{tag}_q_max_ready", NG)
        shifted = s.sig(f"{tag}_shifted", STEPS * NPR)
        exped = s.sig(f"{tag}_exped", STEPS * NPR)
        pv_done = s.sig(f"{tag}_pv_done", STEPS)
        o_kept = s.sig(f"{tag}_o_kept", NO)
        gathered = s.sig(f"{tag}_gathered", 1)
        post = s.sig(f"{tag}_post", 1 if causal else 7)
        squares = s.sig(f"{tag}_squares", 1)
        ms_ready = s.sig(f"{tag}_ms_ready", 1)
        rms_ready = s.sig(f"{tag}_rms_ready", 1)
        o_ready = s.sig(f"{tag}_o_ready", 1)
        projected = s.sig(f"{tag}_projected", 1)
        done = s.sig(f"{tag}_done", 1)
        block = ctx.enter_context(nc.Block())
        NEGT = PS[:, 7, 0:T // 2].bitcast(BF16)

        def o_tile(g):
            return (g // 2, (g % 2) * 2) if causal else (g, 0)

        def head_v(g, j):
            return 2 * g + j if causal else 4 * (g % 4) + j

        def keys(tt):
            return (tt + 1) * P if causal else T

        def first_query(st):
            return st * P if causal else 0

        def keep_o(act, b, g):
            o, slot = o_tile(g)
            if slot + HG == 4:
                pv_done.wait(act, b, (g + 1) * TT)
                act.activation(o_raw[:, o, :], PS[:, 6, :], ACT.Copy).then_inc(o_kept.sem, 1)

        @block.sync
        def _(sp):
            C["load"](sp, tag)

        @block.gpsimd
        def _(pool):
            pool.memset(neg_max[:, :, :, :], 0.0).then_inc(set_up, 1)
            pool.memset(v_aug[:, :, :, :], 0.0).then_inc(set_up, 1)
            pool.wait_ge(set_up, 2)
            pool.memset(v_aug[:, :, :, 8:9], 1.0).then_inc(set_up, 1)

        @block.tensor
        def _(pe):
            C["weights"](pe, tag)

            def pass1(b, g, tt):
                for j in range(HG):
                    u = g * NU + tt * HG + j
                    if u >= 2:
                        maxed.wait(pe, b, u - 1)
                    strip = slice(SW * j, SW * (j + 1))
                    n = keys(tt)
                    mm = pe.matmul(PS[:, u % 2, 0:n], q_str[strip, g, bass.ts(tt, P)], k_str[strip, g, 0:n],
                                   start=True, stop=not causal)
                    if causal:
                        mm = pe.matmul(PS[:, u % 2, tt * P:n], C["ident_bf"], W["mask"],
                                       start=False, stop=True)
                    mm.then_inc(scored.sem, 1)

            def pass2(b, g, st):
                if st == 0:
                    q_max_ready.wait(pe, b, g + 1)
                t0 = first_query(st)
                for pr in range(NPR):
                    v = (g * TT + st) * NPR + pr
                    if v >= 2:
                        exped.wait(pe, b, v - 1)
                    for j in (2 * pr, 2 * pr + 1):
                        bank = 2 + 2 * (v % 2) + j % 2
                        strip = slice(SW * j, SW * (j + 1))
                        mm = pe.matmul(PS[:, bank, 0:T - t0], k_str[strip, g, bass.ts(st, P)],
                                       q_max[strip, g % 2, t0:T], start=True, stop=not causal)
                        if causal:
                            mm = pe.matmul(PS[:, bank, 0:P], C["ident_bf"], W["mask_t"], start=False, stop=True)
                    mm.then_inc(shifted.sem, 1)

            def pv(b, g, st):
                o, slot = o_tile(g)
                exped.wait(pe, b, (g * TT + st + 1) * NPR)
                if st == 0 and slot == 0 and o > 0:
                    o_kept.wait(pe, b, o)
                t0 = first_query(st)
                for j in range(HG):
                    at = 32 * (slot + j)
                    mm = pe.matmul(PS[at:at + 32, 6, t0:T], v_aug[:, st, head_v(g, j), :],
                                   probs[:, (g * TT + st) % 3, j, 0:T - t0], start=(st == 0), stop=(st == TT - 1))
                mm.then_inc(pv_done.sem, 1)

            def turn_max(b, g):
                neg_ready.wait(pe, b, g + 1)
                if g >= 1:
                    q_max_ready.wait(pe, b, g)
                for tt in range(TT):
                    mm = pe.transpose(NEGT[:, bass.ts(tt, P)], neg_max[:, g % 2, tt, :], C["ident_bf"])
                mm.then_inc(neg_turned.sem, 1)

            with pe.Fori(0, NB) as b:
                done.wait(pe, b, 0)
                for n, name in enumerate(["q", "k"] if causal else ["q", "k", "q_sw", "k_sw"]):
                    mm = pe.matmul(PS[:, n, :], W[name], X[:, b, :], start=True, stop=True)
                mm.then_inc(qk_ready.sem, 1)
                xs_ready.wait(pe, b, 1)
                for st in range(TT):
                    mm = pe.matmul(PS[:, 7, bass.ts(st, P)], xs[:, bass.ts(st, P)], W["v"], start=True, stop=True)
                mm.then_inc(v_ready.sem, 1)
                parts_ready.wait(pe, b, 1)
                for g in range(NG):
                    for n, kept in enumerate((q_kept, k_kept)):
                        if g >= 2:
                            kept.wait(pe, b, g - 1)
                        for i in range(3):
                            at = ((n * 3 + i) * NG + g) * P
                            mm = pe.matmul(PS[:, 2 + 2 * n + g % 2, :], W["strips"][:, at:at + P],
                                           qk_parts[:, i, n, :], start=(i == 0), stop=(i == 2))
                        mm.then_inc(spread.sem, 1)
                q_kept.wait(pe, b, NG)
                k_kept.wait(pe, b, NG)
                v_kept.wait(pe, b, 1)
                for g in range(2):
                    for tt in range(TT):
                        pass1(b, g, tt)
                turn_max(b, 0)
                for g in range(NG):
                    for st in range(TT):
                        if g + 2 < NG:
                            pass1(b, g + 2, st)
                        pass2(b, g, st)
                        if (g, st) > (0, 0):
                            pv(b, *((g, st - 1) if st else (g - 1, TT - 1)))
                        if st == 1 and g + 1 < NG:
                            turn_max(b, g + 1)
                pv(b, NG - 1, TT - 1)
                o_kept.wait(pe, b, NO)
                maxed.wait(pe, b, NG * NU)
                for par in range(NO // 4):
                    for n, name in enumerate(("pick_o", "pick_sum")):
                        for i in range(4):
                            mm = pe.matmul(PS[32 * i:32 * i + 32, 2 * par + n, :], W[name],
                                           o_raw[:, 4 * par + i, :], start=True, stop=True)
                mm.then_inc(gathered.sem, 1)
                if not causal:
                    squares.wait(pe, b, 1)
                    pe.matmul(PS[:, 4, :], W["mean8"], sq[:, :], start=True, stop=True).then_inc(ms_ready.sem, 1)
                o_ready.wait(pe, b, 1)
                pe.matmul(PS[:, 5, :], W["out"], oc[:, 0, :], start=True, stop=True).then_inc(projected.sem, 1)

        @block.scalar
        def _(act):
            C["weights"](act, tag)
            if not causal:
                act.wait_ge(lam_in, 1)
                act.activation(lam[:, 2:4], lam[:, 0:2], ACT.Exp).then_inc(lam_exp, 1)
            with act.Fori(0, NB) as b:
                done.wait(act, b, 0)
                act.activation(xs[:, :], X[:, b, :], ACT.Copy).then_inc(xs_ready.sem, 1)
                for g in range(NG):
                    spread.wait(act, b, 2 * g + 2)
                    act.activation(k_str[:, g, :], PS[:, 4 + g % 2, :], ACT.Identity, bias=W["ones_rows"])\
                       .then_inc(k_kept.sem, 1)
                for g in range(NG):
                    for st in range(TT):
                        n = T - first_query(st)
                        step = g * TT + st
                        if step >= 3:
                            pv_done.wait(act, b, step - 2)
                        for pr in range(NPR):
                            v = step * NPR + pr
                            shifted.wait(act, b, v + 1)
                            bank = 2 + 2 * (v % 2)
                            act.activation(probs[:, step % 3, 2 * pr:2 * pr + 2, 0:n], PS[:, bank:bank + 2, 0:n],
                                           ACT.Exp).then_inc(exped.sem, 1)
                        if st == 0 and g > 0:
                            keep_o(act, b, g - 1)
                keep_o(act, b, NG - 1)
                if not causal:
                    post.wait(act, b, 5)
                    act.activation(sq[:, :], oc[:, 0, :], ACT.Square).then_inc(squares.sem, 1)
                    ms_ready.wait(act, b, 1)
                    act.activation(rsum[:, 0, :], PS[:, 4, :], ACT.Sqrt, bias=W["eps"]).then_inc(rms_ready.sem, 1)

        @block.vector
        def _(dve):
            C["weights"](dve, tag)
            if not causal:
                for n in range(2):
                    dve.tensor_tensor(sq[:, 4 * n:4 * n + 4], W["lam_q"][:, 4 * n:4 * n + 4],
                                      W["lam_k"][:, 4 * n:4 * n + 4], ALU.mult).then_inc(lam_step, 1)
                dve.wait_ge(lam_step, 2)
                dve.tensor_reduce(lam[:, 0:2], sq[:, 0:8].rearrange("p (n e) -> p n e", e=4), AX, ALU.add)\
                   .then_inc(lam_in, 1)
                dve.wait_ge(lam_exp, 1)
                dve.tensor_tensor(lam[:, 4:5], lam[:, 3:4], lam[:, 2:3], ALU.subtract).then_inc(lam_step, 1)
                dve.wait_ge(lam_step, 3)
                dve.tensor_scalar(lam[:, 5:6], lam[:, 4:5], -LAMBDA_INIT, None, ALU.add).then_inc(lam_step, 1)
                dve.wait_ge(lam_step, 4)
            dve.wait_ge(set_up, 3)

            def maxima(b, g, tt):
                for j in range(HG):
                    u = g * NU + tt * HG + j
                    scored.wait(dve, b, u + 1)
                    if tt == 0 and j == 0 and g >= 2:
                        max_step.wait(dve, b, 3 * (g - 1))
                    dve.tensor_reduce(mx[:, g % 2, tt, j:j + 1], PS[:, u % 2, 0:keys(tt)], AX, ALU.max)\
                       .then_inc(maxed.sem, 1)

            def negate(b, g):
                rows = neg_max[:, g % 2, :, :].rearrange("p t (j w) -> p t j w", w=SW)
                maxed.wait(dve, b, (g + 1) * NU)
                if g >= 2:
                    neg_turned.wait(dve, b, g - 1)
                m = mx[:, g % 2, :, :]
                dve.tensor_scalar(rows[:, :, :, MR], m, -1.0, None, ALU.mult).then_inc(max_step.sem, 1)
                max_step.wait(dve, b, 3 * g + 1)
                if g >= 1:
                    neg_ready.wait(dve, b, g)
                dve.scalar_tensor_tensor(mx_rest[:, :, :], m, -1.0, rows[:, :, :, MR], ALU.mult, ALU.subtract)\
                   .then_inc(max_step.sem, 1)
                max_step.wait(dve, b, 3 * g + 2)
                dve.tensor_copy(rows[:, :, :, MR + 1], mx_rest[:, :, :]).then_inc(max_step.sem, 1)
                max_step.wait(dve, b, 3 * g + 3)
                dve.tensor_tensor(rows[:, :, :, MR + 2], mx_rest[:, :, :], rows[:, :, :, MR + 1], ALU.subtract)\
                   .then_inc(neg_ready.sem, 1)

            def add_max(b, g):
                neg_turned.wait(dve, b, g + 1)
                if g >= 2:
                    shifted.wait(dve, b, (g - 1) * TT * NPR)
                dve.tensor_tensor(q_max[:, g % 2, :], q_str[:, g, :], NEGT, ALU.add).then_inc(q_max_ready.sem, 1)

            with dve.Fori(0, NB) as b:
                qk_ready.wait(dve, b, 1)
                done.wait(dve, b, 0)
                if causal:
                    dve.tensor_scalar(qk[:, 0, :], PS[:, 0, :], float(D) ** -0.5, None, ALU.mult)\
                       .then_inc(split_step.sem, 1)
                    dve.tensor_copy(qk[:, 1, :], PS[:, 1, :]).then_inc(split_step.sem, 1)
                    n = 2
                else:
                    cos = W["cos"].rearrange("p (n t) -> p n t", n=2)
                    sin = W["sin"].rearrange("p (n t) -> p n t", n=2)
                    dve.tensor_tensor(qk[:, :, :], PS[:, 0:2, :], cos, ALU.mult).then_inc(split_step.sem, 1)
                    dve.tensor_tensor(rot[:, :, :], PS[:, 2:4, :], sin, ALU.mult).then_inc(split_step.sem, 1)
                    split_step.wait(dve, b, 2)
                    dve.tensor_tensor(qk[:, :, :], qk[:, :, :], rot[:, :, :], ALU.add).then_inc(split_step.sem, 1)
                    n = 3
                split_step.wait(dve, b, n)
                dve.tensor_copy(qk_parts[:, 0, :, :], qk[:, :, :]).then_inc(split_step.sem, 1)
                split_step.wait(dve, b, n + 1)
                dve.tensor_tensor(qk[:, :, :], qk[:, :, :], qk_parts[:, 0, :, :], ALU.subtract)\
                   .then_inc(split_step.sem, 1)
                split_step.wait(dve, b, n + 2)
                dve.tensor_copy(qk_parts[:, 1, :, :], qk[:, :, :]).then_inc(split_step.sem, 1)
                split_step.wait(dve, b, n + 3)
                dve.tensor_tensor(qk_parts[:, 2, :, :], qk[:, :, :], qk_parts[:, 1, :, :], ALU.subtract)\
                   .then_inc(parts_ready.sem, 1)
                v_ready.wait(dve, b, 1)
                dve.tensor_copy(v_aug[:, :, :, 0:8].rearrange("p s h e -> p (s h) e"),
                                PS[:, 7, :].rearrange("p (sh e) -> p sh e", e=8)).then_inc(v_kept.sem, 1)
                for g in range(NG):
                    spread.wait(dve, b, 2 * g + 1)
                    dve.tensor_copy(q_str[:, g, :], PS[:, 2 + g % 2, :]).then_inc(q_kept.sem, 1)
                for g in range(2):
                    for tt in range(TT):
                        maxima(b, g, tt)
                    negate(b, g)
                q_kept.wait(dve, b, NG)
                add_max(b, 0)
                for g in range(NG):
                    for st in range(TT):
                        if g + 2 < NG:
                            maxima(b, g + 2, st)
                        if st == 1 and g + 1 < NG:
                            add_max(b, g + 1)
                    if g + 2 < NG:
                        negate(b, g + 2)
                gathered.wait(dve, b, 1)
                if causal:
                    dve.reciprocal(rsum[:, 0, :], PS[:, 1, :]).then_inc(post.sem, 1)
                    post.wait(dve, b, 1)
                    dve.tensor_tensor(oc[:, 0, :], PS[:, 0, :], rsum[:, 0, :], ALU.mult).then_inc(o_ready.sem, 1)
                    projected.wait(dve, b, 1)
                    dve.scalar_tensor_tensor(Y[:, b, :], PS[:, 5, :], W["b_out"], X[:, b, :], ALU.add, ALU.add)\
                       .then_inc(done.sem, 1)
                else:
                    for par in range(2):
                        dve.reciprocal(rsum[:, par, :], PS[:, 2 * par + 1, :]).then_inc(post.sem, 1)
                    post.wait(dve, b, 2)
                    for par in range(2):
                        dve.tensor_tensor(oc[:, par, :], PS[:, 2 * par, :], rsum[:, par, :], ALU.mult)\
                           .then_inc(post.sem, 1)
                    post.wait(dve, b, 4)
                    dve.scalar_tensor_tensor(oc[:, 0, :], oc[:, 1, :], lam[:, 5:6], oc[:, 0, :], ALU.mult, ALU.add)\
                       .then_inc(post.sem, 1)
                    rms_ready.wait(dve, b, 1)
                    dve.reciprocal(rsum[:, 1, :], rsum[:, 0, :]).then_inc(post.sem, 1)
                    post.wait(dve, b, 6)
                    dve.tensor_tensor(oc[:, 1, :], oc[:, 0, :], rsum[:, 1, :], ALU.mult).then_inc(post.sem, 1)
                    post.wait(dve, b, 7)
                    dve.tensor_scalar(oc[:, 0, :], oc[:, 1, :], W["subln"], 1.0 - LAMBDA_INIT, ALU.mult, ALU.mult)\
                       .then_inc(o_ready.sem, 1)
                    projected.wait(dve, b, 1)
                    dve.tensor_tensor(Y[:, b, :], PS[:, 5, :], X[:, b, :], ALU.add).then_inc(done.sem, 1)


def attn0(nc, tag, X, Y, PS, C, W, scratch):
    W1 = 63
    NQ, NK, H = 4, 4, 8
    NCH = 2 * NQ * NK
    RING = 3
    GATE = ACT.Gelu
    with ExitStack() as ctx:
        s = Stage(nc, ctx)
        disp = s.sb(f"{tag}_disp", [P, 2, T])
        a_pad = s.sb(f"{tag}_a_pad", [P, 2, 2, W1 + T])
        d_pad = s.sb(f"{tag}_d_pad", [P, 2, 2, W1 + T])
        x_pad = s.sb(f"{tag}_x_pad", [P, W1 + T + 1])
        v_tok = s.sb(f"{tag}_v_tok", [P, 2, 8, P])
        pos = s.sb(f"{tag}_pos", [P, 64])
        b_half = s.sb(f"{tag}_b_half", [P, 1])
        bond = s.sb(f"{tag}_bond", [P, RING, 4, T])
        dmg = s.sb(f"{tag}_dmg", [P, RING, 4, T])
        tanh = s.sb(f"{tag}_tanh", [P, 2, T])
        logit = s.sb(f"{tag}_logit", [P, 2, 8, T])
        probs = s.sb(f"{tag}_probs", [P, TT, 16, 64])
        masked = s.sb(f"{tag}_masked", [P, 2, T])
        mx = s.sb(f"{tag}_mx", [P, 16])
        tot = s.sb(f"{tag}_tot", [P, TT, 16])
        rtot = s.sb(f"{tag}_rtot", [P, TT, 16])
        band = s.sb(f"{tag}_band", [P, 2, 16, P])
        band_t = s.sb(f"{tag}_band_t", [P, 16, P])
        o_tok = s.sb(f"{tag}_o_tok", [P, P])
        o_t = s.sb(f"{tag}_o_t", [P, T])
        set_up = s.sem(f"{tag}_set_up")
        zeroed = s.sem(f"{tag}_zeroed")
        pos_ready = s.sem(f"{tag}_pos_ready")
        pos_kept = s.sem(f"{tag}_pos_kept")
        x_kept = s.sig(f"{tag}_x_kept", 1)
        disp_ready = s.sig(f"{tag}_disp_ready", 1)
        disp_kept = s.sig(f"{tag}_disp_kept", 1)
        a_ready = s.sig(f"{tag}_a_ready", 1)
        a_kept = s.sig(f"{tag}_a_kept", 1)
        d_ready = s.sig(f"{tag}_d_ready", 1)
        d_kept = s.sig(f"{tag}_d_kept", 1)
        v_ready = s.sig(f"{tag}_v_ready", 1)
        v_kept = s.sig(f"{tag}_v_kept", 1)
        bond_in = s.sig(f"{tag}_bond_in", NCH)
        dmg_in_pool = s.sig(f"{tag}_dmg_in_pool", NCH * 3 // 4)
        dmg_in_dve = s.sig(f"{tag}_dmg_in_dve", NCH // 4)
        bond_gelu = s.sig(f"{tag}_bond_gelu", NCH)
        dmg_gelu = s.sig(f"{tag}_dmg_gelu", NCH)
        bond_used = s.sig(f"{tag}_bond_used", NCH)
        dmg_used = s.sig(f"{tag}_dmg_used", NCH)
        tanh_ready = s.sig(f"{tag}_tanh_ready", 8)
        logit_ready = s.sig(f"{tag}_logit_ready", 8)
        turned = s.sig(f"{tag}_turned", TT)
        masked_ready = s.sig(f"{tag}_masked_ready", 1)
        maxed = s.sig(f"{tag}_maxed", TT)
        centred = s.sig(f"{tag}_centred", TT)
        exped = s.sig(f"{tag}_exped", 1)
        summed = s.sig(f"{tag}_summed", 1)
        inverted = s.sig(f"{tag}_inverted", 1)
        skewed = [s.sig(f"{tag}_skewed{i}", 32) for i in range(TT)]
        banded = [s.sig(f"{tag}_banded{i}", 16) for i in range(TT)]
        band_turned = s.sig(f"{tag}_band_turned", 4 * TT)
        band_kept_act = s.sig(f"{tag}_band_kept_act", 2 * TT)
        band_kept_dve = s.sig(f"{tag}_band_kept_dve", 2 * TT)
        pv_done = s.sig(f"{tag}_pv_done", TT)
        o_scaled = s.sig(f"{tag}_o_scaled", TT)
        o_turned = s.sig(f"{tag}_o_turned", TT)
        o_kept = s.sig(f"{tag}_o_kept", TT)
        projected = s.sig(f"{tag}_projected", 1)
        y_done = s.sig(f"{tag}_y_done", 1)
        block = ctx.enter_context(nc.Block())

        TILE = 16 * 2 * 64 * P

        def chunk(n):
            return n // 16, (n // 4) % 4, n % 4

        def batches(eng, body, tail):
            body(0, 0, None, 1)
            body(1, 1, 0, 2)
            with eng.Fori(1, NB // 2 - 1) as i:
                body(i * 2, 0, i * 2 - 1, i * 2 + 1)
                body(i * 2 + 1, 1, i * 2, i * 2 + 2)
            body(NB - 2, 0, NB - 3, NB - 1)
            body(NB - 1, 1, NB - 2, None)
            tail(NB - 1, 1)

        def plan(n):
            if n in (1, 3, 5, 7):
                return "soften", (n - 1) // 2
            if n == 9:
                return "exp", 0
            if n in (14, 17, 20, 23):
                return "combine", (n - 14) // 3
            if n == 26:
                return "finish", 0
            if n == 28:
                return "project", 0
            return None, 0

        def damage(eng, par, n):
            g, q, k = chunk(n)
            d0 = 16 * q + k
            row = d_pad[:, par, g, :]
            part = [row.ap[0][0], row.ap[0][1]]
            later = bass.AP(tensor=row.tensor, offset=row.offset + d0, ap=[part, [4, 4], [1, T]])
            own = bass.AP(tensor=row.tensor, offset=row.offset + W1, ap=[part, [0, 4], [1, T]])
            return eng.tensor_tensor(dmg[:, n % RING, :, :], later, own, ALU.subtract)

        @block.sync
        def _(sp):
            C["load"](sp, tag)
            sp.wait_ge(set_up, 5)
            for i in range(TT):
                for part in range(2):
                    base = (2 * i + part) * P * 16 * 64
                    sp.dma_start(scratch[base:base + P * 16 * 64].rearrange("(p c) -> p c", p=P),
                                 probs[:, 0, :, :].rearrange("p h d -> p (h d)")).then_inc(zeroed, 16)
            sp.wait_ge(zeroed, 16 * 2 * TT)

            def skew(b):
                for tt in range(TT):
                    base = tt * TILE
                    if tt == 0:
                        exped.wait(sp, b, 1)
                    banded[tt].wait(sp, b, 0)
                    for half in range(2):
                        dst = bass.AP(
                            tensor=scratch.tensor, offset=scratch.offset + base + half * 64 * P,
                            ap=[[P + 1, 64], [2 * 64 * P, 16], [1, 64]])
                        sp.dma_start(dst, probs[64 * half:64 * half + 64, tt, :, :]).then_inc(skewed[tt].sem, 16)
                    skewed[tt].wait(sp, b, 32)
                    if tt >= 2:
                        band_turned.wait(sp, b, 4 * (tt - 1))
                    else:
                        band_turned.wait(sp, b, 0)
                    src = bass.AP(tensor=scratch.tensor, offset=scratch.offset + base,
                                  ap=[[P, P], [2 * 64 * P, 16], [1, P]])
                    sp.dma_start(band[:, tt % 2, :, :], src).then_inc(banded[tt].sem, 16)

            for b in range(NB):
                skew(b)

        @block.gpsimd
        def _(pool):
            pool.memset(a_pad[:, :, :, 0:W1], 0.0).then_inc(set_up, 1)
            pool.memset(d_pad[:, :, :, 0:W1], 0.0).then_inc(set_up, 1)
            pool.memset(x_pad[:, 0:W1], 0.0).then_inc(set_up, 1)
            pool.memset(x_pad[:, W1 + T:W1 + T + 1], 0.0).then_inc(set_up, 1)
            pool.memset(probs[:, 0, :, :], 0.0).then_inc(set_up, 1)
            pool.wait_ge(set_up, 5)

            def body(b, par, before, after):
                d_kept.wait(pool, b, 1)
                for n in range(NCH):
                    g, q, k = chunk(n)
                    if k == 3:
                        continue
                    if n >= RING:
                        dmg_used.wait(pool, b, n - RING + 1)
                    else:
                        dmg_used.wait(pool, b, 0)
                    damage(pool, par, n).then_inc(dmg_in_pool.sem, 1)

            batches(pool, body, lambda b, par: None)

        @block.tensor
        def _(pe):
            C["weights"](pe, tag)
            pe.matmul(PS[:, 0, 0:64], W["w_pos"], W["rel"], start=True, stop=True).then_inc(pos_ready, 1)
            pe.wait_ge(pos_kept, 1)

            def project(b, par, before):
                if before is not None:
                    y_done.wait(pe, before, 1)
                for g in range(2):
                    mm = pe.matmul(PS[:, 4 + g, :], W["disp"][:, bass.ts(g, P)], X[:, b, :], start=True, stop=True)
                mm.then_inc(disp_ready.sem, 1)
                disp_kept.wait(pe, b, 1)
                for g in range(2):
                    mm = pe.matmul(PS[:, 6 + g, :], W["strain"], disp[:, g, :], start=True, stop=True)
                mm.then_inc(a_ready.sem, 1)
                for g in range(2):
                    mm = pe.matmul(PS[:, 4 + g, :], W["dmg"], disp[:, g, :], start=True, stop=True)
                mm.then_inc(d_ready.sem, 1)
                a_kept.wait(pe, b, 1)
                x_kept.wait(pe, b, 1)
                for j in range(8):
                    mm = pe.matmul(PS[:, 6 + j // 4, bass.ts(j % 4, P)], x_pad[:, 64 * j:64 * j + P], W["val"],
                                   start=True, stop=True)
                mm.then_inc(v_ready.sem, 1)
                d_kept.wait(pe, b, 1)
                v_kept.wait(pe, b, 1)

            def soften(b, par, tt):
                logit_ready.wait(pe, b, 8)
                if tt >= 1:
                    centred.wait(pe, b, tt)
                for g in range(2):
                    for q in range(NQ):
                        mm = pe.transpose(PS[:, 4 + g, bass.ts(q, P)], logit[:, par, 4 * g + q, bass.ts(tt, P)],
                                          C["ident"])
                mm.then_inc(turned.sem, 1)

            def combine(b, par, tt):
                banded[tt].wait(pe, b, 16)
                for r in range(4):
                    if tt >= 1 or r >= 2:
                        m = 4 * tt + r - 2
                        (band_kept_act if m % 2 == 0 else band_kept_dve).wait(pe, b, m // 2 + 1)
                    for hh in range(4):
                        mm = pe.transpose(PS[:, 6 + r % 2, bass.ts(hh, P)], band[:, tt % 2, 4 * r + hh, :],
                                          C["ident"])
                    mm.then_inc(band_turned.sem, 1)
                band_kept_act.wait(pe, b, 2 * tt + 2)
                band_kept_dve.wait(pe, b, 2 * tt + 2)
                if tt >= 1:
                    o_scaled.wait(pe, b, tt)
                else:
                    centred.wait(pe, b, TT)
                for h in range(16):
                    for half in range(2):
                        rows = slice(64 * half, 64 * half + 64)
                        mm = pe.matmul(PS[rows, 4, 8 * h:8 * h + 8], band_t[:, h, rows],
                                       v_tok[:, par, 2 * tt + half, 8 * h:8 * h + 8], start=True, stop=True)
                mm.then_inc(pv_done.sem, 1)
                o_scaled.wait(pe, b, tt + 1)
                if tt >= 1:
                    o_kept.wait(pe, b, tt)
                pe.transpose(PS[:, 5, 0:P], o_tok[:, :], C["ident"]).then_inc(o_turned.sem, 1)

            def finish(b):
                o_kept.wait(pe, b, TT)
                pe.matmul(PS[:, 5, :], W["c_proj"], o_t[:, :], start=True, stop=True).then_inc(projected.sem, 1)

            def body(b, par, before, after):
                for n in range(NCH):
                    g, q, k = chunk(n)
                    gq = n // 4
                    if k == 0:
                        if gq >= 2:
                            tanh_ready.wait(pe, b, gq - 1)
                            logit_ready.wait(pe, b, gq - 1)
                        else:
                            tanh_ready.wait(pe, b, 0)
                            logit_ready.wait(pe, b, 0)
                    for bank, data, ready, used, wname in ((gq % 2, bond, bond_gelu, bond_used, "w_bond"),
                                                           (2 + gq % 2, dmg, dmg_gelu, dmg_used, "w_dmg_out")):
                        ready.wait(pe, b, n + 1)
                        for c in range(4):
                            mm = pe.matmul(PS[32 * c:32 * c + 32, bank, :], W[wname][:, 32 * k:32 * k + 32],
                                           data[:, n % RING, c, :], start=(k == 0), stop=(k == 3))
                        mm.then_inc(used.sem, 1)
                    what, tt = plan(n)
                    if what == "soften" and before is not None:
                        soften(before, 1 - par, tt)
                    elif what == "combine" and before is not None:
                        combine(before, 1 - par, tt)
                    elif what == "finish" and before is not None:
                        finish(before)
                    elif what == "project" and after is not None:
                        project(after, 1 - par, before)

            def tail(b, par):
                for tt in range(TT):
                    soften(b, par, tt)
                for tt in range(TT):
                    combine(b, par, tt)
                finish(b)

            project(0, 0, None)
            batches(pe, body, tail)

        @block.scalar
        def _(act):
            C["weights"](act, tag)
            act.wait_ge(set_up, 5)
            act.wait_ge(pos_kept, 2)

            def project(b, par):
                v_ready.wait(act, b, 0)
                act.activation(x_pad[:, W1:W1 + T], X[:, b, :], ACT.Copy).then_inc(x_kept.sem, 1)
                disp_ready.wait(act, b, 1)
                act.activation(disp[:, :, :], PS[:, 4:6, :], ACT.Copy).then_inc(disp_kept.sem, 1)
                v_ready.wait(act, b, 1)
                act.activation(v_tok[:, par, :, :].rearrange("p j c -> p (j c)"),
                               PS[:, 6:8, :].rearrange("p a c -> p (a c)"), ACT.Copy).then_inc(v_kept.sem, 1)

            def exps(b):
                centred.wait(act, b, TT)
                act.activation(probs[:, :, :, :], probs[:, :, :, :], ACT.Exp).then_inc(exped.sem, 1)

            def combine(b, tt):
                for r in (0, 2):
                    band_turned.wait(act, b, 4 * tt + r + 1)
                    if tt >= 1:
                        pv_done.wait(act, b, tt)
                    else:
                        pv_done.wait(act, b, 0)
                    act.activation(band_t[:, 4 * r:4 * r + 4, :], PS[:, 6, :].rearrange("p (h t) -> p h t", h=4),
                                   ACT.Copy).then_inc(band_kept_act.sem, 1)

            def to_tanh(b, gq):
                dmg_used.wait(act, b, 4 * gq + 4)
                if gq >= 2:
                    logit_ready.wait(act, b, gq - 1)
                else:
                    logit_ready.wait(act, b, 0)
                act.activation(tanh[:, gq % 2, :], PS[:, 2 + gq % 2, :], ACT.Tanh, bias=b_half[:, :], scale=0.5)\
                   .then_inc(tanh_ready.sem, 1)

            def body(b, par, before, after):
                for n in range(NCH):
                    g, q, k = chunk(n)
                    bond_in.wait(act, b, n + 1)
                    act.activation(bond[:, n % RING, :, :], bond[:, n % RING, :, :], GATE).then_inc(bond_gelu.sem, 1)
                    if k == 3:
                        dmg_in_dve.wait(act, b, n // 4 + 1)
                    else:
                        dmg_in_pool.wait(act, b, 3 * (n // 4) + k + 1)
                    act.activation(dmg[:, n % RING, :, :], dmg[:, n % RING, :, :], GATE, bias=W["b_dmg"])\
                       .then_inc(dmg_gelu.sem, 1)
                    if k == 0 and n > 0:
                        to_tanh(b, n // 4 - 1)
                    what, tt = plan(n)
                    if what == "exp" and before is not None:
                        exps(before)
                    elif what == "combine" and before is not None:
                        combine(before, tt)
                    elif what == "project" and after is not None:
                        project(after, 1 - par)
                to_tanh(b, 7)

            def tail(b, par):
                exps(b)
                for tt in range(TT):
                    combine(b, tt)

            project(0, 0)
            batches(act, body, tail)

        @block.vector
        def _(dve):
            C["weights"](dve, tag)
            dve.wait_ge(set_up, 5)
            dve.wait_ge(pos_ready, 1)
            dve.tensor_copy(pos[:, :], PS[:, 0, 0:64]).then_inc(pos_kept, 1)
            dve.tensor_scalar(b_half[:, :], W["b_out"], 0.5, None, ALU.mult).then_inc(pos_kept, 1)
            dve.wait_ge(pos_kept, 2)
            dve.wait_ge(zeroed, 16 * 2 * TT)

            def project(b, par):
                a_ready.wait(dve, b, 1)
                dve.tensor_copy(a_pad[:, par, :, W1:W1 + T], PS[:, 6:8, :]).then_inc(a_kept.sem, 1)
                d_ready.wait(dve, b, 1)
                dve.tensor_copy(d_pad[:, par, :, W1:W1 + T], PS[:, 4:6, :]).then_inc(d_kept.sem, 1)

            def soften(b, tt):
                turned.wait(dve, b, tt + 1)
                skewed[tt].wait(dve, b, 0)
                src = PS[:, 4:6, :]
                if tt == 0:
                    dve.tensor_tensor(masked[:, :, :], src, W["mask"].rearrange("p (g c) -> p g c", g=2), ALU.add)\
                       .then_inc(masked_ready.sem, 1)
                    masked_ready.wait(dve, b, 1)
                    summed.wait(dve, b, 0)
                    src = masked[:, :, :]
                by_head = src.rearrange("p g (d h) -> p g h d", h=H)
                dve.tensor_reduce(mx[:, :].rearrange("p (g h) -> p g h", g=2), by_head, AX, ALU.max)\
                   .then_inc(maxed.sem, 1)
                maxed.wait(dve, b, tt + 1)
                for g in range(2):
                    m = dve.tensor_tensor(probs[:, tt, 8 * g:8 * g + 8, :],
                                          src[:, g, :].rearrange("p (d h) -> p h d", h=H),
                                          mx[:, 8 * g:8 * g + 8].rearrange("p (h o) -> p h o", o=1)
                                          .to_broadcast([P, H, 64]), ALU.subtract)
                m.then_inc(centred.sem, 1)

            def sums(b):
                exped.wait(dve, b, 1)
                dve.tensor_reduce(tot[:, :, :], probs[:, :, :, :], AX, ALU.add).then_inc(summed.sem, 1)
                summed.wait(dve, b, 1)
                dve.reciprocal(rtot[:, :, :], tot[:, :, :]).then_inc(inverted.sem, 1)

            def combine(b, tt):
                for r in (1, 3):
                    band_turned.wait(dve, b, 4 * tt + r + 1)
                    dve.tensor_copy(band_t[:, 4 * r:4 * r + 4, :], PS[:, 7, :].rearrange("p (h t) -> p h t", h=4))\
                       .then_inc(band_kept_dve.sem, 1)
                pv_done.wait(dve, b, tt + 1)
                inverted.wait(dve, b, 1)
                if tt >= 1:
                    o_turned.wait(dve, b, tt)
                dve.tensor_tensor(o_tok[:, :].rearrange("p (h e) -> p h e", e=8),
                                  PS[:, 4, 0:P].rearrange("p (h e) -> p h e", e=8),
                                  rtot[:, tt, :].rearrange("p (h o) -> p h o", o=1).to_broadcast([P, 16, 8]),
                                  ALU.mult).then_inc(o_scaled.sem, 1)
                o_turned.wait(dve, b, tt + 1)
                dve.tensor_copy(o_t[:, bass.ts(tt, P)], PS[:, 5, 0:P]).then_inc(o_kept.sem, 1)

            def finish(b):
                projected.wait(dve, b, 1)
                dve.tensor_tensor(Y[:, b, :], X[:, b, :], PS[:, 5, :], ALU.add).then_inc(y_done.sem, 1)

            def to_logit(b, par, gq):
                bond_used.wait(dve, b, 4 * gq + 4)
                tanh_ready.wait(dve, b, gq + 1)
                dve.scalar_tensor_tensor(logit[:, par, gq, :], tanh[:, gq % 2, :], -5.0, PS[:, gq % 2, :],
                                         ALU.mult, ALU.add).then_inc(logit_ready.sem, 1)

            def body(b, par, before, after):
                a_kept.wait(dve, b, 1)
                d_kept.wait(dve, b, 1)
                for n in range(NCH):
                    g, q, k = chunk(n)
                    if n >= RING:
                        bond_used.wait(dve, b, n - RING + 1)
                    else:
                        bond_used.wait(dve, b, 0)
                    for c in range(4):
                        d = 16 * q + 4 * c + k
                        m = dve.scalar_tensor_tensor(bond[:, n % RING, c, :], a_pad[:, par, g, d:d + T],
                                                     pos[:, d:d + 1], a_pad[:, par, g, W1:W1 + T],
                                                     ALU.add, ALU.subtract)
                    m.then_inc(bond_in.sem, 1)
                    if k == 3:
                        dmg_used.wait(dve, b, n - RING + 1)
                        damage(dve, par, n).then_inc(dmg_in_dve.sem, 1)
                    if k == 1 and n > 4:
                        to_logit(b, par, n // 4 - 1)
                    what, tt = plan(n)
                    if what == "soften" and before is not None:
                        soften(before, tt)
                    elif what == "exp" and before is not None:
                        sums(before)
                    elif what == "combine" and before is not None:
                        combine(before, tt)
                    elif what == "finish" and before is not None:
                        finish(before)
                    elif what == "project" and after is not None:
                        project(after, 1 - par)
                to_logit(b, par, 7)

            def tail(b, par):
                for tt in range(TT):
                    soften(b, tt)
                sums(b)
                for tt in range(TT):
                    combine(b, tt)
                finish(b)

            project(0, 0)
            batches(dve, body, tail)


def attn2(nc, tag, X, Y, PS, C, W):
    with ExitStack() as ctx:
        s = Stage(nc, ctx)
        q_sb = s.sb(f"{tag}_q", [P, T])
        v_sb = s.sb(f"{tag}_v", [P, T])
        sq = s.sb(f"{tag}_sq", [P, 2, T])
        kv = s.sb(f"{tag}_kv", [P, T])
        scaled = s.sb(f"{tag}_scaled", [P, T])
        norm = s.sb(f"{tag}_norm", [P, 8])
        rnorm = s.sb(f"{tag}_rnorm", [P, 8])
        feat = s.sb(f"{tag}_feat", [P, 1])
        projected = s.sig(f"{tag}_projected", 1)
        squared = s.sig(f"{tag}_squared", 2)
        copied = s.sig(f"{tag}_copied", 2)
        summed = s.sig(f"{tag}_summed", 1)
        norm_ready = s.sig(f"{tag}_norm_ready", 1)
        clipped = s.sig(f"{tag}_clipped", 1)
        rnorm_ready = s.sig(f"{tag}_rnorm_ready", 1)
        spread = s.sig(f"{tag}_spread", 1)
        kv_ready = s.sig(f"{tag}_kv_ready", 1)
        feat_ready = s.sig(f"{tag}_feat_ready", 1)
        scaled_ready = s.sig(f"{tag}_scaled_ready", 1)
        done = s.sig(f"{tag}_done", 1)
        block = ctx.enter_context(nc.Block())

        @block.sync
        def _(sp):
            C["load"](sp, tag)

        @block.tensor
        def _(pe):
            C["weights"](pe, tag)
            with pe.Fori(0, NB) as b:
                done.wait(pe, b, 0)
                for n, name in enumerate(("q", "k", "v")):
                    mm = pe.matmul(PS[:, n, :], W[name], X[:, b, :], start=True, stop=True)
                mm.then_inc(projected.sem, 1)
                for n in range(2):
                    squared.wait(pe, b, n + 1)
                    for t in range(TT):
                        mm = pe.matmul(PS[:, 3, 4 * n + t:4 * n + t + 1], sq[:, n, bass.ts(t, P)],
                                       W["ones"][:, 0:1], start=True, stop=True)
                mm.then_inc(summed.sem, 1)
                rnorm_ready.wait(pe, b, 1)
                for n in range(2):
                    for t in range(TT):
                        col = 4 * n + t
                        mm = pe.matmul(PS[:, 4 + n, bass.ts(t, P)], rnorm[:, col:col + 1].to_broadcast([P, P]),
                                       C["ident"], start=True, stop=True)
                mm.then_inc(spread.sem, 1)

        @block.scalar
        def _(act):
            with act.Fori(0, NB) as b:
                done.wait(act, b, 0)
                projected.wait(act, b, 1)
                for n in range(2):
                    act.activation(sq[:, n, :], PS[:, n, :], ACT.Square).then_inc(squared.sem, 1)
                act.activation(v_sb[:, :], PS[:, 2, :], ACT.Copy).then_inc(copied.sem, 1)
                act.activation(q_sb[:, :], PS[:, 0, :], ACT.Copy).then_inc(copied.sem, 1)
                summed.wait(act, b, 1)
                act.activation(norm[:, :], PS[:, 3, 0:8], ACT.Sqrt).then_inc(norm_ready.sem, 1)

        @block.vector
        def _(dve):
            with dve.Fori(0, NB) as b:
                projected.wait(dve, b, 1)
                copied.wait(dve, b, 1)
                squared.wait(dve, b, 2)
                dve.tensor_tensor(kv[:, :], PS[:, 1, :], v_sb[:, :], ALU.mult).then_inc(kv_ready.sem, 1)
                norm_ready.wait(dve, b, 1)
                dve.tensor_scalar(norm[:, :], norm[:, :], 1e-12, None, ALU.max).then_inc(clipped.sem, 1)
                clipped.wait(dve, b, 1)
                dve.reciprocal(rnorm[:, :], norm[:, :]).then_inc(rnorm_ready.sem, 1)
                spread.wait(dve, b, 1)
                kv_ready.wait(dve, b, 1)
                scaled_ready.wait(dve, b, 0)
                done.wait(dve, b, 0)
                dve.scalar_tensor_tensor(scaled[:, :], kv[:, :], 1.0 / T, PS[:, 5, :], ALU.mult, ALU.mult,
                                         accum_out=feat[:, :]).then_inc(feat_ready.sem, 1)
                feat_ready.wait(dve, b, 1)
                copied.wait(dve, b, 2)
                dve.scalar_tensor_tensor(scaled[:, :], q_sb[:, :], feat[:, 0:1], PS[:, 4, :], ALU.mult, ALU.mult)\
                   .then_inc(scaled_ready.sem, 1)
                scaled_ready.wait(dve, b, 1)
                dve.tensor_tensor(Y[:, b, :], scaled[:, :], X[:, b, :], ALU.add).then_inc(done.sem, 1)


def local_ffn(nc, tag, X, Y, PS, C, W):
    HID_T = 3
    JW = 192
    with ExitStack() as ctx:
        s = Stage(nc, ctx)
        z = s.sb(f"{tag}_z", [P, T])
        h = s.sb(f"{tag}_h", [P, T])
        v = s.sb(f"{tag}_v", [P, TT, T])
        sq = s.sb(f"{tag}_sq", [P, 2, T])
        rot = s.sb(f"{tag}_rot", [P, 2, T])
        qk = s.sb(f"{tag}_qk", [P, 8, T])
        norm = s.sb(f"{tag}_norm", [16, T])
        rnorm = s.sb(f"{tag}_rnorm", [16, T])
        mx = s.sb(f"{tag}_mx", [P, 8])
        nmx = s.sb(f"{tag}_nmx", [P, 8])
        tot = s.sb(f"{tag}_tot", [P, 8])
        rtot = s.sb(f"{tag}_rtot", [P, 8])
        probs = s.sb(f"{tag}_probs", [P, 8, 2 * P])
        probs_t = s.sb(f"{tag}_probs_t", [P, 4, 2, P])
        o = s.sb(f"{tag}_o", [P, 4, T])
        std = s.sb(f"{tag}_std", [P, TT])
        rstd = s.sb(f"{tag}_rstd", [P, TT])
        hn = s.sb(f"{tag}_hn", [P, T])
        gelu = s.sb(f"{tag}_gelu", [P, HID_T, T])
        gated = s.sb(f"{tag}_gated", [P, HID_T, T])
        set_up = s.sem(f"{tag}_set_up")
        z_ready = s.sig(f"{tag}_z_ready", 1)
        shifted = s.sig(f"{tag}_shifted", 2)
        v_ready = s.sig(f"{tag}_v_ready", TT)
        v_kept = s.sig(f"{tag}_v_kept", TT)
        proj_ready = s.sig(f"{tag}_proj_ready", 8)
        squared = s.sig(f"{tag}_squared", 8)
        sq_used = s.sig(f"{tag}_sq_used", 8)
        rot1 = s.sig(f"{tag}_rot1", 8)
        rot2 = s.sig(f"{tag}_rot2", 8)
        rotated = s.sig(f"{tag}_rotated", 8)
        norm_ready = s.sig(f"{tag}_norm_ready", 1)
        clipped = s.sig(f"{tag}_clipped", 1)
        rnorm_ready = s.sig(f"{tag}_rnorm_ready", 1)
        rnorm_spread = s.sig(f"{tag}_rnorm_spread", 8)
        qk_ready = s.sig(f"{tag}_qk_ready", 8)
        scored = s.sig(f"{tag}_scored", TT)
        maxed = s.sig(f"{tag}_maxed", TT)
        negated = s.sig(f"{tag}_negated", TT)
        exped = s.sig(f"{tag}_exped", TT)
        inverted = s.sig(f"{tag}_inverted", TT)
        probs_ready = s.sig(f"{tag}_probs_ready", TT)
        turned = s.sig(f"{tag}_turned", 2 * TT)
        turned_kept = s.sig(f"{tag}_turned_kept", 2 * TT)
        pv_done = s.sig(f"{tag}_pv_done", 2 * TT)
        o_kept = s.sig(f"{tag}_o_kept", TT)
        attn_out = s.sig(f"{tag}_attn_out", 1)
        z_mid = s.sig(f"{tag}_z_mid", 1)
        shifted_mid = s.sig(f"{tag}_shifted_mid", 2)
        mean_ready = s.sig(f"{tag}_mean_ready", 1)
        centred = s.sig(f"{tag}_centred", 1)
        sq_mid = s.sig(f"{tag}_sq_mid", 1)
        var_ready = s.sig(f"{tag}_var_ready", 1)
        eps_added = s.sig(f"{tag}_eps_added", 1)
        std_ready = s.sig(f"{tag}_std_ready", 1)
        rstd_ready = s.sig(f"{tag}_rstd_ready", 1)
        rstd_spread = s.sig(f"{tag}_rstd_spread", 1)
        scaled = s.sig(f"{tag}_scaled", 1)
        hn_ready = s.sig(f"{tag}_hn_ready", 1)
        hidden = s.sig(f"{tag}_hidden", HID_T)
        gelu_ready = s.sig(f"{tag}_gelu_ready", HID_T)
        gated_ready = s.sig(f"{tag}_gated_ready", HID_T)
        ffn_out = s.sig(f"{tag}_ffn_out", 1)
        done = s.sig(f"{tag}_done", 1)
        summed = s.sig(f"{tag}_summed", 1)
        block = ctx.enter_context(nc.Block())

        def w(l, name):
            return W[f"{name}{l}"]

        def head(sl):
            return 4 * (sl // 4) + 2 * (sl % 2) + (sl // 2) % 2

        def keys(tt):
            return (slice(0, P), slice(P, 2 * P)) if tt == 0 else (slice(tt * P - 64, (tt + 1) * P), slice(64, 2 * P))

        @block.sync
        def _(sp):
            C["load"](sp, tag)

        @block.gpsimd
        def _(pool):
            pool.memset(h[64:P, 0:1], 0.0).then_inc(set_up, 1)
            pool.wait_ge(set_up, 1)
            pool.memset(probs[:, :, 0:64], 0.0).then_inc(set_up, 1)
            pool.wait_ge(set_up, 2)
            with pool.Fori(0, NB) as b:
                for l in range(2):
                    t = b * 2 + l
                    for i in range(8):
                        rot1.wait(pool, t, i + 1)
                        rot2.wait(pool, t, i + 1)
                        pool.tensor_tensor(qk[:, i, :], rot[:, 0, :], rot[:, 1, :], ALU.add).then_inc(rotated.sem, 1)

        @block.tensor
        def _(pe):
            C["weights"](pe, tag)
            with pe.Fori(0, NB) as b:
                for l in range(2):
                    t = b * 2 + l
                    shifted.wait(pe, t, 2)
                    for st in range(TT):
                        if st >= 2:
                            v_kept.wait(pe, t, st - 1)
                        pe.matmul(PS[:, 6 + st % 2, :], h[:, bass.ts(st, P)], w(l, "v"), start=True, stop=True)\
                          .then_inc(v_ready.sem, 1)
                    for i in range(8):
                        bank = 2 * (i % 2)
                        if i >= 2:
                            rot2.wait(pe, t, i - 1)
                            squared.wait(pe, t, i - 1)
                        pe.matmul(PS[:, bank, :], w(l, "qk")[:, bass.ts(i, P)], h[:, :], start=True, stop=True)
                        pe.matmul(PS[:, bank + 1, :], w(l, "qk_sw")[:, bass.ts(i, P)], h[:, :], start=True, stop=True)\
                          .then_inc(proj_ready.sem, 1)
                        if i >= 1:
                            squared.wait(pe, t, i)
                            pe.matmul(PS[0:16, 4, :], W["head_sum"][:, bass.ts(i - 1, 16)], sq[:, (i - 1) % 2, :],
                                      start=(i == 1), stop=False).then_inc(sq_used.sem, 1)
                    squared.wait(pe, t, 8)
                    pe.matmul(PS[0:16, 4, :], W["head_sum"][:, bass.ts(7, 16)], sq[:, 1, :],
                              start=False, stop=True).then_inc(sq_used.sem, 1)
                    rnorm_ready.wait(pe, t, 1)
                    v_kept.wait(pe, t, TT)
                    for i in range(8):
                        if i >= 2:
                            qk_ready.wait(pe, t, i - 1)
                        pe.matmul(PS[:, 6 + i % 2, :], W["head_bc"][:, bass.ts(i, P)], rnorm[:, :],
                                  start=True, stop=True).then_inc(rnorm_spread.sem, 1)
                    qk_ready.wait(pe, t, 8)

                    def scores(tt):
                        js, cols = keys(tt)
                        if tt >= 1:
                            exped.wait(pe, t, tt)
                        for sl in range(8):
                            hd = head(sl)
                            strip = slice(64 * (hd % 2), 64 * (hd % 2) + 64)
                            out = PS[:, sl // 2, (sl % 2) * 256:(sl % 2) * 256 + 256][:, cols]
                            pe.matmul(out, qk[strip, hd // 2, bass.ts(tt, P)], qk[strip, 4 + hd // 2, js],
                                      start=True, stop=False)
                            mm = pe.matmul(out, C["ident_bf"], W["mask"][:, cols], start=False, stop=True)
                        mm.then_inc(scored.sem, 1)

                    def turn(tt, half):
                        n = 2 * tt + half
                        probs_ready.wait(pe, t, tt + 1)
                        if n >= 1:
                            turned_kept.wait(pe, t, n)
                        for hd in range(4):
                            for kt in range(0 if tt else 1, 2):
                                at = (hd * 2 + kt) * P
                                mm = pe.transpose(PS[:, 4 + at // T, at % T:at % T + P],
                                                  probs[:, 4 * half + hd, bass.ts(kt, P)], C["ident"])
                        mm.then_inc(turned.sem, 1)

                    def pv(tt, half):
                        n = 2 * tt + half
                        turned_kept.wait(pe, t, n + 1)
                        if half == 0 and tt >= 1:
                            o_kept.wait(pe, t, tt)
                        for hd in range(4):
                            hh = head(4 * half + hd)
                            rows = slice(64 * (hh % 2), 64 * (hh % 2) + 64)
                            kts = range(0 if tt else 1, 2)
                            for kt in kts:
                                mm = pe.matmul(PS[rows, 6, bass.ts(hh // 2, P)],
                                               v[:, tt - 1 + kt, bass.ts(hh, 64)], probs_t[:, hd, kt, :],
                                               start=(kt == kts[0]), stop=(kt == 1))
                        mm.then_inc(pv_done.sem, 1)

                    scores(0)
                    for tt in range(TT):
                        for half in range(2):
                            turn(tt, half)
                            if half == 0 and tt + 1 < TT:
                                scores(tt + 1)
                            pv(tt, half)
                    o_kept.wait(pe, t, TT)
                    for i in range(4):
                        mm = pe.matmul(PS[:, 7, :], w(l, "wo")[:, bass.ts(i, P)], o[:, i, :],
                                       start=(i == 0), stop=(i == 3))
                    mm.then_inc(attn_out.sem, 1)
                    shifted_mid.wait(pe, t, 2)
                    pe.matmul(PS[:, 6, :], C["inv_d"], h[:, :], start=True, stop=True).then_inc(mean_ready.sem, 1)
                    sq_mid.wait(pe, t, 1)
                    for tt in range(TT):
                        mm = pe.matmul(PS[:, 5, tt:tt + 1], sq[:, 0, bass.ts(tt, P)], C["inv_d"][:, 0:1],
                                       start=True, stop=True)
                    mm.then_inc(var_ready.sem, 1)
                    rstd_ready.wait(pe, t, 1)
                    for tt in range(TT):
                        mm = pe.matmul(PS[:, 4, bass.ts(tt, P)], rstd[:, tt:tt + 1].to_broadcast([P, P]),
                                       C["ident"], start=True, stop=True)
                    mm.then_inc(rstd_spread.sem, 1)
                    hn_ready.wait(pe, t, 1)
                    for i in range(HID_T):
                        if i >= 2:
                            gated_ready.wait(pe, t, i - 1)
                        pe.matmul(PS[:, 2 * (i % 2), :], w(l, "w1a")[:, bass.ts(i, P)], hn[:, :], start=True, stop=True)
                        pe.matmul(PS[:, 2 * (i % 2) + 1, :], w(l, "w1g")[:, bass.ts(i, P)], hn[:, :],
                                  start=True, stop=True).then_inc(hidden.sem, 1)
                    for i in range(HID_T):
                        gated_ready.wait(pe, t, i + 1)
                        mm = pe.matmul(PS[:, 7, :], w(l, "w2")[:, bass.ts(i, P)], gated[:, i, :],
                                       start=(i == 0), stop=(i == HID_T - 1))
                    mm.then_inc(ffn_out.sem, 1)

        @block.scalar
        def _(act):
            C["weights"](act, tag)
            with act.Fori(0, NB) as b:
                for l in range(2):
                    t = b * 2 + l
                    for st in range(TT):
                        v_ready.wait(act, t, st + 1)
                        act.activation(v[:, st, :], PS[:, 6 + st % 2, :], ACT.Copy).then_inc(v_kept.sem, 1)
                    for i in range(8):
                        proj_ready.wait(act, t, i + 1)
                        if i >= 2:
                            sq_used.wait(act, t, i - 1)
                        act.activation(sq[:, i % 2, :], PS[:, 2 * (i % 2), :], ACT.Square).then_inc(squared.sem, 1)
                    sq_used.wait(act, t, 8)
                    act.activation(norm[:, :], PS[0:16, 4, :], ACT.Sqrt).then_inc(norm_ready.sem, 1)
                    for tt in range(TT):
                        js, cols = keys(tt)
                        negated.wait(act, t, tt + 1)
                        scored.wait(act, t, tt + 1)
                        if tt >= 1:
                            turned.wait(act, t, 2 * tt)
                        for hd in range(8):
                            src = PS[:, hd // 2, (hd % 2) * 256:(hd % 2) * 256 + 256][:, cols]
                            a = act.activation(probs[:, hd, cols], src, ACT.Exp, bias=nmx[:, hd:hd + 1], scale=8.0,
                                               accum_out=tot[:, hd:hd + 1])
                        a.then_inc(exped.sem, 1)
                        for half in range(2):
                            n = 2 * tt + half
                            turned.wait(act, t, n + 1)
                            if n >= 1:
                                pv_done.wait(act, t, n)
                            lo = 0 if tt else 1
                            act.activation(probs_t[:, :, lo:2, :],
                                           PS[:, 4:6, :].rearrange("p a (h k i) -> p (a h) k i", k=2, i=P)[:, :, lo:2, :],
                                           ACT.Copy).then_inc(turned_kept.sem, 1)
                        pv_done.wait(act, t, 2 * tt + 2)
                        act.activation(o[:, :, bass.ts(tt, P)], PS[:, 6, :].rearrange("p (i q) -> p i q", i=4),
                                       ACT.Copy).then_inc(o_kept.sem, 1)
                    centred.wait(act, t, 1)
                    act.activation(sq[:, 0, :], hn[:, :], ACT.Square).then_inc(sq_mid.sem, 1)
                    eps_added.wait(act, t, 1)
                    act.activation(std[:, :], std[:, :], ACT.Sqrt).then_inc(std_ready.sem, 1)
                    for i in range(HID_T):
                        hidden.wait(act, t, i + 1)
                        act.activation(gelu[:, i, :], PS[:, 2 * (i % 2) + 1, :], ACT.Gelu,
                                       bias=w(l, "b1g")[:, i:i + 1]).then_inc(gelu_ready.sem, 1)

        @block.vector
        def _(dve):
            C["weights"](dve, tag)
            dve.wait_ge(set_up, 2)
            cos, sin = W["cos"], W["sin"]

            def shift(t, sig):
                dve.tensor_copy(h[0:64, :], z[0:64, :]).then_inc(sig.sem, 1)
                dve.tensor_copy(h[64:P, 1:T], z[64:P, 0:T - 1]).then_inc(sig.sem, 1)

            with dve.Fori(0, NB) as b:
                for l in range(2):
                    t = b * 2 + l
                    if l == 0:
                        summed.wait(dve, b, 0)
                        dve.tensor_copy(z[:, :], X[:, b, :]).then_inc(z_ready.sem, 2)
                        z_ready.wait(dve, b * 2, 2)
                    else:
                        done.wait(dve, t, 0)
                    shift(t, shifted)
                    for i in range(8):
                        proj_ready.wait(dve, t, i + 1)
                        squared.wait(dve, t, i + 1)
                        if i >= 1:
                            rotated.wait(dve, t, i)
                        qs = w(l, "q_scale") if i < 4 else w(l, "k_scale")
                        tab = slice(0, T) if i < 4 else slice(T, 2 * T)
                        bank = 2 * (i % 2)
                        dve.scalar_tensor_tensor(rot[:, 0, :], PS[:, bank, :], qs[:, 0:1], cos[:, tab],
                                                 ALU.mult, ALU.mult).then_inc(rot1.sem, 1)
                        dve.scalar_tensor_tensor(rot[:, 1, :], PS[:, bank + 1, :], qs[:, 1:2], sin[:, tab],
                                                 ALU.mult, ALU.mult).then_inc(rot2.sem, 1)
                    norm_ready.wait(dve, t, 1)
                    dve.tensor_scalar(norm[:, :], norm[:, :], 1e-12, None, ALU.max).then_inc(clipped.sem, 1)
                    clipped.wait(dve, t, 1)
                    dve.reciprocal(rnorm[:, :], norm[:, :]).then_inc(rnorm_ready.sem, 1)
                    rotated.wait(dve, t, 8)
                    for i in range(8):
                        rnorm_spread.wait(dve, t, i + 1)
                        dve.tensor_tensor(qk[:, i, :], qk[:, i, :], PS[:, 6 + i % 2, :], ALU.mult)\
                           .then_inc(qk_ready.sem, 1)
                    for tt in range(TT):
                        js, cols = keys(tt)
                        scored.wait(dve, t, tt + 1)
                        src = PS[:, 0:4, :].rearrange("p a (h j) -> p (a h) j", j=256)[:, :, cols]
                        dve.tensor_reduce(mx[:, :], src, AX, ALU.max).then_inc(maxed.sem, 1)
                        maxed.wait(dve, t, tt + 1)
                        if tt >= 1:
                            exped.wait(dve, t, tt)
                        dve.tensor_scalar(nmx[:, :], mx[:, :], -8.0, None, ALU.mult).then_inc(negated.sem, 1)
                        exped.wait(dve, t, tt + 1)
                        dve.reciprocal(rtot[:, :], tot[:, :]).then_inc(inverted.sem, 1)
                        inverted.wait(dve, t, tt + 1)
                        n = cols.stop - cols.start
                        dve.tensor_tensor(probs[:, :, cols], probs[:, :, cols],
                                          rtot[:, :].rearrange("p (h o) -> p h o", o=1)
                                          .to_broadcast([P, 8, n]), ALU.mult).then_inc(probs_ready.sem, 1)
                    attn_out.wait(dve, t, 1)
                    dve.tensor_tensor(z[:, :], z[:, :], PS[:, 7, :], ALU.add).then_inc(z_mid.sem, 1)
                    z_mid.wait(dve, t, 1)
                    shift(t, shifted_mid)
                    mean_ready.wait(dve, t, 1)
                    shifted_mid.wait(dve, t, 2)
                    dve.tensor_tensor(hn[:, :], h[:, :], PS[:, 6, :], ALU.subtract).then_inc(centred.sem, 1)
                    var_ready.wait(dve, t, 1)
                    dve.tensor_scalar(std[:, :], PS[:, 5, 0:TT], 1e-5, None, ALU.add).then_inc(eps_added.sem, 1)
                    std_ready.wait(dve, t, 1)
                    dve.reciprocal(rstd[:, :], std[:, :]).then_inc(rstd_ready.sem, 1)
                    rstd_spread.wait(dve, t, 1)
                    sq_mid.wait(dve, t, 1)
                    dve.scalar_tensor_tensor(hn[:, :], hn[:, :], w(l, "ln_g"), PS[:, 4, :], ALU.mult, ALU.mult)\
                       .then_inc(scaled.sem, 1)
                    scaled.wait(dve, t, 1)
                    dve.tensor_scalar(hn[:, :], hn[:, :], w(l, "ln_b"), None, ALU.add).then_inc(hn_ready.sem, 1)
                    for i in range(HID_T):
                        gelu_ready.wait(dve, t, i + 1)
                        dve.scalar_tensor_tensor(gated[:, i, :], PS[:, 2 * (i % 2), :], w(l, "b1a")[:, i:i + 1],
                                                 gelu[:, i, :], ALU.add, ALU.mult).then_inc(gated_ready.sem, 1)
                    ffn_out.wait(dve, t, 1)
                    dve.scalar_tensor_tensor(z[:, :], PS[:, 7, :], w(l, "b2"), z[:, :], ALU.add, ALU.add)\
                       .then_inc(done.sem, 1)
                    if l == 1:
                        done.wait(dve, t, 1)
                        dve.tensor_tensor(Y[:, b, :], X[:, b, :], z[:, :], ALU.add).then_inc(summed.sem, 1)




class Pack:

    def __init__(self):
        self.items, self.cols = [], 0

    def add(self, name, array):
        self.items.append((name, array, self.cols))
        self.cols += array.shape[1]

    def data(self, dtype):
        out = np.zeros((P, self.cols), dtype)
        for _, a, at in self.items:
            out[:a.shape[0], at:at + a.shape[1]] = a
        return out


def moe_sel(sizes, dtype):
    units = np.concatenate([np.full(n, e) for e, n in enumerate(sizes)])
    nt = -(-len(units) // P)
    sel = np.zeros((96, nt * P), dtype)
    for part in range(3):
        sel[32 * part + units, np.arange(len(units))] = 1
    return sel


def tiles_of(w, nt):
    out = np.zeros((nt * P, w.shape[1]), w.dtype)
    out[:w.shape[0]] = w
    return out.reshape(nt, P, w.shape[1]).transpose(1, 0, 2).reshape(P, -1)


def padded(w, cols):
    out = np.zeros((w.shape[0], cols), w.dtype)
    out[:, :w.shape[1]] = w
    return out


def lay_out(a, bf):
    fs, bs = {}, {}

    def stage(name):
        fs[name], bs[name] = Pack(), Pack()
        return fs[name], bs[name]

    f, h = stage("const")
    f.add("inv_d", np.full((P, P), 1.0 / P, np.float32))
    f.add("ident", np.eye(P, dtype=np.float32))
    h.add("ident_bf", np.eye(P).astype(bf))

    f, h = stage("m0")
    E, D, F = a["L0_ffn_Wg"].shape
    nt = (E * F + 128) // P
    f.add("router", a["L0_ffn_Wr"])
    f.add("bias", np.tile(a["L0_ffn_expert_bias"], (P, 1)))
    f.add("gate", np.concatenate([a["L0_ffn_Wg"].transpose(1, 0, 2).reshape(D, -1), a["L0_ffn_Sg"]], 1))
    f.add("up", np.concatenate([a["L0_ffn_Wu"].transpose(1, 0, 2).reshape(D, -1), a["L0_ffn_Su"]], 1))
    f.add("down", tiles_of(np.concatenate([a["L0_ffn_Wd"].reshape(-1, D), a["L0_ffn_Sd"]], 0), nt))
    h.add("sel", moe_sel([F] * E + [128], bf))

    f, h = stage("m1")
    gu = a["L1_ffn_experts_gate_up"]
    E, I = gu.shape[0], gu.shape[1] // 2
    SI = a["L1_ffn_shared_gate_w"].shape[0]
    nt = -(-(E * I + SI) // P)
    f.add("router", np.concatenate([a["L1_ffn_gate_w"], a["L1_ffn_shared_expert_gate_w"]], 0).T)
    f.add("gate", padded(np.concatenate([gu[:, :I].reshape(-1, P), a["L1_ffn_shared_gate_w"]], 0).T, nt * P))
    f.add("up", padded(np.concatenate([gu[:, I:].reshape(-1, P), a["L1_ffn_shared_up_w"]], 0).T, nt * P))
    f.add("down", tiles_of(np.concatenate([a["L1_ffn_experts_down"].transpose(0, 2, 1).reshape(-1, P),
                                           a["L1_ffn_shared_down_w"].T], 0), nt))
    h.add("sel", moe_sel([I] * E + [SI], bf))

    f, h = stage("m2")
    E, D, I = a["L2_ffn_w1"].shape
    nt = E * I // P
    f.add("router", a["L2_ffn_gate_w"].T)
    f.add("bias", np.tile(a["L2_ffn_e_bias"], (P, 1)))
    f.add("gate", a["L2_ffn_w1"].transpose(1, 0, 2).reshape(D, -1))
    f.add("up", a["L2_ffn_w3"].transpose(1, 0, 2).reshape(D, -1))
    f.add("down", tiles_of(a["L2_ffn_w2"].reshape(-1, D), nt))
    h.add("sel", moe_sel([I] * E, bf))
    more_layout(a, bf, stage)
    return fs, bs


def strips(heads, D, SW, bf):
    out = np.zeros((P, 2, 3, len(heads), P), bf)
    for g, hs in enumerate(heads):
        for j, h in enumerate(hs):
            for term, parts in enumerate(TERMS):
                for e in range(D):
                    for n in range(2):
                        out[h * D + e, n, parts[n], g, j * SW + term * D + e] = 1
    return out.reshape(P, -1)


def attn_common(f, h, D, SW, heads, bf):
    ones = np.zeros((P, 1), np.float32)
    for j in range(P // SW):
        ones[j * SW + 6 * D:j * SW + 6 * D + 3] = 1
    f.add("ones_rows", ones)
    h.add("strips", strips(heads, D, SW, bf))
    pick_o, pick_sum = np.zeros((P, 32), np.float32), np.zeros((P, 32), np.float32)
    for j in range(4):
        for e in range(8):
            pick_o[32 * j + e, 8 * j + e] = 1
            pick_sum[32 * j + 8, 8 * j + e] = 1
    f.add("pick_o", pick_o)
    f.add("pick_sum", pick_sum)


def more_layout(a, bf, stage):
    f, h = stage("a1")
    w = a["L1_attn_w_qkv"]
    f.add("q", w[:, :P])
    f.add("k", w[:, P:2 * P])
    f.add("v", w[:, 2 * P:])
    f.add("out", a["L1_attn_w_out"])
    f.add("b_out", a["L1_attn_b_out"][:, None])
    attn_common(f, h, 8, 64, [[2 * g, 2 * g + 1] for g in range(8)], bf)
    mask = np.where(np.arange(P)[None, :] > np.arange(P)[:, None], -1e10, 0.0)
    h.add("mask", mask.astype(bf))
    h.add("mask_t", np.ascontiguousarray(mask.T).astype(bf))

    f, h = stage("a3")
    f.add("q", a["L3_attn_Wq"])
    f.add("k", a["L3_attn_Wk"])
    swap = np.arange(P) ^ 1
    f.add("q_sw", a["L3_attn_Wq"][:, swap])
    f.add("k_sw", a["L3_attn_Wk"][:, swap])
    f.add("v", a["L3_attn_Wv"])
    f.add("out", a["L3_attn_Wo"])
    attn_common(f, h, 4, 32, [[2 * (4 * (g % 4) + j) + g // 4 for j in range(4)] for g in range(8)], bf)
    pos = np.arange(T, dtype=np.float32)[:, None]
    freq = np.float32(1.0) / np.float32(0.0001) ** (np.float32(2.0) * np.arange(2, dtype=np.float32) / np.float32(4))
    ang = (pos * freq.astype(np.float32)).astype(np.float32)
    pair = (np.arange(P) % 4) // 2
    cos = np.cos(ang).astype(np.float32).T[pair]
    sin = np.sin(ang).astype(np.float32).T[pair] * np.where(np.arange(P) % 2 == 0, -1, 1)[:, None]
    f.add("cos", np.concatenate([cos * 0.5, cos], 1).astype(np.float32))
    f.add("sin", np.concatenate([sin * 0.5, sin], 1).astype(np.float32))
    f.add("lam_q", np.tile(np.concatenate([a["L3_attn_lambda_q1"], a["L3_attn_lambda_q2"]]), (P, 1)))
    f.add("lam_k", np.tile(np.concatenate([a["L3_attn_lambda_k1"], a["L3_attn_lambda_k2"]]), (P, 1)))
    f.add("subln", np.tile(a["L3_attn_subln_g"], 16)[:, None])
    f.add("eps", np.full((P, 1), 1e-5, np.float32))
    mean8 = np.kron(np.eye(16, dtype=np.float32), np.full((8, 8), 1 / 8, np.float32))
    f.add("mean8", mean8)
    rest_layout(a, bf, stage)


def rest_layout(a, bf, stage):
    f, h = stage("a2")
    for name, w in (("q", "W_q"), ("k", "W_k"), ("v", "W_v")):
        f.add(name, a[f"L2_attn_{w}"].T)
    f.add("ones", np.ones((P, 1), np.float32))

    f, h = stage("f3")
    wqkv = a["L3_ffn_wqkv"]
    swap = np.arange(512) // 64 * 64 + (np.arange(512) % 64 + 32) % 64
    swap64 = (np.arange(64) + 32) % 64
    for l in range(2):
        q, k, v = wqkv[l][:, :512], wqkv[l][:, 512:1024], wqkv[l][:, 1024:]
        f.add(f"qk{l}", np.concatenate([q, k], 1))
        f.add(f"qk_sw{l}", np.concatenate([q[:, swap], k[:, swap]], 1))
        f.add(f"v{l}", v)
        for name, key in (("q_scale", "L3_ffn_q_scale"), ("k_scale", "L3_ffn_k_scale")):
            sc = a[key][l]
            f.add(f"{name}{l}", np.stack([np.tile(sc, 2), np.tile(sc[swap64], 2)], 1))
        f.add(f"wo{l}", tiles_of(a["L3_ffn_wo"][l], 4))
        f.add(f"ln_g{l}", a["L3_ffn_ln_g"][l][:, None])
        f.add(f"ln_b{l}", a["L3_ffn_ln_b"][l][:, None])
        hid = a["L3_ffn_w2"].shape[1]
        w1, b1 = a["L3_ffn_w1"][l], a["L3_ffn_b1"][l][None]
        f.add(f"w1a{l}", padded(w1[:, :hid], 3 * P))
        f.add(f"w1g{l}", padded(w1[:, hid:], 3 * P))
        f.add(f"b1a{l}", padded(b1[:, :hid], 3 * P).reshape(3, P).T)
        f.add(f"b1g{l}", padded(b1[:, hid:], 3 * P).reshape(3, P).T)
        f.add(f"w2{l}", tiles_of(a["L3_ffn_w2"][l], 3))
        f.add(f"b2{l}", a["L3_ffn_b2"][l][:, None])
    head_sum, head_bc = np.zeros((P, 8, 16), np.float32), np.zeros((16, 8, P), np.float32)
    for i in range(8):
        for c in range(P):
            head_sum[c, i, 2 * i + c // 64] = 1
            head_bc[2 * i + c // 64, i, c] = 1
    f.add("head_sum", head_sum.reshape(P, -1))
    f.add("head_bc", head_bc.reshape(16, -1))
    half = np.arange(0, 64, 2, dtype=np.float32)
    inv = (np.float32(1.0) / np.float32(10000.0) ** (half / np.float32(64))).astype(np.float32)
    t = np.arange(T, dtype=np.float32)
    fr = (t[:, None] * inv[None]).astype(np.float32)
    base = ((half + np.float32(0.4 * 64)) / np.float32(1.4 * 64)).astype(np.float32)
    power = ((t - T // 2) / np.float32(32)).astype(np.float32)
    sc = (base[None] ** power[:, None]).astype(np.float32)
    row = np.arange(P) % 32
    sign = np.where(np.arange(P) % 64 < 32, -1, 1)[:, None].astype(np.float32)
    cos, sin, sc = np.cos(fr).T[row], np.sin(fr).T[row] * sign, sc.T[row]
    f.add("cos", np.concatenate([cos * sc, cos / sc], 1).astype(np.float32))
    f.add("sin", np.concatenate([sin * sc, sin / sc], 1).astype(np.float32))
    j = np.arange(2 * P)[None, :] - P
    i = np.arange(P)[:, None]
    h.add("mask", np.where((i < j) | (i > j + 64), -BIG, 0.0).astype(bf))
    first_layout(a, bf, stage)


def first_layout(a, bf, stage):
    f, h = stage("a0")
    f.add("disp", a["L0_attn_W_disp"])
    f.add("val", a["L0_attn_W_val"])

    def blocks(w):
        out = np.zeros((8, 16, 8, 16), np.float32)
        for i in range(8):
            out[i, :, i, :] = w
        return out.reshape(P, P)

    f.add("strain", blocks(a["L0_attn_W_strain"]))
    f.add("dmg", blocks(a["L0_attn_W_dmg"]))
    f.add("w_pos", np.tile(a["L0_attn_W_pos"], (1, 8)))
    f.add("rel", a["L0_attn_rel_pos_emb"].T)
    f.add("b_dmg", np.tile(a["L0_attn_b_dmg"], 8)[:, None])
    f.add("b_out", np.tile(a["L0_attn_b_dmg_out"], P)[:, None])
    for name, key in (("w_bond", "L0_attn_W_bond"), ("w_dmg_out", "L0_attn_W_dmg_out")):
        out = np.zeros((8, 16, 4, 4, 8), np.float32)
        for k in range(4):
            for i in range(8):
                out[i, :, k, k, i] = a[key][:, 0]
        f.add(name, out.reshape(P, P))
    f.add("c_proj", a["L0_attn_W_cproj"])
    d = (np.arange(T) // 8)[None, :]
    m = np.where(np.arange(P)[:, None] - 63 + d < 0, -BIG, 0.0).astype(np.float32)
    f.add("mask", np.concatenate([m, m], 1))


def build(nc, x_d, out_d, f_d, b_d, fs, bs, stages):
    Stage.CLEARED = []
    with ExitStack() as top:
        X = top.enter_context(nc.sbuf_tensor("X", [P, NB, T], F32))
        Y = top.enter_context(nc.sbuf_tensor("Y", [P, NB, T], F32))
        PS = top.enter_context(nc.psum_tensor("PS", [P, NB, T], F32))
        x_loaded = top.enter_context(nc.semaphore("x_loaded"))
        stored = top.enter_context(nc.semaphore("stored"))

        def load(eng, name):
            wf, wb, sem, _ = bufs[name]
            eng.dma_start(wf[:, :], f_d[name]).then_inc(sem, 16)
            if name in b_d:
                eng.dma_start(wb[:, :], b_d[name]).then_inc(sem, 16)

        def weights(eng, name):
            eng.wait_ge(bufs[name][2], 32 if name in b_d else 16)

        def hold(ctx, name):
            wf = ctx.enter_context(nc.sbuf_tensor(f"w_{name}", [P, fs[name].cols], F32))
            wb = ctx.enter_context(nc.sbuf_tensor(f"wb_{name}", [P, max(bs[name].cols, 1)], BF16))
            sem = top.enter_context(nc.semaphore(f"{name}_weights"))
            views = {k: wf[0:v.shape[0], at:at + v.shape[1]] for k, v, at in fs[name].items}
            views |= {k: wb[0:v.shape[0], at:at + v.shape[1]] for k, v, at in bs[name].items}
            bufs[name] = (wf, wb, sem, views)
            return views

        scratch = nc.dram_tensor("scratch", (TT * 16 * 2 * 64 * P,), F32, kind="Internal").ap()
        first, last = stages
        bufs = {}
        C = dict(hold(top, "const"), weights=weights, load=load)

        with ExitStack() as ctx:
            block = ctx.enter_context(nc.Block())

            @block.sync
            def _(sp):
                sp.dma_start(X[:, :, :], x_d.rearrange("p (b t) -> p b t", b=NB)).then_inc(x_loaded, 16)
                load(sp, "const")
                sp.wait_ge(x_loaded, 16)
                weights(sp, "const")

        stage_of = [
            ("a0", lambda w: attn0(nc, "a0", X, Y, PS, C, w, scratch)),
            ("m0", lambda w: moe(nc, "m0", X, Y, PS, C, w, "top_softmax", 8, 2, 5)),
            ("a1", lambda w: attn(nc, "a1", X, Y, PS, C, w, True)),
            ("m1", lambda w: moe(nc, "m1", X, Y, PS, C, w, "softmax_top", 8, 2, 14)),
            ("a2", lambda w: attn2(nc, "a2", X, Y, PS, C, w)),
            ("m2", lambda w: moe(nc, "m2", X, Y, PS, C, w, "sigmoid_top", 32, 4, 24)),
            ("a3", lambda w: attn(nc, "a3", X, Y, PS, C, w, False)),
            ("f3", lambda w: local_ffn(nc, "f3", X, Y, PS, C, w)),
        ]
        for n, (name, emit) in enumerate(stage_of):
            if first <= n <= last:
                with ExitStack() as ctx:
                    emit(hold(ctx, name))
                layernorm(nc, f"ln{n}", X, Y, PS, C)
        with ExitStack() as ctx:
            block = ctx.enter_context(nc.Block())

            @block.sync
            def _(sp):
                sp.dma_start(out_d.rearrange("p (b t) -> p b t", b=NB), X[:, :, :]).then_inc(stored, 16)
                sp.wait_ge(stored, 16)


def kernel(**inputs):
    import ml_dtypes
    import concourse.bacc as bacc
    from concourse.bass_utils import run_bass_kernel_spmd

    bf = ml_dtypes.bfloat16
    a = {k: np.asarray(v) for k, v in inputs.items()}
    x = np.ascontiguousarray(a["L0_attn_x"].reshape(NB * T, P).T)
    fs, bs = lay_out(a, bf)
    nc = bacc.Bacc("TRN2", target_bir_lowering=False, num_devices=1)
    arrays = {"x_dram": x}
    f_d, b_d = {}, {}
    x_d = nc.dram_tensor("x_dram", x.shape, F32, kind="ExternalInput").ap()
    for name in fs:
        arrays[f"{name}_f_dram"] = fs[name].data(np.float32)
        f_d[name] = nc.dram_tensor(f"{name}_f_dram", (P, fs[name].cols), F32, kind="ExternalInput").ap()
        if bs[name].cols:
            arrays[f"{name}_b_dram"] = bs[name].data(bf)
            b_d[name] = nc.dram_tensor(f"{name}_b_dram", (P, bs[name].cols), BF16, kind="ExternalInput").ap()
    out_d = nc.dram_tensor("out_dram", (P, NB * T), F32, kind="ExternalOutput").ap()
    build(nc, x_d, out_d, f_d, b_d, fs, bs, STAGES)
    r = run_bass_kernel_spmd(nc, [arrays], core_ids=[0])
    return np.ascontiguousarray(r.results[0]["out_dram"].T).reshape(NB, T, P)
```

```python
import math
from contextlib import ExitStack

import numpy as np

import concourse.bass as bass
from concourse import mybir

F32 = mybir.dt.float32
BF16 = mybir.dt.bfloat16
ALU = mybir.AluOpType
ACT = mybir.ActivationFunctionType
AX = mybir.AxisListType.X

P = 128
NB = 8
T = 512
TT = T // P
NTOK = NB * T // P
BIG = 1e30
LAMBDA_INIT = 0.8 - 0.6 * math.exp(-0.3 * 12)

STAGES = (0, 7)


class Signals:

    def __init__(self, sem, per):
        self.sem, self.per = sem, per

    def at(self, turn, n):
        return turn * self.per + n


class Stage:

    def __init__(self, nc, ctx):
        self.nc, self.ctx, self.sems = nc, ctx, []
        ctx.callback(self.clear)

    CLEARED = []

    def clear(self):
        for sem in Stage.CLEARED:
            self.nc.release_semaphore(sem)
        Stage.CLEARED = list(self.sems)
        for sem in self.sems:
            self.nc.gpsimd.sem_clear(sem)

    def sb(self, name, shape, dt=F32):
        return self.ctx.enter_context(self.nc.sbuf_tensor(name, shape, dt))

    def sem(self, name):
        self.sems.append(self.nc.alloc_semaphore(name))
        return self.sems[-1]

    def sig(self, name, per):
        return Signals(self.sem(name), per)


def layernorm(nc, tag, X, Y, PS, C):
    with ExitStack() as ctx:
        s = Stage(nc, ctx)
        std = s.sb(f"{tag}_std", [P, NTOK])
        rstd = s.sb(f"{tag}_rstd", [P, NTOK])
        mean_ready = s.sem(f"{tag}_mean_ready")
        centred = s.sem(f"{tag}_centred")
        squared = s.sem(f"{tag}_squared")
        var_ready = s.sem(f"{tag}_var_ready")
        eps_added = s.sem(f"{tag}_eps_added")
        std_ready = s.sem(f"{tag}_std_ready")
        rstd_ready = s.sem(f"{tag}_rstd_ready")
        spread = s.sem(f"{tag}_spread")
        block = ctx.enter_context(nc.Block())

        @block.tensor
        def _(pe):
            with pe.Fori(0, NB) as b:
                pe.matmul(PS[:, b, :], C["inv_d"], Y[:, b, :], start=True, stop=True).then_inc(mean_ready, 1)
            for n in range(NTOK):
                if n % TT == 0:
                    pe.wait_ge(squared, n // TT + 1)
                mm = pe.matmul(PS[:, 0, n:n + 1], X[:, n // TT, bass.ts(n % TT, P)], C["inv_d"][:, 0:1],
                               start=True, stop=True)
            mm.then_inc(var_ready, 1)
            pe.wait_ge(rstd_ready, 1)
            for n in range(NTOK):
                mm = pe.matmul(PS[:, n // TT, bass.ts(n % TT, P)], rstd[:, n:n + 1].to_broadcast([P, P]),
                               C["ident"], start=True, stop=True)
                if n % TT == TT - 1:
                    mm.then_inc(spread, 1)

        @block.vector
        def _(dve):
            with dve.Fori(0, NB) as b:
                dve.wait_ge(mean_ready, b + 1)
                dve.tensor_tensor(Y[:, b, :], Y[:, b, :], PS[:, b, :], ALU.subtract).then_inc(centred, 1)
            dve.wait_ge(var_ready, 1)
            dve.tensor_scalar(std[:, :], PS[:, 0, 0:NTOK], 1e-5, None, ALU.add).then_inc(eps_added, 1)
            dve.wait_ge(std_ready, 1)
            dve.reciprocal(rstd[:, :], std[:, :]).then_inc(rstd_ready, 1)
            with dve.Fori(0, NB) as b:
                dve.wait_ge(spread, b + 1)
                dve.tensor_tensor(X[:, b, :], Y[:, b, :], PS[:, b, :], ALU.mult)

        @block.scalar
        def _(act):
            with act.Fori(0, NB) as b:
                act.wait_ge(centred, b + 1)
                act.activation(X[:, b, :], Y[:, b, :], ACT.Square).then_inc(squared, 1)
            act.wait_ge(eps_added, 1)
            act.activation(std[:, :], std[:, :], ACT.Sqrt).then_inc(std_ready, 1)


def moe(nc, tag, X, Y, PS, C, W, kind, E, K, NT):
    EW = E + (1 if kind in ("top_softmax", "softmax_top") else 0)
    NV = E + 8 - K
    NR = W["router"].shape[1]
    SENT, PICKED = -3e38, 3e38
    with ExitStack() as ctx:
        s = Stage(nc, ctx)
        vals = s.sb(f"{tag}_vals", [P, NTOK, NV])
        top = s.sb(f"{tag}_top", [P, NTOK, 8])
        marked = s.sb(f"{tag}_marked", [P, NTOK, NV])
        score = s.sb(f"{tag}_score", [P, NTOK, NR])
        wt = s.sb(f"{tag}_wt", [P, NTOK, EW])
        tot = s.sb(f"{tag}_tot", [P, NTOK])
        rtot = s.sb(f"{tag}_rtot", [P, NTOK])
        parts = s.sb(f"{tag}_parts", [P, NTOK, 96], BF16)
        partsT = s.sb(f"{tag}_partsT", [96, NB, T], BF16)
        silu = s.sb(f"{tag}_silu", [P, 3, T])
        prod = s.sb(f"{tag}_prod", [P, T])
        hid = s.sb(f"{tag}_hid", [P, 3, T])
        logits_ready = s.sem(f"{tag}_logits_ready")
        step = s.sem(f"{tag}_router_step")
        exp_in = s.sem(f"{tag}_exp_in")
        exp_out = s.sem(f"{tag}_exp_out")
        cleared = s.sem(f"{tag}_cleared")
        parts_ready = s.sem(f"{tag}_parts_ready")
        turned = s.sem(f"{tag}_turned")
        turned_kept = s.sem(f"{tag}_turned_kept")
        gate_ready = s.sig(f"{tag}_gate_ready", NT)
        up_ready = s.sig(f"{tag}_up_ready", NT)
        silu_ready = s.sig(f"{tag}_silu_ready", NT)
        prod_ready = s.sig(f"{tag}_prod_ready", NT)
        hid_ready = s.sig(f"{tag}_hid_ready", NT)
        hid_used = s.sig(f"{tag}_hid_used", NT)
        out_kept = s.sig(f"{tag}_out_kept", 1)
        block = ctx.enter_context(nc.Block())
        LOG = PS[:, 0:2, :].rearrange("p a b -> p (a b)")[:, 0:NTOK * 32].rearrange("p (n e) -> p n e", e=32)

        @block.sync
        def _(sp):
            C["load"](sp, tag)

        @block.gpsimd
        def _(pool):
            pool.memset(parts[:, :, :], 0.0).then_inc(cleared, 1)
            pool.memset(vals[:, :, E:NV], SENT).then_inc(cleared, 1)

        @block.tensor
        def _(pe):
            C["weights"](pe, tag)
            for n in range(NTOK):
                mm = pe.matmul(LOG[:, n, 0:NR], X[:, n // TT, bass.ts(n % TT, P)], W["router"],
                               start=True, stop=True)
            mm.then_inc(logits_ready, 1)
            pe.wait_ge(parts_ready, 1)
            for b in range(NB):
                TP = PS[:, b, 0:T // 2].bitcast(BF16)
                for t in range(TT):
                    mm = pe.transpose(TP[0:96, bass.ts(t, P)], parts[:, b * TT + t, :], C["ident_bf"])
                mm.then_inc(turned, 1)
            pe.wait_ge(turned_kept, NB)

            def down(b, f):
                pe.wait_ge(hid_ready.sem, hid_ready.at(b, f + 1))
                if f == 0:
                    pe.wait_ge(out_kept.sem, out_kept.at(b, 0))
                pe.matmul(PS[:, 6, :], W["down"][:, bass.ts(f, P)], hid[:, f % 3, :],
                          start=(f == 0), stop=(f == NT - 1)).then_inc(hid_used.sem, 1)

            with pe.Fori(0, NB) as b:
                for f in range(NT):
                    if f >= 2:
                        pe.wait_ge(silu_ready.sem, silu_ready.at(b, f - 1))
                        pe.wait_ge(hid_ready.sem, hid_ready.at(b, f - 1))
                    else:
                        pe.wait_ge(hid_ready.sem, hid_ready.at(b, 0))
                    pe.matmul(PS[:, f % 2, :], W["gate"][:, bass.ts(f, P)], X[:, b, :],
                              start=True, stop=True).then_inc(gate_ready.sem, 1)
                    pe.matmul(PS[:, 2 + f % 2, :], W["up"][:, bass.ts(f, P)], X[:, b, :], start=True, stop=True)
                    pe.matmul(PS[:, 4 + f % 2, :], W["sel"][:, bass.ts(f, P)], partsT[:, b, :],
                              start=True, stop=True).then_inc(up_ready.sem, 1)
                    if f >= 2:
                        down(b, f - 2)
                down(b, NT - 2)
                down(b, NT - 1)

        @block.scalar
        def _(act):
            if kind == "top_softmax":
                act.wait_ge(exp_in, 1)
                act.activation(score[:, :, :], score[:, :, :], ACT.Exp).then_inc(exp_out, 1)
            elif kind == "softmax_top":
                act.wait_ge(exp_in, 1)
                act.activation(score[:, :, :], score[:, :, :], ACT.Exp).then_inc(exp_out, 1)
            else:
                act.wait_ge(logits_ready, 1)
                act.activation(score[:, 0:NTOK // 2, :], LOG[:, 0:NTOK // 2, 0:NR], ACT.Sigmoid)
                act.activation(score[:, NTOK // 2:, :], LOG[:, NTOK // 2:, 0:NR], ACT.Sigmoid).then_inc(exp_out, 1)
            with act.Fori(0, NB) as b:
                for f in range(NT):
                    act.wait_ge(gate_ready.sem, gate_ready.at(b, f + 1))
                    if f >= 3:
                        act.wait_ge(prod_ready.sem, prod_ready.at(b, f - 2))
                    else:
                        act.wait_ge(prod_ready.sem, prod_ready.at(b, 0))
                    act.activation(silu[:, f % 3, :], PS[:, f % 2, :], ACT.Silu).then_inc(silu_ready.sem, 1)

        @block.vector
        def _(dve):
            chain = [0]

            def then(ins):
                chain[0] += 1
                ins.then_inc(step, 1)
                dve.wait_ge(step, chain[0])

            def over(a, n):
                return a.rearrange("p (n o) -> p n o", o=1).to_broadcast([P, NTOK, n])

            C["weights"](dve, tag)
            dve.wait_ge(logits_ready, 1)
            if kind == "top_softmax":
                bias = W["bias"].rearrange("p (o e) -> p o e", o=1).to_broadcast([P, NTOK, E])
                dve.wait_ge(cleared, 2)
                then(dve.tensor_tensor(vals[:, :, 0:E], LOG[:, :, 0:E], bias, ALU.add))
                pick_from = vals
            elif kind == "softmax_top":
                then(dve.tensor_reduce(tot[:, :], LOG[:, :, 0:E], AX, ALU.max))
                then(dve.tensor_tensor(score[:, :, 0:E], LOG[:, :, 0:E], over(tot[:, :], E), ALU.subtract))
                dve.tensor_scalar(score[:, :, E:E + 1], LOG[:, :, E:E + 1], -1.0, None, ALU.mult).then_inc(exp_in, 1)
                dve.wait_ge(exp_out, 1)
                then(dve.tensor_reduce(tot[:, :], score[:, :, 0:E], AX, ALU.add))
                then(dve.reciprocal(rtot[:, :], tot[:, :]))
                dve.wait_ge(cleared, 2)
                then(dve.tensor_tensor(vals[:, :, 0:E], score[:, :, 0:E], over(rtot[:, :], E), ALU.mult))
            else:
                bias = W["bias"].rearrange("p (o e) -> p o e", o=1).to_broadcast([P, NTOK, E])
                dve.wait_ge(exp_out, 1)
                dve.wait_ge(cleared, 2)
                then(dve.tensor_tensor(vals[:, :, 0:E], score[:, :, 0:E], bias, ALU.add))
            for n in range(NTOK):
                m = dve.max(top[:, n, :], vals[:, n, 0:E])
            then(m)
            then(dve.memset(top[:, :, K:8], SENT))
            for n in range(NTOK):
                m = dve.match_replace(marked[:, n, :], top[:, n, :], vals[:, n, :], PICKED)
            then(m)
            then(dve.tensor_scalar(marked[:, :, 0:E], marked[:, :, 0:E], 1e38, None, ALU.is_ge))
            if kind == "top_softmax":
                best = top[:, :, 0:1].to_broadcast([P, NTOK, E])
                dve.tensor_tensor(score[:, :, :], vals[:, :, 0:E], best, ALU.subtract).then_inc(exp_in, 1)
                dve.wait_ge(exp_out, 1)
                source = score
            elif kind == "softmax_top":
                source = vals
            else:
                source = score
            then(dve.tensor_tensor(wt[:, :, 0:E], source[:, :, 0:E], marked[:, :, 0:E], ALU.mult))
            if kind != "softmax_top":
                then(dve.tensor_reduce(tot[:, :], wt[:, :, 0:E], AX, ALU.add))
                then(dve.reciprocal(rtot[:, :], tot[:, :]))
                then(dve.tensor_tensor(wt[:, :, 0:E], wt[:, :, 0:E], over(rtot[:, :], E), ALU.mult))
            if kind == "top_softmax":
                then(dve.memset(wt[:, :, E:EW], 1.0))
            elif kind == "softmax_top":
                then(dve.tensor_scalar(score[:, :, E:EW], score[:, :, E:EW], 1.0, None, ALU.add))
                then(dve.reciprocal(wt[:, :, E:EW], score[:, :, E:EW]))
            then(dve.tensor_copy(parts[:, :, 0:EW], wt[:, :, :]))
            then(dve.tensor_tensor(wt[:, :, :], wt[:, :, :], parts[:, :, 0:EW], ALU.subtract))
            then(dve.tensor_copy(parts[:, :, 32:32 + EW], wt[:, :, :]))
            then(dve.tensor_tensor(wt[:, :, :], wt[:, :, :], parts[:, :, 32:32 + EW], ALU.subtract))
            dve.tensor_copy(parts[:, :, 64:64 + EW], wt[:, :, :]).then_inc(parts_ready, 1)
            for b in range(NB):
                dve.wait_ge(turned, b + 1)
                dve.tensor_copy(partsT[:, b, :], PS[:, b, 0:T // 2].bitcast(BF16)[0:96, :]).then_inc(turned_kept, 1)

            with dve.Fori(0, NB) as b:
                for f in range(NT):
                    dve.wait_ge(silu_ready.sem, silu_ready.at(b, f + 1))
                    dve.wait_ge(up_ready.sem, up_ready.at(b, f + 1))
                    if f >= 1:
                        dve.wait_ge(hid_ready.sem, hid_ready.at(b, f))
                    else:
                        dve.wait_ge(hid_ready.sem, hid_ready.at(b, 0))
                    dve.tensor_tensor(prod[:, :], silu[:, f % 3, :], PS[:, 2 + f % 2, :], ALU.mult)\
                       .then_inc(prod_ready.sem, 1)
                    dve.wait_ge(prod_ready.sem, prod_ready.at(b, f + 1))
                    if f >= 3:
                        dve.wait_ge(hid_used.sem, hid_used.at(b, f - 2))
                    else:
                        dve.wait_ge(hid_used.sem, hid_used.at(b, 0))
                    dve.tensor_tensor(hid[:, f % 3, :], prod[:, :], PS[:, 4 + f % 2, :], ALU.mult)\
                       .then_inc(hid_ready.sem, 1)
                dve.wait_ge(hid_used.sem, hid_used.at(b, NT))
                dve.tensor_tensor(Y[:, b, :], X[:, b, :], PS[:, 6, :], ALU.add).then_inc(out_kept.sem, 1)


TERMS = [(0, 0), (0, 1), (1, 0), (0, 2), (2, 0), (1, 1)]


def attn(nc, tag, X, Y, PS, C, W, causal):
    D = 8 if causal else 4
    SW = 64 if causal else 32
    HG = P // SW
    NG = 8
    NO = NG * HG // 4
    MR = 6 * D
    NU = TT * HG
    NPR = HG // 2
    STEPS = NG * TT
    KA = HG * 3 // 4 if HG > 2 else HG
    with ExitStack() as ctx:
        s = Stage(nc, ctx)
        xs = s.sb(f"{tag}_xs", [P, T])
        qk = s.sb(f"{tag}_qk", [P, 2, T])
        rot = s.sb(f"{tag}_rot", [P, 2, T])
        qk_parts = s.sb(f"{tag}_qk_parts", [P, 3, 2, T], BF16)
        q_str = s.sb(f"{tag}_q_str", [P, NG, T], BF16)
        k_str = s.sb(f"{tag}_k_str", [P, NG, HG, T], BF16)
        q_max = s.sb(f"{tag}_q_max", [P, 2, T], BF16)
        v_aug = s.sb(f"{tag}_v_aug", [P, TT, 16, 32])
        mx = s.sb(f"{tag}_mx", [P, 2, TT, HG])
        mx_rest = s.sb(f"{tag}_mx_rest", [P, TT, HG])
        neg_max = s.sb(f"{tag}_neg_max", [P, 2, TT, P], BF16)
        probs = s.sb(f"{tag}_probs", [P, 3, HG, T])
        o_raw = s.sb(f"{tag}_o_raw", [P, NO, T])
        rsum = s.sb(f"{tag}_rsum", [P, 2, T])
        oc = s.sb(f"{tag}_oc", [P, 2, T])
        sq = s.sb(f"{tag}_sq", [P, T])
        lam = s.sb(f"{tag}_lam", [P, 8])
        set_up = s.sem(f"{tag}_set_up")
        lam_in = s.sem(f"{tag}_lam_in")
        lam_exp = s.sem(f"{tag}_lam_exp")
        lam_step = s.sem(f"{tag}_lam_step")
        xs_ready = s.sig(f"{tag}_xs_ready", 1)
        qk_ready = s.sig(f"{tag}_qk_ready", 1)
        v_ready = s.sig(f"{tag}_v_ready", 1)
        v_kept = s.sig(f"{tag}_v_kept", 1)
        split_step = s.sig(f"{tag}_split_step", 6 if not causal else 5)
        parts_ready = s.sig(f"{tag}_parts_ready", 1)
        spread = s.sig(f"{tag}_spread", 2 * NG)
        q_kept = s.sig(f"{tag}_q_kept", NG)
        k_kept = s.sig(f"{tag}_k_kept", NG * KA)
        k_kept_dve = s.sig(f"{tag}_k_kept_dve", NG * (HG - KA))
        scored = s.sig(f"{tag}_scored", NG * NU)
        maxed = s.sig(f"{tag}_maxed", NG * NU)
        max_step = s.sig(f"{tag}_max_step", 3 * NG)
        neg_ready = s.sig(f"{tag}_neg_ready", NG)
        neg_turned = s.sig(f"{tag}_neg_turned", NG)
        q_max_ready = s.sig(f"{tag}_q_max_ready", NG)
        shifted = s.sig(f"{tag}_shifted", STEPS * NPR)
        exped = s.sig(f"{tag}_exped", STEPS * NPR)
        pv_done = s.sig(f"{tag}_pv_done", STEPS)
        o_kept = s.sig(f"{tag}_o_kept", NO)
        gathered = s.sig(f"{tag}_gathered", 1)
        post = s.sig(f"{tag}_post", 1 if causal else 7)
        squares = s.sig(f"{tag}_squares", 1)
        ms_ready = s.sig(f"{tag}_ms_ready", 1)
        rms_ready = s.sig(f"{tag}_rms_ready", 1)
        o_ready = s.sig(f"{tag}_o_ready", 1)
        projected = s.sig(f"{tag}_projected", 1)
        done = s.sig(f"{tag}_done", 1)
        block = ctx.enter_context(nc.Block())
        NEGT = PS[:, 7, 0:T // 2].bitcast(BF16)

        def o_tile(g):
            return (g // 2, (g % 2) * 2) if causal else (g, 0)

        def head_v(g, j):
            return 2 * g + j if causal else 4 * (g % 4) + j

        def keys(tt):
            return (tt + 1) * P if causal else T

        def first_query(st):
            return st * P if causal else 0

        def keep_o(act, b, g):
            o, slot = o_tile(g)
            if slot + HG == 4:
                act.wait_ge(pv_done.sem, pv_done.at(b, (g + 1) * TT))
                act.activation(o_raw[:, o, :], PS[:, 6, :], ACT.Copy).then_inc(o_kept.sem, 1)

        @block.sync
        def _(sp):
            C["load"](sp, tag)

        @block.gpsimd
        def _(pool):
            pool.memset(neg_max[:, :, :, :], 0.0).then_inc(set_up, 1)
            pool.memset(v_aug[:, :, :, :], 0.0).then_inc(set_up, 1)
            pool.wait_ge(set_up, 2)
            pool.memset(v_aug[:, :, :, 8:9], 1.0).then_inc(set_up, 1)

        @block.tensor
        def _(pe):
            C["weights"](pe, tag)

            def pass1(b, g, tt, heads=range(HG)):
                for j in heads:
                    u = g * NU + tt * HG + j
                    if u >= 2:
                        pe.wait_ge(maxed.sem, maxed.at(b, u - 1))
                    n = keys(tt)
                    mm = pe.matmul(PS[:, u % 2, 0:n], q_str[:, g, bass.ts(tt, P)], k_str[:, g, j, 0:n],
                                   start=True, stop=not causal)
                    if causal:
                        mm = pe.matmul(PS[:, u % 2, tt * P:n], C["ident_bf"], W["mask"],
                                       start=False, stop=True)
                    mm.then_inc(scored.sem, 1)

            def pass2(b, g, st, pr):
                if st == 0 and pr == 0:
                    pe.wait_ge(q_max_ready.sem, q_max_ready.at(b, g + 1))
                t0 = first_query(st)
                v = (g * TT + st) * NPR + pr
                if v >= 2:
                    pe.wait_ge(exped.sem, exped.at(b, v - 1))
                for j in (2 * pr, 2 * pr + 1):
                    bank = 2 + 2 * (v % 2) + j % 2
                    mm = pe.matmul(PS[:, bank, 0:T - t0], k_str[:, g, j, bass.ts(st, P)],
                                   q_max[:, g % 2, t0:T], start=True, stop=not causal)
                    if causal:
                        mm = pe.matmul(PS[:, bank, 0:P], C["ident_bf"], W["mask_t"], start=False, stop=True)
                mm.then_inc(shifted.sem, 1)

            def pv(b, g, st):
                o, slot = o_tile(g)
                pe.wait_ge(exped.sem, exped.at(b, (g * TT + st + 1) * NPR))
                if st == 0 and slot == 0 and o > 0:
                    pe.wait_ge(o_kept.sem, o_kept.at(b, o))
                t0 = first_query(st)
                for j in range(HG):
                    at = 32 * (slot + j)
                    mm = pe.matmul(PS[at:at + 32, 6, t0:T], v_aug[:, st, head_v(g, j), :],
                                   probs[:, (g * TT + st) % 3, j, 0:T - t0], start=(st == 0), stop=(st == TT - 1))
                mm.then_inc(pv_done.sem, 1)

            def turn_max(b, g):
                pe.wait_ge(neg_ready.sem, neg_ready.at(b, g + 1))
                if g >= 1:
                    pe.wait_ge(q_max_ready.sem, q_max_ready.at(b, g))
                for tt in range(TT):
                    mm = pe.transpose(NEGT[:, bass.ts(tt, P)], neg_max[:, g % 2, tt, :], C["ident_bf"])
                mm.then_inc(neg_turned.sem, 1)

            with pe.Fori(0, NB) as b:
                pe.wait_ge(done.sem, done.at(b, 0))
                for n, name in enumerate(["q", "k"] if causal else ["q", "k", "q_sw", "k_sw"]):
                    mm = pe.matmul(PS[:, n, :], W[name], X[:, b, :], start=True, stop=True)
                mm.then_inc(qk_ready.sem, 1)
                pe.wait_ge(xs_ready.sem, xs_ready.at(b, 1))
                for st in range(TT):
                    mm = pe.matmul(PS[:, 7, bass.ts(st, P)], xs[:, bass.ts(st, P)], W["v"], start=True, stop=True)
                mm.then_inc(v_ready.sem, 1)
                pe.wait_ge(parts_ready.sem, parts_ready.at(b, 1))
                for g in range(NG):
                    for n in range(2):
                        if g >= 2 and n == 0:
                            pe.wait_ge(q_kept.sem, q_kept.at(b, g - 1))
                        elif g >= 2:
                            pe.wait_ge(k_kept.sem, k_kept.at(b, (g - 1) * KA))
                            if KA < HG:
                                pe.wait_ge(k_kept_dve.sem, k_kept_dve.at(b, (g - 1) * (HG - KA)))
                        for i in range(3):
                            at = ((n * 3 + i) * NG + g) * P
                            mm = pe.matmul(PS[:, 2 + 2 * n + g % 2, :], W["strips"][:, at:at + P],
                                           qk_parts[:, i, n, :], start=(i == 0), stop=(i == 2))
                        mm.then_inc(spread.sem, 1)
                pe.wait_ge(q_kept.sem, q_kept.at(b, NG))
                pe.wait_ge(k_kept.sem, k_kept.at(b, NG * KA))
                if KA < HG:
                    pe.wait_ge(k_kept_dve.sem, k_kept_dve.at(b, NG * (HG - KA)))
                pe.wait_ge(v_kept.sem, v_kept.at(b, 1))
                for g in range(2):
                    for tt in range(TT):
                        pass1(b, g, tt)
                turn_max(b, 0)
                for g in range(NG):
                    for st in range(TT):
                        ahead = g + 2 < NG
                        for pr in range(NPR):
                            if ahead:
                                pass1(b, g + 2, st, (pr,))
                            pass2(b, g, st, pr)
                        for j in range(NPR, HG - 1):
                            if ahead:
                                pass1(b, g + 2, st, (j,))
                        if (g, st) > (0, 0):
                            pv(b, *((g, st - 1) if st else (g - 1, TT - 1)))
                        if ahead:
                            pass1(b, g + 2, st, (HG - 1,))
                        if st == 1 and g + 1 < NG:
                            turn_max(b, g + 1)
                pv(b, NG - 1, TT - 1)
                pe.wait_ge(o_kept.sem, o_kept.at(b, NO))
                pe.wait_ge(maxed.sem, maxed.at(b, NG * NU))
                for par in range(NO // 4):
                    for n, name in enumerate(("pick_o", "pick_sum")):
                        for i in range(4):
                            mm = pe.matmul(PS[32 * i:32 * i + 32, 2 * par + n, :], W[name],
                                           o_raw[:, 4 * par + i, :], start=True, stop=True)
                mm.then_inc(gathered.sem, 1)
                if not causal:
                    pe.wait_ge(squares.sem, squares.at(b, 1))
                    pe.matmul(PS[:, 4, :], W["mean8"], sq[:, :], start=True, stop=True).then_inc(ms_ready.sem, 1)
                pe.wait_ge(o_ready.sem, o_ready.at(b, 1))
                pe.matmul(PS[:, 5, :], W["out"], oc[:, 0, :], start=True, stop=True).then_inc(projected.sem, 1)

        @block.scalar
        def _(act):
            C["weights"](act, tag)
            if not causal:
                act.wait_ge(lam_in, 1)
                act.activation(lam[:, 2:4], lam[:, 0:2], ACT.Exp).then_inc(lam_exp, 1)
            with act.Fori(0, NB) as b:
                act.wait_ge(done.sem, done.at(b, 0))
                act.activation(xs[:, :], X[:, b, :], ACT.Copy).then_inc(xs_ready.sem, 1)
                for g in range(NG):
                    act.wait_ge(spread.sem, spread.at(b, 2 * g + 2))
                    for j in range(KA):
                        act.activation(k_str[:, g, j, :], PS[:, 4 + g % 2, :], ACT.Identity,
                                       bias=W["ones_rows"][:, j:j + 1], scale=W["strip_rows"][:, j:j + 1])\
                           .then_inc(k_kept.sem, 1)
                for g in range(NG):
                    for st in range(TT):
                        n = T - first_query(st)
                        step = g * TT + st
                        if step >= 3:
                            act.wait_ge(pv_done.sem, pv_done.at(b, step - 2))
                        for pr in range(NPR):
                            v = step * NPR + pr
                            act.wait_ge(shifted.sem, shifted.at(b, v + 1))
                            bank = 2 + 2 * (v % 2)
                            act.activation(probs[:, step % 3, 2 * pr:2 * pr + 2, 0:n], PS[:, bank:bank + 2, 0:n],
                                           ACT.Exp).then_inc(exped.sem, 1)
                        if st == 0 and g > 0:
                            keep_o(act, b, g - 1)
                keep_o(act, b, NG - 1)
                if not causal:
                    act.wait_ge(post.sem, post.at(b, 5))
                    act.activation(sq[:, :], oc[:, 0, :], ACT.Square).then_inc(squares.sem, 1)
                    act.wait_ge(ms_ready.sem, ms_ready.at(b, 1))
                    act.activation(rsum[:, 0, :], PS[:, 4, :], ACT.Sqrt, bias=W["eps"]).then_inc(rms_ready.sem, 1)

        @block.vector
        def _(dve):
            C["weights"](dve, tag)
            if not causal:
                for n in range(2):
                    dve.tensor_tensor(sq[:, 4 * n:4 * n + 4], W["lam_q"][:, 4 * n:4 * n + 4],
                                      W["lam_k"][:, 4 * n:4 * n + 4], ALU.mult).then_inc(lam_step, 1)
                dve.wait_ge(lam_step, 2)
                dve.tensor_reduce(lam[:, 0:2], sq[:, 0:8].rearrange("p (n e) -> p n e", e=4), AX, ALU.add)\
                   .then_inc(lam_in, 1)
                dve.wait_ge(lam_exp, 1)
                dve.tensor_tensor(lam[:, 4:5], lam[:, 3:4], lam[:, 2:3], ALU.subtract).then_inc(lam_step, 1)
                dve.wait_ge(lam_step, 3)
                dve.tensor_scalar(lam[:, 5:6], lam[:, 4:5], -LAMBDA_INIT, None, ALU.add).then_inc(lam_step, 1)
                dve.wait_ge(lam_step, 4)
            dve.wait_ge(set_up, 3)

            def maxima(b, g, tt):
                for j in range(HG):
                    u = g * NU + tt * HG + j
                    dve.wait_ge(scored.sem, scored.at(b, u + 1))
                    if tt == 0 and j == 0 and g >= 2:
                        dve.wait_ge(max_step.sem, max_step.at(b, 3 * (g - 1)))
                    dve.tensor_reduce(mx[:, g % 2, tt, j:j + 1], PS[:, u % 2, 0:keys(tt)], AX, ALU.max)\
                       .then_inc(maxed.sem, 1)

            def negate(b, g):
                rows = neg_max[:, g % 2, :, :].rearrange("p t (j w) -> p t j w", w=SW)
                dve.wait_ge(maxed.sem, maxed.at(b, (g + 1) * NU))
                if g >= 2:
                    dve.wait_ge(neg_turned.sem, neg_turned.at(b, g - 1))
                m = mx[:, g % 2, :, :]
                dve.tensor_scalar(rows[:, :, :, MR], m, -1.0, None, ALU.mult).then_inc(max_step.sem, 1)
                dve.wait_ge(max_step.sem, max_step.at(b, 3 * g + 1))
                if g >= 1:
                    dve.wait_ge(neg_ready.sem, neg_ready.at(b, g))
                dve.scalar_tensor_tensor(mx_rest[:, :, :], m, -1.0, rows[:, :, :, MR], ALU.mult, ALU.subtract)\
                   .then_inc(max_step.sem, 1)
                dve.wait_ge(max_step.sem, max_step.at(b, 3 * g + 2))
                dve.tensor_copy(rows[:, :, :, MR + 1], mx_rest[:, :, :]).then_inc(max_step.sem, 1)
                dve.wait_ge(max_step.sem, max_step.at(b, 3 * g + 3))
                dve.tensor_tensor(rows[:, :, :, MR + 2], mx_rest[:, :, :], rows[:, :, :, MR + 1], ALU.subtract)\
                   .then_inc(neg_ready.sem, 1)

            def add_max(b, g):
                dve.wait_ge(neg_turned.sem, neg_turned.at(b, g + 1))
                if g >= 2:
                    dve.wait_ge(shifted.sem, shifted.at(b, (g - 1) * TT * NPR))
                dve.tensor_tensor(q_max[:, g % 2, :], q_str[:, g, :], NEGT, ALU.add).then_inc(q_max_ready.sem, 1)

            with dve.Fori(0, NB) as b:
                dve.wait_ge(qk_ready.sem, qk_ready.at(b, 1))
                dve.wait_ge(done.sem, done.at(b, 0))
                if causal:
                    dve.tensor_scalar(qk[:, 0, :], PS[:, 0, :], float(D) ** -0.5, None, ALU.mult)\
                       .then_inc(split_step.sem, 1)
                    dve.tensor_copy(qk[:, 1, :], PS[:, 1, :]).then_inc(split_step.sem, 1)
                    n = 2
                else:
                    cos = W["cos"].rearrange("p (n t) -> p n t", n=2)
                    sin = W["sin"].rearrange("p (n t) -> p n t", n=2)
                    dve.tensor_tensor(qk[:, :, :], PS[:, 0:2, :], cos, ALU.mult).then_inc(split_step.sem, 1)
                    dve.tensor_tensor(rot[:, :, :], PS[:, 2:4, :], sin, ALU.mult).then_inc(split_step.sem, 1)
                    dve.wait_ge(split_step.sem, split_step.at(b, 2))
                    dve.tensor_tensor(qk[:, :, :], qk[:, :, :], rot[:, :, :], ALU.add).then_inc(split_step.sem, 1)
                    n = 3
                dve.wait_ge(split_step.sem, split_step.at(b, n))
                dve.tensor_copy(qk_parts[:, 0, :, :], qk[:, :, :]).then_inc(split_step.sem, 1)
                dve.wait_ge(split_step.sem, split_step.at(b, n + 1))
                dve.tensor_tensor(qk[:, :, :], qk[:, :, :], qk_parts[:, 0, :, :], ALU.subtract)\
                   .then_inc(split_step.sem, 1)
                dve.wait_ge(split_step.sem, split_step.at(b, n + 2))
                dve.tensor_copy(qk_parts[:, 1, :, :], qk[:, :, :]).then_inc(split_step.sem, 1)
                dve.wait_ge(split_step.sem, split_step.at(b, n + 3))
                dve.tensor_tensor(qk_parts[:, 2, :, :], qk[:, :, :], qk_parts[:, 1, :, :], ALU.subtract)\
                   .then_inc(parts_ready.sem, 1)
                dve.wait_ge(v_ready.sem, v_ready.at(b, 1))
                dve.tensor_copy(v_aug[:, :, :, 0:8].rearrange("p s h e -> p (s h) e"),
                                PS[:, 7, :].rearrange("p (sh e) -> p sh e", e=8)).then_inc(v_kept.sem, 1)
                for g in range(NG):
                    dve.wait_ge(spread.sem, spread.at(b, 2 * g + 1))
                    dve.tensor_copy(q_str[:, g, :], PS[:, 2 + g % 2, :]).then_inc(q_kept.sem, 1)
                    if KA < HG:
                        dve.wait_ge(k_kept.sem, k_kept.at(b, (g + 1) * KA))
                    for j in range(KA, HG):
                        dve.tensor_scalar(k_str[:, g, j, :], PS[:, 4 + g % 2, :], W["strip_rows"][:, j:j + 1],
                                          W["ones_rows"][:, j:j + 1], ALU.mult, ALU.add).then_inc(k_kept_dve.sem, 1)
                for g in range(2):
                    for tt in range(TT):
                        maxima(b, g, tt)
                    negate(b, g)
                dve.wait_ge(q_kept.sem, q_kept.at(b, NG))
                add_max(b, 0)
                for g in range(NG):
                    for st in range(TT):
                        if g + 2 < NG:
                            maxima(b, g + 2, st)
                        if st == 1 and g + 1 < NG:
                            add_max(b, g + 1)
                    if g + 2 < NG:
                        negate(b, g + 2)
                dve.wait_ge(gathered.sem, gathered.at(b, 1))
                if causal:
                    dve.reciprocal(rsum[:, 0, :], PS[:, 1, :]).then_inc(post.sem, 1)
                    dve.wait_ge(post.sem, post.at(b, 1))
                    dve.tensor_tensor(oc[:, 0, :], PS[:, 0, :], rsum[:, 0, :], ALU.mult).then_inc(o_ready.sem, 1)
                    dve.wait_ge(projected.sem, projected.at(b, 1))
                    dve.scalar_tensor_tensor(Y[:, b, :], PS[:, 5, :], W["b_out"], X[:, b, :], ALU.add, ALU.add)\
                       .then_inc(done.sem, 1)
                else:
                    for par in range(2):
                        dve.reciprocal(rsum[:, par, :], PS[:, 2 * par + 1, :]).then_inc(post.sem, 1)
                    dve.wait_ge(post.sem, post.at(b, 2))
                    for par in range(2):
                        dve.tensor_tensor(oc[:, par, :], PS[:, 2 * par, :], rsum[:, par, :], ALU.mult)\
                           .then_inc(post.sem, 1)
                    dve.wait_ge(post.sem, post.at(b, 4))
                    dve.scalar_tensor_tensor(oc[:, 0, :], oc[:, 1, :], lam[:, 5:6], oc[:, 0, :], ALU.mult, ALU.add)\
                       .then_inc(post.sem, 1)
                    dve.wait_ge(rms_ready.sem, rms_ready.at(b, 1))
                    dve.reciprocal(rsum[:, 1, :], rsum[:, 0, :]).then_inc(post.sem, 1)
                    dve.wait_ge(post.sem, post.at(b, 6))
                    dve.tensor_tensor(oc[:, 1, :], oc[:, 0, :], rsum[:, 1, :], ALU.mult).then_inc(post.sem, 1)
                    dve.wait_ge(post.sem, post.at(b, 7))
                    dve.tensor_scalar(oc[:, 0, :], oc[:, 1, :], W["subln"], 1.0 - LAMBDA_INIT, ALU.mult, ALU.mult)\
                       .then_inc(o_ready.sem, 1)
                    dve.wait_ge(projected.sem, projected.at(b, 1))
                    dve.tensor_tensor(Y[:, b, :], PS[:, 5, :], X[:, b, :], ALU.add).then_inc(done.sem, 1)


def attn0(nc, tag, X, Y, PS, C, W, scratch):
    W1 = 63
    NQ, NK, H = 4, 4, 8
    NCH = 2 * NQ * NK
    RING = 3
    GATE = ACT.Gelu
    with ExitStack() as ctx:
        s = Stage(nc, ctx)
        disp = s.sb(f"{tag}_disp", [P, 2, T])
        a_pad = s.sb(f"{tag}_a_pad", [P, 2, 2, W1 + T])
        d_pad = s.sb(f"{tag}_d_pad", [P, 2, 2, W1 + T])
        x_pad = s.sb(f"{tag}_x_pad", [P, W1 + T + 1])
        v_tok = s.sb(f"{tag}_v_tok", [P, 2, 8, P])
        pos = s.sb(f"{tag}_pos", [P, 64])
        b_half = s.sb(f"{tag}_b_half", [P, 1])
        bond = s.sb(f"{tag}_bond", [P, RING, 4, T])
        dmg = s.sb(f"{tag}_dmg", [P, RING, 4, T])
        tanh = s.sb(f"{tag}_tanh", [P, 2, T])
        logit = s.sb(f"{tag}_logit", [P, 2, 8, T])
        probs = s.sb(f"{tag}_probs", [P, TT, 16, 64])
        masked = s.sb(f"{tag}_masked", [P, 2, T])
        mx = s.sb(f"{tag}_mx", [P, 16])
        tot = s.sb(f"{tag}_tot", [P, TT, 16])
        rtot = s.sb(f"{tag}_rtot", [P, TT, 16])
        band = s.sb(f"{tag}_band", [P, 2, 16, P])
        band_t = s.sb(f"{tag}_band_t", [P, 16, P])
        o_tok = s.sb(f"{tag}_o_tok", [P, P])
        o_t = s.sb(f"{tag}_o_t", [P, T])
        set_up = s.sem(f"{tag}_set_up")
        zeroed = s.sem(f"{tag}_zeroed")
        pos_ready = s.sem(f"{tag}_pos_ready")
        pos_kept = s.sem(f"{tag}_pos_kept")
        x_kept = s.sig(f"{tag}_x_kept", 1)
        disp_ready = s.sig(f"{tag}_disp_ready", 1)
        disp_kept = s.sig(f"{tag}_disp_kept", 1)
        a_ready = s.sig(f"{tag}_a_ready", 1)
        a_kept = s.sig(f"{tag}_a_kept", 1)
        d_ready = s.sig(f"{tag}_d_ready", 1)
        d_kept = s.sig(f"{tag}_d_kept", 1)
        v_ready = s.sig(f"{tag}_v_ready", 1)
        v_kept = s.sig(f"{tag}_v_kept", 1)
        bond_in = s.sig(f"{tag}_bond_in", NCH)
        dmg_in_pool = s.sig(f"{tag}_dmg_in_pool", NCH * 3 // 4)
        dmg_in_dve = s.sig(f"{tag}_dmg_in_dve", NCH // 4)
        bond_gelu = s.sig(f"{tag}_bond_gelu", NCH)
        dmg_gelu = s.sig(f"{tag}_dmg_gelu", NCH)
        bond_used = s.sig(f"{tag}_bond_used", NCH)
        dmg_used = s.sig(f"{tag}_dmg_used", NCH)
        tanh_ready = s.sig(f"{tag}_tanh_ready", 8)
        logit_ready = s.sig(f"{tag}_logit_ready", 8)
        turned = s.sig(f"{tag}_turned", TT)
        masked_ready = s.sig(f"{tag}_masked_ready", 1)
        maxed = s.sig(f"{tag}_maxed", TT)
        centred = s.sig(f"{tag}_centred", TT)
        exped = s.sig(f"{tag}_exped", 1)
        summed = s.sig(f"{tag}_summed", 1)
        inverted = s.sig(f"{tag}_inverted", 1)
        skewed = [s.sig(f"{tag}_skewed{i}", 32) for i in range(TT)]
        banded = [s.sig(f"{tag}_banded{i}", 16) for i in range(TT)]
        band_turned = s.sig(f"{tag}_band_turned", 4 * TT)
        band_kept_act = s.sig(f"{tag}_band_kept_act", 2 * TT)
        band_kept_dve = s.sig(f"{tag}_band_kept_dve", 2 * TT)
        pv_done = s.sig(f"{tag}_pv_done", TT)
        o_scaled = s.sig(f"{tag}_o_scaled", TT)
        o_turned = s.sig(f"{tag}_o_turned", TT)
        o_kept = s.sig(f"{tag}_o_kept", TT)
        projected = s.sig(f"{tag}_projected", 1)
        y_done = s.sig(f"{tag}_y_done", 1)
        block = ctx.enter_context(nc.Block())

        TILE = 16 * 2 * 64 * P

        def chunk(n):
            return n // 16, (n // 4) % 4, n % 4

        def batches(eng, body, tail):
            body(0, 0, None, 1)
            body(1, 1, 0, 2)
            with eng.Fori(1, NB // 2 - 1) as i:
                body(i * 2, 0, i * 2 - 1, i * 2 + 1)
                body(i * 2 + 1, 1, i * 2, i * 2 + 2)
            body(NB - 2, 0, NB - 3, NB - 1)
            body(NB - 1, 1, NB - 2, None)
            tail(NB - 1, 1)

        def plan(n):
            if n in (1, 3, 5, 7):
                return "soften", (n - 1) // 2
            if n == 9:
                return "exp", 0
            if n in (14, 17, 20, 23):
                return "combine", (n - 14) // 3
            if n == 26:
                return "finish", 0
            if n == 28:
                return "project", 0
            return None, 0

        def damage(eng, par, n):
            g, q, k = chunk(n)
            d0 = 16 * q + k
            row = d_pad[:, par, g, :]
            part = [row.ap[0][0], row.ap[0][1]]
            later = bass.AP(tensor=row.tensor, offset=row.offset + d0, ap=[part, [4, 4], [1, T]])
            own = bass.AP(tensor=row.tensor, offset=row.offset + W1, ap=[part, [0, 4], [1, T]])
            return eng.tensor_tensor(dmg[:, n % RING, :, :], later, own, ALU.subtract)

        @block.sync
        def _(sp):
            C["load"](sp, tag)
            sp.wait_ge(set_up, 5)
            for i in range(TT):
                for part in range(2):
                    base = (2 * i + part) * P * 16 * 64
                    sp.dma_start(scratch[base:base + P * 16 * 64].rearrange("(p c) -> p c", p=P),
                                 probs[:, 0, :, :].rearrange("p h d -> p (h d)")).then_inc(zeroed, 16)
            sp.wait_ge(zeroed, 16 * 2 * TT)

            def skew(b):
                for tt in range(TT):
                    base = tt * TILE
                    if tt == 0:
                        sp.wait_ge(exped.sem, exped.at(b, 1))
                    sp.wait_ge(banded[tt].sem, banded[tt].at(b, 0))
                    for half in range(2):
                        dst = bass.AP(
                            tensor=scratch.tensor, offset=scratch.offset + base + half * 64 * P,
                            ap=[[P + 1, 64], [2 * 64 * P, 16], [1, 64]])
                        sp.dma_start(dst, probs[64 * half:64 * half + 64, tt, :, :]).then_inc(skewed[tt].sem, 16)
                    sp.wait_ge(skewed[tt].sem, skewed[tt].at(b, 32))
                    if tt >= 2:
                        sp.wait_ge(band_turned.sem, band_turned.at(b, 4 * (tt - 1)))
                    else:
                        sp.wait_ge(band_turned.sem, band_turned.at(b, 0))
                    src = bass.AP(tensor=scratch.tensor, offset=scratch.offset + base,
                                  ap=[[P, P], [2 * 64 * P, 16], [1, P]])
                    sp.dma_start(band[:, tt % 2, :, :], src).then_inc(banded[tt].sem, 16)

            for b in range(NB):
                skew(b)

        @block.gpsimd
        def _(pool):
            pool.memset(a_pad[:, :, :, 0:W1], 0.0).then_inc(set_up, 1)
            pool.memset(d_pad[:, :, :, 0:W1], 0.0).then_inc(set_up, 1)
            pool.memset(x_pad[:, 0:W1], 0.0).then_inc(set_up, 1)
            pool.memset(x_pad[:, W1 + T:W1 + T + 1], 0.0).then_inc(set_up, 1)
            pool.memset(probs[:, 0, :, :], 0.0).then_inc(set_up, 1)
            pool.wait_ge(set_up, 5)

            def body(b, par, before, after):
                pool.wait_ge(d_kept.sem, d_kept.at(b, 1))
                for n in range(NCH):
                    g, q, k = chunk(n)
                    if k == 3:
                        continue
                    if n >= RING:
                        pool.wait_ge(dmg_used.sem, dmg_used.at(b, n - RING + 1))
                    else:
                        pool.wait_ge(dmg_used.sem, dmg_used.at(b, 0))
                    damage(pool, par, n).then_inc(dmg_in_pool.sem, 1)

            batches(pool, body, lambda b, par: None)

        @block.tensor
        def _(pe):
            C["weights"](pe, tag)
            pe.matmul(PS[:, 0, 0:64], W["w_pos"], W["rel"], start=True, stop=True).then_inc(pos_ready, 1)
            pe.wait_ge(pos_kept, 1)

            def project(b, par, before):
                if before is not None:
                    pe.wait_ge(y_done.sem, y_done.at(before, 1))
                for g in range(2):
                    mm = pe.matmul(PS[:, 4 + g, :], W["disp"][:, bass.ts(g, P)], X[:, b, :], start=True, stop=True)
                mm.then_inc(disp_ready.sem, 1)
                pe.wait_ge(disp_kept.sem, disp_kept.at(b, 1))
                for g in range(2):
                    mm = pe.matmul(PS[:, 6 + g, :], W["strain"], disp[:, g, :], start=True, stop=True)
                mm.then_inc(a_ready.sem, 1)
                for g in range(2):
                    mm = pe.matmul(PS[:, 4 + g, :], W["dmg"], disp[:, g, :], start=True, stop=True)
                mm.then_inc(d_ready.sem, 1)
                pe.wait_ge(a_kept.sem, a_kept.at(b, 1))
                pe.wait_ge(x_kept.sem, x_kept.at(b, 1))
                for j in range(8):
                    mm = pe.matmul(PS[:, 6 + j // 4, bass.ts(j % 4, P)], x_pad[:, 64 * j:64 * j + P], W["val"],
                                   start=True, stop=True)
                mm.then_inc(v_ready.sem, 1)
                pe.wait_ge(d_kept.sem, d_kept.at(b, 1))
                pe.wait_ge(v_kept.sem, v_kept.at(b, 1))

            def soften(b, par, tt):
                pe.wait_ge(logit_ready.sem, logit_ready.at(b, 8))
                if tt >= 1:
                    pe.wait_ge(centred.sem, centred.at(b, tt))
                for g in range(2):
                    for q in range(NQ):
                        mm = pe.transpose(PS[:, 4 + g, bass.ts(q, P)], logit[:, par, 4 * g + q, bass.ts(tt, P)],
                                          C["ident"])
                mm.then_inc(turned.sem, 1)

            def combine(b, par, tt):
                pe.wait_ge(banded[tt].sem, banded[tt].at(b, 16))
                for r in range(4):
                    if tt >= 1 or r >= 2:
                        m = 4 * tt + r - 2
                        kept = band_kept_act if m % 2 == 0 else band_kept_dve
                        pe.wait_ge(kept.sem, kept.at(b, m // 2 + 1))
                    for hh in range(4):
                        mm = pe.transpose(PS[:, 6 + r % 2, bass.ts(hh, P)], band[:, tt % 2, 4 * r + hh, :],
                                          C["ident"])
                    mm.then_inc(band_turned.sem, 1)
                pe.wait_ge(band_kept_act.sem, band_kept_act.at(b, 2 * tt + 2))
                pe.wait_ge(band_kept_dve.sem, band_kept_dve.at(b, 2 * tt + 2))
                if tt >= 1:
                    pe.wait_ge(o_scaled.sem, o_scaled.at(b, tt))
                else:
                    pe.wait_ge(centred.sem, centred.at(b, TT))
                for h in range(16):
                    for half in range(2):
                        rows = slice(64 * half, 64 * half + 64)
                        mm = pe.matmul(PS[rows, 4, 8 * h:8 * h + 8], band_t[:, h, rows],
                                       v_tok[:, par, 2 * tt + half, 8 * h:8 * h + 8], start=True, stop=True)
                mm.then_inc(pv_done.sem, 1)
                pe.wait_ge(o_scaled.sem, o_scaled.at(b, tt + 1))
                if tt >= 1:
                    pe.wait_ge(o_kept.sem, o_kept.at(b, tt))
                pe.transpose(PS[:, 5, 0:P], o_tok[:, :], C["ident"]).then_inc(o_turned.sem, 1)

            def finish(b):
                pe.wait_ge(o_kept.sem, o_kept.at(b, TT))
                pe.matmul(PS[:, 5, :], W["c_proj"], o_t[:, :], start=True, stop=True).then_inc(projected.sem, 1)

            def body(b, par, before, after):
                for n in range(NCH):
                    g, q, k = chunk(n)
                    gq = n // 4
                    if k == 0:
                        if gq >= 2:
                            pe.wait_ge(tanh_ready.sem, tanh_ready.at(b, gq - 1))
                            pe.wait_ge(logit_ready.sem, logit_ready.at(b, gq - 1))
                        else:
                            pe.wait_ge(tanh_ready.sem, tanh_ready.at(b, 0))
                            pe.wait_ge(logit_ready.sem, logit_ready.at(b, 0))
                    for bank, data, ready, used, wname in ((gq % 2, bond, bond_gelu, bond_used, "w_bond"),
                                                           (2 + gq % 2, dmg, dmg_gelu, dmg_used, "w_dmg_out")):
                        pe.wait_ge(ready.sem, ready.at(b, n + 1))
                        for c in range(4):
                            mm = pe.matmul(PS[32 * c:32 * c + 32, bank, :], W[wname][:, 32 * k:32 * k + 32],
                                           data[:, n % RING, c, :], start=(k == 0), stop=(k == 3))
                        mm.then_inc(used.sem, 1)
                    what, tt = plan(n)
                    if what == "soften" and before is not None:
                        soften(before, 1 - par, tt)
                    elif what == "combine" and before is not None:
                        combine(before, 1 - par, tt)
                    elif what == "finish" and before is not None:
                        finish(before)
                    elif what == "project" and after is not None:
                        project(after, 1 - par, before)

            def tail(b, par):
                for tt in range(TT):
                    soften(b, par, tt)
                for tt in range(TT):
                    combine(b, par, tt)
                finish(b)

            project(0, 0, None)
            batches(pe, body, tail)

        @block.scalar
        def _(act):
            C["weights"](act, tag)
            act.wait_ge(set_up, 5)
            act.wait_ge(pos_kept, 2)

            def project(b, par):
                act.wait_ge(v_ready.sem, v_ready.at(b, 0))
                act.activation(x_pad[:, W1:W1 + T], X[:, b, :], ACT.Copy).then_inc(x_kept.sem, 1)
                act.wait_ge(disp_ready.sem, disp_ready.at(b, 1))
                act.activation(disp[:, :, :], PS[:, 4:6, :], ACT.Copy).then_inc(disp_kept.sem, 1)
                act.wait_ge(v_ready.sem, v_ready.at(b, 1))
                act.activation(v_tok[:, par, :, :].rearrange("p j c -> p (j c)"),
                               PS[:, 6:8, :].rearrange("p a c -> p (a c)"), ACT.Copy).then_inc(v_kept.sem, 1)

            def exps(b):
                act.wait_ge(centred.sem, centred.at(b, TT))
                act.activation(probs[:, :, :, :], probs[:, :, :, :], ACT.Exp).then_inc(exped.sem, 1)

            def combine(b, tt):
                for r in (0, 2):
                    act.wait_ge(band_turned.sem, band_turned.at(b, 4 * tt + r + 1))
                    if tt >= 1:
                        act.wait_ge(pv_done.sem, pv_done.at(b, tt))
                    else:
                        act.wait_ge(pv_done.sem, pv_done.at(b, 0))
                    act.activation(band_t[:, 4 * r:4 * r + 4, :], PS[:, 6, :].rearrange("p (h t) -> p h t", h=4),
                                   ACT.Copy).then_inc(band_kept_act.sem, 1)

            def to_tanh(b, gq):
                act.wait_ge(dmg_used.sem, dmg_used.at(b, 4 * gq + 4))
                if gq >= 2:
                    act.wait_ge(logit_ready.sem, logit_ready.at(b, gq - 1))
                else:
                    act.wait_ge(logit_ready.sem, logit_ready.at(b, 0))
                act.activation(tanh[:, gq % 2, :], PS[:, 2 + gq % 2, :], ACT.Tanh, bias=b_half[:, :], scale=0.5)\
                   .then_inc(tanh_ready.sem, 1)

            def body(b, par, before, after):
                for n in range(NCH):
                    g, q, k = chunk(n)
                    act.wait_ge(bond_in.sem, bond_in.at(b, n + 1))
                    act.activation(bond[:, n % RING, :, :], bond[:, n % RING, :, :], GATE).then_inc(bond_gelu.sem, 1)
                    if k == 3:
                        act.wait_ge(dmg_in_dve.sem, dmg_in_dve.at(b, n // 4 + 1))
                    else:
                        act.wait_ge(dmg_in_pool.sem, dmg_in_pool.at(b, 3 * (n // 4) + k + 1))
                    act.activation(dmg[:, n % RING, :, :], dmg[:, n % RING, :, :], GATE, bias=W["b_dmg"])\
                       .then_inc(dmg_gelu.sem, 1)
                    if k == 0 and n > 0:
                        to_tanh(b, n // 4 - 1)
                    what, tt = plan(n)
                    if what == "exp" and before is not None:
                        exps(before)
                    elif what == "combine" and before is not None:
                        combine(before, tt)
                    elif what == "project" and after is not None:
                        project(after, 1 - par)
                to_tanh(b, 7)

            def tail(b, par):
                exps(b)
                for tt in range(TT):
                    combine(b, tt)

            project(0, 0)
            batches(act, body, tail)

        @block.vector
        def _(dve):
            C["weights"](dve, tag)
            dve.wait_ge(set_up, 5)
            dve.wait_ge(pos_ready, 1)
            dve.tensor_copy(pos[:, :], PS[:, 0, 0:64]).then_inc(pos_kept, 1)
            dve.tensor_scalar(b_half[:, :], W["b_out"], 0.5, None, ALU.mult).then_inc(pos_kept, 1)
            dve.wait_ge(pos_kept, 2)
            dve.wait_ge(zeroed, 16 * 2 * TT)

            def project(b, par):
                dve.wait_ge(a_ready.sem, a_ready.at(b, 1))
                dve.tensor_copy(a_pad[:, par, :, W1:W1 + T], PS[:, 6:8, :]).then_inc(a_kept.sem, 1)
                dve.wait_ge(d_ready.sem, d_ready.at(b, 1))
                dve.tensor_copy(d_pad[:, par, :, W1:W1 + T], PS[:, 4:6, :]).then_inc(d_kept.sem, 1)

            def soften(b, tt):
                dve.wait_ge(turned.sem, turned.at(b, tt + 1))
                dve.wait_ge(skewed[tt].sem, skewed[tt].at(b, 0))
                src = PS[:, 4:6, :]
                if tt == 0:
                    dve.tensor_tensor(masked[:, :, :], src, W["mask"].rearrange("p (g c) -> p g c", g=2), ALU.add)\
                       .then_inc(masked_ready.sem, 1)
                    dve.wait_ge(masked_ready.sem, masked_ready.at(b, 1))
                    dve.wait_ge(summed.sem, summed.at(b, 0))
                    src = masked[:, :, :]
                by_head = src.rearrange("p g (d h) -> p g h d", h=H)
                dve.tensor_reduce(mx[:, :].rearrange("p (g h) -> p g h", g=2), by_head, AX, ALU.max)\
                   .then_inc(maxed.sem, 1)
                dve.wait_ge(maxed.sem, maxed.at(b, tt + 1))
                for g in range(2):
                    m = dve.tensor_tensor(probs[:, tt, 8 * g:8 * g + 8, :],
                                          src[:, g, :].rearrange("p (d h) -> p h d", h=H),
                                          mx[:, 8 * g:8 * g + 8].rearrange("p (h o) -> p h o", o=1)
                                          .to_broadcast([P, H, 64]), ALU.subtract)
                m.then_inc(centred.sem, 1)

            def sums(b):
                dve.wait_ge(exped.sem, exped.at(b, 1))
                dve.tensor_reduce(tot[:, :, :], probs[:, :, :, :], AX, ALU.add).then_inc(summed.sem, 1)
                dve.wait_ge(summed.sem, summed.at(b, 1))
                dve.reciprocal(rtot[:, :, :], tot[:, :, :]).then_inc(inverted.sem, 1)

            def combine(b, tt):
                for r in (1, 3):
                    dve.wait_ge(band_turned.sem, band_turned.at(b, 4 * tt + r + 1))
                    dve.tensor_copy(band_t[:, 4 * r:4 * r + 4, :], PS[:, 7, :].rearrange("p (h t) -> p h t", h=4))\
                       .then_inc(band_kept_dve.sem, 1)
                dve.wait_ge(pv_done.sem, pv_done.at(b, tt + 1))
                dve.wait_ge(inverted.sem, inverted.at(b, 1))
                if tt >= 1:
                    dve.wait_ge(o_turned.sem, o_turned.at(b, tt))
                dve.tensor_tensor(o_tok[:, :].rearrange("p (h e) -> p h e", e=8),
                                  PS[:, 4, 0:P].rearrange("p (h e) -> p h e", e=8),
                                  rtot[:, tt, :].rearrange("p (h o) -> p h o", o=1).to_broadcast([P, 16, 8]),
                                  ALU.mult).then_inc(o_scaled.sem, 1)
                dve.wait_ge(o_turned.sem, o_turned.at(b, tt + 1))
                dve.tensor_copy(o_t[:, bass.ts(tt, P)], PS[:, 5, 0:P]).then_inc(o_kept.sem, 1)

            def finish(b):
                dve.wait_ge(projected.sem, projected.at(b, 1))
                dve.tensor_tensor(Y[:, b, :], X[:, b, :], PS[:, 5, :], ALU.add).then_inc(y_done.sem, 1)

            def to_logit(b, par, gq):
                dve.wait_ge(bond_used.sem, bond_used.at(b, 4 * gq + 4))
                dve.wait_ge(tanh_ready.sem, tanh_ready.at(b, gq + 1))
                dve.scalar_tensor_tensor(logit[:, par, gq, :], tanh[:, gq % 2, :], -5.0, PS[:, gq % 2, :],
                                         ALU.mult, ALU.add).then_inc(logit_ready.sem, 1)

            def body(b, par, before, after):
                dve.wait_ge(a_kept.sem, a_kept.at(b, 1))
                dve.wait_ge(d_kept.sem, d_kept.at(b, 1))
                for n in range(NCH):
                    g, q, k = chunk(n)
                    if n >= RING:
                        dve.wait_ge(bond_used.sem, bond_used.at(b, n - RING + 1))
                    else:
                        dve.wait_ge(bond_used.sem, bond_used.at(b, 0))
                    for c in range(4):
                        d = 16 * q + 4 * c + k
                        m = dve.scalar_tensor_tensor(bond[:, n % RING, c, :], a_pad[:, par, g, d:d + T],
                                                     pos[:, d:d + 1], a_pad[:, par, g, W1:W1 + T],
                                                     ALU.add, ALU.subtract)
                    m.then_inc(bond_in.sem, 1)
                    if k == 3:
                        dve.wait_ge(dmg_used.sem, dmg_used.at(b, n - RING + 1))
                        damage(dve, par, n).then_inc(dmg_in_dve.sem, 1)
                    if k == 1 and n > 4:
                        to_logit(b, par, n // 4 - 1)
                    what, tt = plan(n)
                    if what == "soften" and before is not None:
                        soften(before, tt)
                    elif what == "exp" and before is not None:
                        sums(before)
                    elif what == "combine" and before is not None:
                        combine(before, tt)
                    elif what == "finish" and before is not None:
                        finish(before)
                    elif what == "project" and after is not None:
                        project(after, 1 - par)
                to_logit(b, par, 7)

            def tail(b, par):
                for tt in range(TT):
                    soften(b, tt)
                sums(b)
                for tt in range(TT):
                    combine(b, tt)
                finish(b)

            project(0, 0)
            batches(dve, body, tail)


def attn2(nc, tag, X, Y, PS, C, W):
    with ExitStack() as ctx:
        s = Stage(nc, ctx)
        q_sb = s.sb(f"{tag}_q", [P, T])
        v_sb = s.sb(f"{tag}_v", [P, T])
        sq = s.sb(f"{tag}_sq", [P, 2, T])
        kv = s.sb(f"{tag}_kv", [P, T])
        scaled = s.sb(f"{tag}_scaled", [P, T])
        norm = s.sb(f"{tag}_norm", [P, 8])
        rnorm = s.sb(f"{tag}_rnorm", [P, 8])
        feat = s.sb(f"{tag}_feat", [P, 1])
        projected = s.sig(f"{tag}_projected", 1)
        squared = s.sig(f"{tag}_squared", 2)
        copied = s.sig(f"{tag}_copied", 2)
        summed = s.sig(f"{tag}_summed", 1)
        norm_ready = s.sig(f"{tag}_norm_ready", 1)
        clipped = s.sig(f"{tag}_clipped", 1)
        rnorm_ready = s.sig(f"{tag}_rnorm_ready", 1)
        spread = s.sig(f"{tag}_spread", 1)
        kv_ready = s.sig(f"{tag}_kv_ready", 1)
        feat_ready = s.sig(f"{tag}_feat_ready", 1)
        scaled_ready = s.sig(f"{tag}_scaled_ready", 1)
        done = s.sig(f"{tag}_done", 1)
        block = ctx.enter_context(nc.Block())

        @block.sync
        def _(sp):
            C["load"](sp, tag)

        @block.tensor
        def _(pe):
            C["weights"](pe, tag)
            with pe.Fori(0, NB) as b:
                pe.wait_ge(done.sem, done.at(b, 0))
                for n, name in enumerate(("q", "k", "v")):
                    mm = pe.matmul(PS[:, n, :], W[name], X[:, b, :], start=True, stop=True)
                mm.then_inc(projected.sem, 1)
                for n in range(2):
                    pe.wait_ge(squared.sem, squared.at(b, n + 1))
                    for t in range(TT):
                        mm = pe.matmul(PS[:, 3, 4 * n + t:4 * n + t + 1], sq[:, n, bass.ts(t, P)],
                                       W["ones"][:, 0:1], start=True, stop=True)
                mm.then_inc(summed.sem, 1)
                pe.wait_ge(rnorm_ready.sem, rnorm_ready.at(b, 1))
                for n in range(2):
                    for t in range(TT):
                        col = 4 * n + t
                        mm = pe.matmul(PS[:, 4 + n, bass.ts(t, P)], rnorm[:, col:col + 1].to_broadcast([P, P]),
                                       C["ident"], start=True, stop=True)
                mm.then_inc(spread.sem, 1)

        @block.scalar
        def _(act):
            with act.Fori(0, NB) as b:
                act.wait_ge(done.sem, done.at(b, 0))
                act.wait_ge(projected.sem, projected.at(b, 1))
                for n in range(2):
                    act.activation(sq[:, n, :], PS[:, n, :], ACT.Square).then_inc(squared.sem, 1)
                act.activation(v_sb[:, :], PS[:, 2, :], ACT.Copy).then_inc(copied.sem, 1)
                act.activation(q_sb[:, :], PS[:, 0, :], ACT.Copy).then_inc(copied.sem, 1)
                act.wait_ge(summed.sem, summed.at(b, 1))
                act.activation(norm[:, :], PS[:, 3, 0:8], ACT.Sqrt).then_inc(norm_ready.sem, 1)

        @block.vector
        def _(dve):
            with dve.Fori(0, NB) as b:
                dve.wait_ge(projected.sem, projected.at(b, 1))
                dve.wait_ge(copied.sem, copied.at(b, 1))
                dve.wait_ge(squared.sem, squared.at(b, 2))
                dve.tensor_tensor(kv[:, :], PS[:, 1, :], v_sb[:, :], ALU.mult).then_inc(kv_ready.sem, 1)
                dve.wait_ge(norm_ready.sem, norm_ready.at(b, 1))
                dve.tensor_scalar(norm[:, :], norm[:, :], 1e-12, None, ALU.max).then_inc(clipped.sem, 1)
                dve.wait_ge(clipped.sem, clipped.at(b, 1))
                dve.reciprocal(rnorm[:, :], norm[:, :]).then_inc(rnorm_ready.sem, 1)
                dve.wait_ge(spread.sem, spread.at(b, 1))
                dve.wait_ge(kv_ready.sem, kv_ready.at(b, 1))
                dve.wait_ge(scaled_ready.sem, scaled_ready.at(b, 0))
                dve.wait_ge(done.sem, done.at(b, 0))
                dve.scalar_tensor_tensor(scaled[:, :], kv[:, :], 1.0 / T, PS[:, 5, :], ALU.mult, ALU.mult,
                                         accum_out=feat[:, :]).then_inc(feat_ready.sem, 1)
                dve.wait_ge(feat_ready.sem, feat_ready.at(b, 1))
                dve.wait_ge(copied.sem, copied.at(b, 2))
                dve.scalar_tensor_tensor(scaled[:, :], q_sb[:, :], feat[:, 0:1], PS[:, 4, :], ALU.mult, ALU.mult)\
                   .then_inc(scaled_ready.sem, 1)
                dve.wait_ge(scaled_ready.sem, scaled_ready.at(b, 1))
                dve.tensor_tensor(Y[:, b, :], scaled[:, :], X[:, b, :], ALU.add).then_inc(done.sem, 1)


def local_ffn(nc, tag, X, Y, PS, C, W):
    HID_T = 3
    HALVES = 2 * TT
    LANES = 2
    with ExitStack() as ctx:
        s = Stage(nc, ctx)

        def bufs(name, shape):
            return [s.sb(f"{tag}_{name}{g}", shape) for g in range(LANES)]

        def sigs(name, per):
            return [s.sig(f"{tag}_{name}{g}", per) for g in range(LANES)]

        z = bufs("z", [P, T])
        h = bufs("h", [P, T])
        v = bufs("v", [P, TT, T])
        qk = bufs("qk", [P, 8, T])
        norm = bufs("norm", [P, TT * 16])
        rnorm = bufs("rnorm", [P, TT * 16])
        rnorm8 = bufs("rnorm8", [P, TT * 16])
        rnorm_t = bufs("rnorm_t", [16, T])
        mx = bufs("mx", [P, 4])
        nmx = bufs("nmx", [P, 4])
        tot = bufs("tot", [P, 2, 4])
        rtot = bufs("rtot", [P, 4])
        probs = bufs("probs", [P, 8, 2 * P])
        probs_t = bufs("probs_t", [P, 4, 2, P])
        o = bufs("o", [P, 4, T])
        std = bufs("std", [P, TT])
        rstd = bufs("rstd", [P, TT])
        hn = bufs("hn", [P, T])
        rot = [o[g][:, 0:2, :] for g in range(LANES)]
        sq = [o[g][:, 2:4, :] for g in range(LANES)]
        gated = [qk[g][:, 0:HID_T, :] for g in range(LANES)]
        gelu = [qk[g][:, 4:4 + HID_T, :] for g in range(LANES)]
        set_up = s.sem(f"{tag}_set_up")
        z_ready = sigs("z_ready", 1)
        shifted = sigs("shifted", 2)
        v_ready = sigs("v_ready", TT)
        v_kept = sigs("v_kept", TT)
        proj_ready = sigs("proj_ready", 8)
        squared = sigs("squared", 8)
        sq_used = sigs("sq_used", 8)
        rot1 = sigs("rot1", 8)
        rot2 = sigs("rot2", 8)
        rotated = sigs("rotated", 8)
        norm_ready = sigs("norm_ready", 1)
        clipped = sigs("clipped", 1)
        rnorm_ready = sigs("rnorm_ready", 1)
        rnorm8_ready = sigs("rnorm8_ready", 1)
        rnorm_turned = sigs("rnorm_turned", 1)
        rnorm_t_kept = sigs("rnorm_t_kept", 1)
        rnorm_spread = sigs("rnorm_spread", 4)
        k_ready = sigs("k_ready", 4)
        scored = sigs("scored", HALVES)
        maxed = sigs("maxed", HALVES)
        negated = sigs("negated", HALVES)
        exped = sigs("exped", HALVES)
        inverted = sigs("inverted", HALVES)
        probs_ready = sigs("probs_ready", HALVES)
        turned = sigs("turned", HALVES)
        turned_kept = sigs("turned_kept", HALVES)
        pv_done = sigs("pv_done", HALVES)
        o_kept = sigs("o_kept", HALVES)
        attn_out = sigs("attn_out", 1)
        z_mid = sigs("z_mid", 1)
        shifted_mid = sigs("shifted_mid", 2)
        mean_ready = sigs("mean_ready", 1)
        centred = sigs("centred", 1)
        sq_mid = sigs("sq_mid", 1)
        var_ready = sigs("var_ready", 1)
        eps_added = sigs("eps_added", 1)
        std_ready = sigs("std_ready", 1)
        rstd_ready = sigs("rstd_ready", 1)
        rstd_spread = sigs("rstd_spread", 1)
        scaled = sigs("scaled", 1)
        hn_ready = sigs("hn_ready", 1)
        hidden = sigs("hidden", HID_T)
        gelu_ready = sigs("gelu_ready", HID_T)
        gated_ready = sigs("gated_ready", HID_T)
        ffn_out = sigs("ffn_out", 1)
        done = sigs("done", 1)
        summed = sigs("summed", 1)
        block = ctx.enter_context(nc.Block())

        def w(l, name):
            return W[f"{name}{l}"]

        def head(n, sl):
            return 4 * (n % 2) + 2 * (sl % 2) + sl // 2

        def keys(tt):
            return (slice(0, P), slice(P, 2 * P)) if tt == 0 else (slice(tt * P - 64, (tt + 1) * P), slice(64, 2 * P))

        def probs_of(g, n):
            return probs[g][:, 4 * (n % 2):4 * (n % 2) + 4, :]

        @block.sync
        def _(sp):
            C["load"](sp, tag)

        @block.gpsimd
        def _(pool):
            for g in range(LANES):
                pool.memset(h[g][64:P, 0:1], 0.0).then_inc(set_up, 1)
                pool.wait_ge(set_up, 2 * g + 1)
                pool.memset(probs[g][:, :, 0:64], 0.0).then_inc(set_up, 1)
                pool.wait_ge(set_up, 2 * g + 2)
            with pool.Fori(0, NB // LANES) as c:
                for l in range(2):
                    t = c * 2 + l
                    for i in range(8):
                        for g in range(LANES):
                            pool.wait_ge(rot1[g].sem, rot1[g].at(t, i + 1))
                            pool.wait_ge(rot2[g].sem, rot2[g].at(t, i + 1))
                            pool.tensor_tensor(qk[g][:, i, :], rot[g][:, 0, :], rot[g][:, 1, :], ALU.add)\
                                .then_inc(rotated[g].sem, 1)

        @block.tensor
        def _(pe):
            C["weights"](pe, tag)

            def bank(g, n):
                return PS[:, 4 * g + n, :]

            def norm_sums(g, t, i):
                pe.wait_ge(squared[g].sem, squared[g].at(t, i + 1))
                for tt in range(TT):
                    mm = pe.matmul(bank(g, 2)[:, bass.ts(tt, 16)], sq[g][:, i % 2, bass.ts(tt, P)],
                                   W["head_sum"][:, bass.ts(i, 16)], start=(i == 0 and tt == 0), stop=(i == 7 and tt == TT - 1))
                mm.then_inc(sq_used[g].sem, 1)

            def scores(g, t, n):
                tt = n // 2
                js, cols = keys(tt)
                if n == 0:
                    pe.wait_ge(k_ready[g].sem, k_ready[g].at(t, 4))
                    pe.wait_ge(rotated[g].sem, rotated[g].at(t, 8))
                else:
                    pe.wait_ge(exped[g].sem, exped[g].at(t, n))
                for sl in range(4):
                    hd = head(n, sl)
                    strip = slice(64 * (hd % 2), 64 * (hd % 2) + 64)
                    out = bank(g, sl // 2)[:, (sl % 2) * 256:(sl % 2) * 256 + 256][:, cols]
                    pe.matmul(out, qk[g][strip, hd // 2, bass.ts(tt, P)], qk[g][strip, 4 + hd // 2, js],
                              start=True, stop=False)
                    mm = pe.matmul(out, C["ident_bf"], W["mask"][:, cols], start=False, stop=True)
                mm.then_inc(scored[g].sem, 1)

            def turn(g, t, n):
                pe.wait_ge(probs_ready[g].sem, probs_ready[g].at(t, n + 1))
                if n >= 1:
                    pe.wait_ge(o_kept[g].sem, o_kept[g].at(t, n))
                for hd in range(4):
                    for kt in range(0 if n >= 2 else 1, 2):
                        at = (hd * 2 + kt) * P
                        mm = pe.transpose(bank(g, 2 + at // T)[:, at % T:at % T + P],
                                          probs_of(g, n)[:, hd, bass.ts(kt, P)], C["ident"])
                mm.then_inc(turned[g].sem, 1)

            def pv(g, t, n):
                tt = n // 2
                pe.wait_ge(turned_kept[g].sem, turned_kept[g].at(t, n + 1))
                kts = range(0 if tt else 1, 2)
                for sl in range(4):
                    hd = head(n, sl)
                    rows = slice(64 * (hd % 2), 64 * (hd % 2) + 64)
                    for kt in kts:
                        mm = pe.matmul(PS[rows, 4 * g + 2, bass.ts(hd // 2 % 2, P)],
                                       v[g][:, tt - 1 + kt, bass.ts(hd, 64)], probs_t[g][:, sl, kt, :],
                                       start=(kt == kts[0]), stop=(kt == 1))
                mm.then_inc(pv_done[g].sem, 1)

            def ffn_down(g, t, l, i):
                pe.wait_ge(gated_ready[g].sem, gated_ready[g].at(t, i + 1))
                mm = pe.matmul(bank(g, 2), w(l, "w2")[:, bass.ts(i, P)], gated[g][:, i, :],
                               start=(i == 0), stop=(i == HID_T - 1))
                if i == HID_T - 1:
                    mm.then_inc(ffn_out[g].sem, 1)

            lanes = range(LANES)
            with pe.Fori(0, NB // LANES) as c:
                for l in range(2):
                    t = c * 2 + l
                    for st in range(TT):
                        for g in lanes:
                            if st == 0:
                                pe.wait_ge(shifted[g].sem, shifted[g].at(t, 2))
                            if st >= 2:
                                pe.wait_ge(v_kept[g].sem, v_kept[g].at(t, st - 1))
                            pe.matmul(bank(g, 2 + st % 2), h[g][:, bass.ts(st, P)], w(l, "v"), start=True, stop=True)\
                              .then_inc(v_ready[g].sem, 1)
                    for i in range(8):
                        for g in lanes:
                            if i >= 1:
                                pe.wait_ge(rot2[g].sem, rot2[g].at(t, i))
                                pe.wait_ge(squared[g].sem, squared[g].at(t, i))
                            pe.matmul(bank(g, 0), w(l, "qk")[:, bass.ts(i, P)], h[g][:, :], start=True, stop=True)
                            pe.matmul(bank(g, 1), w(l, "qk_sw")[:, bass.ts(i, P)], h[g][:, :], start=True, stop=True)\
                              .then_inc(proj_ready[g].sem, 1)
                        for g in lanes:
                            if i == 1:
                                pe.wait_ge(v_kept[g].sem, v_kept[g].at(t, TT))
                            if i >= 1:
                                norm_sums(g, t, i - 1)
                    for g in lanes:
                        norm_sums(g, t, 7)
                    for g in lanes:
                        pe.wait_ge(rnorm_ready[g].sem, rnorm_ready[g].at(t, 1))
                        for tt in range(TT):
                            mm = pe.transpose(bank(g, 3)[0:16, bass.ts(tt, P)], rnorm[g][:, bass.ts(tt, 16)], C["ident"])
                        mm.then_inc(rnorm_turned[g].sem, 1)
                    for i in range(4):
                        for g in lanes:
                            if i == 0:
                                pe.wait_ge(rnorm_t_kept[g].sem, rnorm_t_kept[g].at(t, 1))
                                pe.wait_ge(rot2[g].sem, rot2[g].at(t, 8))
                            if i >= 2:
                                pe.wait_ge(k_ready[g].sem, k_ready[g].at(t, i - 1))
                            pe.matmul(bank(g, i % 2), W["head_bc"][:, bass.ts(4 + i, P)], rnorm_t[g][:, :],
                                      start=True, stop=True).then_inc(rnorm_spread[g].sem, 1)
                    for g in lanes:
                        scores(g, t, 0)
                    for n in range(HALVES):
                        if n + 1 < HALVES:
                            for g in lanes:
                                scores(g, t, n + 1)
                        for g in lanes:
                            turn(g, t, n)
                        for g in lanes:
                            pv(g, t, n)
                    for g in lanes:
                        pe.wait_ge(o_kept[g].sem, o_kept[g].at(t, HALVES))
                        for i in range(4):
                            mm = pe.matmul(bank(g, 0), w(l, "wo")[:, bass.ts(i, P)], o[g][:, i, :],
                                           start=(i == 0), stop=(i == 3))
                        mm.then_inc(attn_out[g].sem, 1)
                    for g in lanes:
                        pe.wait_ge(shifted_mid[g].sem, shifted_mid[g].at(t, 2))
                        pe.matmul(bank(g, 1), C["inv_d"], h[g][:, :], start=True, stop=True).then_inc(mean_ready[g].sem, 1)
                    for g in lanes:
                        pe.wait_ge(sq_mid[g].sem, sq_mid[g].at(t, 1))
                        for tt in range(TT):
                            mm = pe.matmul(bank(g, 2)[:, tt:tt + 1], sq[g][:, 0, bass.ts(tt, P)], C["inv_d"][:, 0:1],
                                           start=True, stop=True)
                        mm.then_inc(var_ready[g].sem, 1)
                    for g in lanes:
                        pe.wait_ge(rstd_ready[g].sem, rstd_ready[g].at(t, 1))
                        for tt in range(TT):
                            mm = pe.matmul(bank(g, 3)[:, bass.ts(tt, P)], rstd[g][:, tt:tt + 1].to_broadcast([P, P]),
                                           C["ident"], start=True, stop=True)
                        mm.then_inc(rstd_spread[g].sem, 1)
                    for i in range(HID_T):
                        for g in lanes:
                            if i == 0:
                                pe.wait_ge(hn_ready[g].sem, hn_ready[g].at(t, 1))
                            else:
                                pe.wait_ge(gated_ready[g].sem, gated_ready[g].at(t, i))
                            pe.matmul(bank(g, 0), w(l, "w1a")[:, bass.ts(i, P)], hn[g][:, :], start=True, stop=True)
                            pe.matmul(bank(g, 1), w(l, "w1g")[:, bass.ts(i, P)], hn[g][:, :],
                                      start=True, stop=True).then_inc(hidden[g].sem, 1)
                        if i >= 1:
                            for g in lanes:
                                ffn_down(g, t, l, i - 1)
                    for g in lanes:
                        ffn_down(g, t, l, HID_T - 1)

        @block.scalar
        def _(act):
            C["weights"](act, tag)

            def bank(g, n):
                return PS[:, 4 * g + n, :]

            def exps(g, t, n):
                tt = n // 2
                js, cols = keys(tt)
                act.wait_ge(negated[g].sem, negated[g].at(t, n + 1))
                if n >= 2:
                    act.wait_ge(turned[g].sem, turned[g].at(t, n - 1))
                for sl in range(4):
                    hd = tt * 16 + head(n, sl)
                    a = act.activation(probs_of(g, n)[:, sl, cols],
                                       bank(g, sl // 2)[:, (sl % 2) * 256:(sl % 2) * 256 + 256][:, cols], ACT.Exp,
                                       bias=nmx[g][:, sl:sl + 1], scale=rnorm8[g][:, hd:hd + 1],
                                       accum_out=tot[g][:, n % 2, sl:sl + 1])
                a.then_inc(exped[g].sem, 1)

            def keep_turned(g, t, n):
                act.wait_ge(turned[g].sem, turned[g].at(t, n + 1))
                if n >= 1:
                    act.wait_ge(pv_done[g].sem, pv_done[g].at(t, n))
                lo = 0 if n >= 2 else 1
                act.activation(probs_t[g][:, :, lo:2, :],
                               PS[:, 4 * g + 2:4 * g + 4, :].rearrange("p a (h k i) -> p (a h) k i", k=2, i=P)[:, :, lo:2, :],
                               ACT.Copy).then_inc(turned_kept[g].sem, 1)

            lanes = range(LANES)
            with act.Fori(0, NB // LANES) as c:
                for l in range(2):
                    t = c * 2 + l
                    for st in range(TT):
                        for g in lanes:
                            act.wait_ge(v_ready[g].sem, v_ready[g].at(t, st + 1))
                            act.activation(v[g][:, st, :], bank(g, 2 + st % 2), ACT.Copy).then_inc(v_kept[g].sem, 1)
                    for i in range(8):
                        for g in lanes:
                            act.wait_ge(proj_ready[g].sem, proj_ready[g].at(t, i + 1))
                            if i >= 2:
                                act.wait_ge(sq_used[g].sem, sq_used[g].at(t, i - 1))
                            act.activation(sq[g][:, i % 2, :], bank(g, 0), ACT.Square).then_inc(squared[g].sem, 1)
                    for g in lanes:
                        act.wait_ge(sq_used[g].sem, sq_used[g].at(t, 8))
                        act.activation(norm[g][:, :], bank(g, 2)[:, 0:TT * 16], ACT.Sqrt).then_inc(norm_ready[g].sem, 1)
                    for g in lanes:
                        act.wait_ge(rnorm_turned[g].sem, rnorm_turned[g].at(t, 1))
                        act.activation(rnorm_t[g][:, :], bank(g, 3)[0:16, :], ACT.Copy).then_inc(rnorm_t_kept[g].sem, 1)
                    for g in lanes:
                        exps(g, t, 0)
                    for n in range(HALVES):
                        for g in lanes:
                            if n + 1 < HALVES:
                                exps(g, t, n + 1)
                            keep_turned(g, t, n)
                    for g in lanes:
                        act.wait_ge(centred[g].sem, centred[g].at(t, 1))
                        act.activation(sq[g][:, 0, :], hn[g][:, :], ACT.Square).then_inc(sq_mid[g].sem, 1)
                    for g in lanes:
                        act.wait_ge(eps_added[g].sem, eps_added[g].at(t, 1))
                        act.activation(std[g][:, :], std[g][:, :], ACT.Sqrt).then_inc(std_ready[g].sem, 1)
                    for i in range(HID_T):
                        for g in lanes:
                            act.wait_ge(hidden[g].sem, hidden[g].at(t, i + 1))
                            act.activation(gelu[g][:, i, :], bank(g, 1), ACT.Gelu,
                                           bias=w(l, "b1g")[:, i:i + 1]).then_inc(gelu_ready[g].sem, 1)

        @block.vector
        def _(dve):
            C["weights"](dve, tag)
            dve.wait_ge(set_up, 2 * LANES)
            cos, sin = W["cos"], W["sin"]

            def bank(g, n):
                return PS[:, 4 * g + n, :]

            def shift(g, sig):
                dve.tensor_copy(h[g][0:64, :], z[g][0:64, :]).then_inc(sig[g].sem, 1)
                dve.tensor_copy(h[g][64:P, 1:T], z[g][64:P, 0:T - 1]).then_inc(sig[g].sem, 1)

            def maxima(g, t, n):
                tt = n // 2
                js, cols = keys(tt)
                dve.wait_ge(scored[g].sem, scored[g].at(t, n + 1))
                src = PS[:, 4 * g:4 * g + 2, :].rearrange("p a (h j) -> p (a h) j", j=256)[:, :, cols]
                dve.tensor_reduce(mx[g][:, :], src, AX, ALU.max).then_inc(maxed[g].sem, 1)
                dve.wait_ge(maxed[g].sem, maxed[g].at(t, n + 1))
                rn = rnorm8[g][:, tt * 16 + 4 * (n % 2):tt * 16 + 4 * (n % 2) + 4].rearrange("p (y x) -> p x y", x=2)
                dve.scalar_tensor_tensor(nmx[g][:, :].rearrange("p (x y) -> p x y", x=2),
                                         mx[g][:, :].rearrange("p (x y) -> p x y", x=2), -1.0, rn,
                                         ALU.mult, ALU.mult).then_inc(negated[g].sem, 1)

            def normalise(g, t, n):
                js, cols = keys(n // 2)
                dve.wait_ge(exped[g].sem, exped[g].at(t, n + 1))
                dve.reciprocal(rtot[g][:, :], tot[g][:, n % 2, :]).then_inc(inverted[g].sem, 1)
                dve.wait_ge(inverted[g].sem, inverted[g].at(t, n + 1))
                pr = probs_of(g, n)[:, :, cols]
                dve.tensor_tensor(pr, pr, rtot[g][:, :].rearrange("p (h o) -> p h o", o=1)
                                  .to_broadcast([P, 4, cols.stop - cols.start]), ALU.mult)\
                   .then_inc(probs_ready[g].sem, 1)

            def keep_o(g, t, n):
                dve.wait_ge(pv_done[g].sem, pv_done[g].at(t, n + 1))
                dve.tensor_copy(o[g][:, 2 * (n % 2):2 * (n % 2) + 2, bass.ts(n // 2, P)],
                                bank(g, 2)[:, 0:2 * P].rearrange("p (i q) -> p i q", i=2)).then_inc(o_kept[g].sem, 1)

            lanes = range(LANES)
            with dve.Fori(0, NB // LANES) as c:
                for l in range(2):
                    t = c * 2 + l
                    for g in lanes:
                        if l == 0:
                            dve.tensor_copy(z[g][:, :], X[:, c * 2 + g, :]).then_inc(z_ready[g].sem, 2)
                            dve.wait_ge(z_ready[g].sem, z_ready[g].at(c * 2, 2))
                        else:
                            dve.wait_ge(done[g].sem, done[g].at(t, 0))
                        shift(g, shifted)
                    for i in range(8):
                        for g in lanes:
                            dve.wait_ge(proj_ready[g].sem, proj_ready[g].at(t, i + 1))
                            dve.wait_ge(squared[g].sem, squared[g].at(t, i + 1))
                            if i >= 1:
                                dve.wait_ge(rotated[g].sem, rotated[g].at(t, i))
                            qs = w(l, "q_scale") if i < 4 else w(l, "k_scale")
                            tab = slice(0, T) if i < 4 else slice(T, 2 * T)
                            dve.scalar_tensor_tensor(rot[g][:, 0, :], bank(g, 0), qs[:, 0:1], cos[:, tab],
                                                     ALU.mult, ALU.mult).then_inc(rot1[g].sem, 1)
                            dve.scalar_tensor_tensor(rot[g][:, 1, :], bank(g, 1), qs[:, 1:2], sin[:, tab],
                                                     ALU.mult, ALU.mult).then_inc(rot2[g].sem, 1)
                    for g in lanes:
                        dve.wait_ge(norm_ready[g].sem, norm_ready[g].at(t, 1))
                        dve.tensor_scalar(norm[g][:, :], norm[g][:, :], 1e-12, None, ALU.max).then_inc(clipped[g].sem, 1)
                        dve.wait_ge(clipped[g].sem, clipped[g].at(t, 1))
                        dve.reciprocal(rnorm[g][:, :], norm[g][:, :]).then_inc(rnorm_ready[g].sem, 1)
                        dve.wait_ge(rnorm_ready[g].sem, rnorm_ready[g].at(t, 1))
                        dve.tensor_scalar(rnorm8[g][:, :], rnorm[g][:, :], 8.0, None, ALU.mult)\
                           .then_inc(rnorm8_ready[g].sem, 1)
                    for i in range(4):
                        for g in lanes:
                            if i == 0:
                                dve.wait_ge(rotated[g].sem, rotated[g].at(t, 8))
                            dve.wait_ge(rnorm_spread[g].sem, rnorm_spread[g].at(t, i + 1))
                            dve.tensor_tensor(qk[g][:, 4 + i, :], qk[g][:, 4 + i, :], bank(g, i % 2), ALU.mult)\
                               .then_inc(k_ready[g].sem, 1)
                    for g in lanes:
                        dve.wait_ge(rnorm8_ready[g].sem, rnorm8_ready[g].at(t, 1))
                        maxima(g, t, 0)
                    for g in lanes:
                        normalise(g, t, 0)
                    for n in range(HALVES):
                        if n + 1 < HALVES:
                            for g in lanes:
                                maxima(g, t, n + 1)
                            for g in lanes:
                                normalise(g, t, n + 1)
                        for g in lanes:
                            keep_o(g, t, n)
                    for g in lanes:
                        dve.wait_ge(attn_out[g].sem, attn_out[g].at(t, 1))
                        dve.tensor_tensor(z[g][:, :], z[g][:, :], bank(g, 0), ALU.add).then_inc(z_mid[g].sem, 1)
                        dve.wait_ge(z_mid[g].sem, z_mid[g].at(t, 1))
                        shift(g, shifted_mid)
                    for g in lanes:
                        dve.wait_ge(mean_ready[g].sem, mean_ready[g].at(t, 1))
                        dve.wait_ge(shifted_mid[g].sem, shifted_mid[g].at(t, 2))
                        dve.tensor_tensor(hn[g][:, :], h[g][:, :], bank(g, 1), ALU.subtract).then_inc(centred[g].sem, 1)
                    for g in lanes:
                        dve.wait_ge(var_ready[g].sem, var_ready[g].at(t, 1))
                        dve.tensor_scalar(std[g][:, :], bank(g, 2)[:, 0:TT], 1e-5, None, ALU.add)\
                           .then_inc(eps_added[g].sem, 1)
                    for g in lanes:
                        dve.wait_ge(std_ready[g].sem, std_ready[g].at(t, 1))
                        dve.reciprocal(rstd[g][:, :], std[g][:, :]).then_inc(rstd_ready[g].sem, 1)
                    for g in lanes:
                        dve.wait_ge(rstd_spread[g].sem, rstd_spread[g].at(t, 1))
                        dve.wait_ge(sq_mid[g].sem, sq_mid[g].at(t, 1))
                        dve.scalar_tensor_tensor(hn[g][:, :], hn[g][:, :], w(l, "ln_g"), bank(g, 3), ALU.mult, ALU.mult)\
                           .then_inc(scaled[g].sem, 1)
                        dve.wait_ge(scaled[g].sem, scaled[g].at(t, 1))
                        dve.tensor_scalar(hn[g][:, :], hn[g][:, :], w(l, "ln_b"), None, ALU.add)\
                           .then_inc(hn_ready[g].sem, 1)
                    for i in range(HID_T):
                        for g in lanes:
                            dve.wait_ge(gelu_ready[g].sem, gelu_ready[g].at(t, i + 1))
                            dve.scalar_tensor_tensor(gated[g][:, i, :], bank(g, 0), w(l, "b1a")[:, i:i + 1],
                                                     gelu[g][:, i, :], ALU.add, ALU.mult).then_inc(gated_ready[g].sem, 1)
                    for g in lanes:
                        dve.wait_ge(ffn_out[g].sem, ffn_out[g].at(t, 1))
                        dve.scalar_tensor_tensor(z[g][:, :], bank(g, 2), w(l, "b2"), z[g][:, :], ALU.add, ALU.add)\
                           .then_inc(done[g].sem, 1)
                    if l == 1:
                        for g in lanes:
                            dve.wait_ge(done[g].sem, done[g].at(t, 1))
                            dve.tensor_tensor(Y[:, c * 2 + g, :], X[:, c * 2 + g, :], z[g][:, :], ALU.add)\
                               .then_inc(summed[g].sem, 1)
                            dve.wait_ge(summed[g].sem, summed[g].at(c, 1))




class Pack:

    def __init__(self):
        self.items, self.cols = [], 0

    def add(self, name, array):
        self.items.append((name, array, self.cols))
        self.cols += array.shape[1]

    def data(self, dtype):
        out = np.zeros((P, self.cols), dtype)
        for _, a, at in self.items:
            out[:a.shape[0], at:at + a.shape[1]] = a
        return out


def moe_sel(sizes, dtype):
    units = np.concatenate([np.full(n, e) for e, n in enumerate(sizes)])
    nt = -(-len(units) // P)
    sel = np.zeros((96, nt * P), dtype)
    for part in range(3):
        sel[32 * part + units, np.arange(len(units))] = 1
    return sel


def tiles_of(w, nt):
    out = np.zeros((nt * P, w.shape[1]), w.dtype)
    out[:w.shape[0]] = w
    return out.reshape(nt, P, w.shape[1]).transpose(1, 0, 2).reshape(P, -1)


def padded(w, cols):
    out = np.zeros((w.shape[0], cols), w.dtype)
    out[:, :w.shape[1]] = w
    return out


def lay_out(a, bf):
    fs, bs = {}, {}

    def stage(name):
        fs[name], bs[name] = Pack(), Pack()
        return fs[name], bs[name]

    f, h = stage("const")
    f.add("inv_d", np.full((P, P), 1.0 / P, np.float32))
    f.add("ident", np.eye(P, dtype=np.float32))
    h.add("ident_bf", np.eye(P).astype(bf))

    f, h = stage("m0")
    E, D, F = a["L0_ffn_Wg"].shape
    nt = (E * F + 128) // P
    f.add("router", a["L0_ffn_Wr"])
    f.add("bias", np.tile(a["L0_ffn_expert_bias"], (P, 1)))
    f.add("gate", np.concatenate([a["L0_ffn_Wg"].transpose(1, 0, 2).reshape(D, -1), a["L0_ffn_Sg"]], 1))
    f.add("up", np.concatenate([a["L0_ffn_Wu"].transpose(1, 0, 2).reshape(D, -1), a["L0_ffn_Su"]], 1))
    f.add("down", tiles_of(np.concatenate([a["L0_ffn_Wd"].reshape(-1, D), a["L0_ffn_Sd"]], 0), nt))
    h.add("sel", moe_sel([F] * E + [128], bf))

    f, h = stage("m1")
    gu = a["L1_ffn_experts_gate_up"]
    E, I = gu.shape[0], gu.shape[1] // 2
    SI = a["L1_ffn_shared_gate_w"].shape[0]
    nt = -(-(E * I + SI) // P)
    f.add("router", np.concatenate([a["L1_ffn_gate_w"], a["L1_ffn_shared_expert_gate_w"]], 0).T)
    f.add("gate", padded(np.concatenate([gu[:, :I].reshape(-1, P), a["L1_ffn_shared_gate_w"]], 0).T, nt * P))
    f.add("up", padded(np.concatenate([gu[:, I:].reshape(-1, P), a["L1_ffn_shared_up_w"]], 0).T, nt * P))
    f.add("down", tiles_of(np.concatenate([a["L1_ffn_experts_down"].transpose(0, 2, 1).reshape(-1, P),
                                           a["L1_ffn_shared_down_w"].T], 0), nt))
    h.add("sel", moe_sel([I] * E + [SI], bf))

    f, h = stage("m2")
    E, D, I = a["L2_ffn_w1"].shape
    nt = E * I // P
    f.add("router", a["L2_ffn_gate_w"].T)
    f.add("bias", np.tile(a["L2_ffn_e_bias"], (P, 1)))
    f.add("gate", a["L2_ffn_w1"].transpose(1, 0, 2).reshape(D, -1))
    f.add("up", a["L2_ffn_w3"].transpose(1, 0, 2).reshape(D, -1))
    f.add("down", tiles_of(a["L2_ffn_w2"].reshape(-1, D), nt))
    h.add("sel", moe_sel([I] * E, bf))
    more_layout(a, bf, stage)
    return fs, bs


def strips(heads, D, SW, bf):
    out = np.zeros((P, 2, 3, len(heads), P), bf)
    for g, hs in enumerate(heads):
        for j, h in enumerate(hs):
            for term, parts in enumerate(TERMS):
                for e in range(D):
                    for n in range(2):
                        out[h * D + e, n, parts[n], g, j * SW + term * D + e] = 1
    return out.reshape(P, -1)


def attn_common(f, h, D, SW, heads, bf):
    ones, strip = np.zeros((2, P, P // SW), np.float32)
    for j in range(P // SW):
        ones[j * SW + 6 * D:j * SW + 6 * D + 3, j] = 1
        strip[j * SW:(j + 1) * SW, j] = 1
    f.add("ones_rows", ones)
    f.add("strip_rows", strip)
    h.add("strips", strips(heads, D, SW, bf))
    pick_o, pick_sum = np.zeros((P, 32), np.float32), np.zeros((P, 32), np.float32)
    for j in range(4):
        for e in range(8):
            pick_o[32 * j + e, 8 * j + e] = 1
            pick_sum[32 * j + 8, 8 * j + e] = 1
    f.add("pick_o", pick_o)
    f.add("pick_sum", pick_sum)


def more_layout(a, bf, stage):
    f, h = stage("a1")
    w = a["L1_attn_w_qkv"]
    f.add("q", w[:, :P])
    f.add("k", w[:, P:2 * P])
    f.add("v", w[:, 2 * P:])
    f.add("out", a["L1_attn_w_out"])
    f.add("b_out", a["L1_attn_b_out"][:, None])
    attn_common(f, h, 8, 64, [[2 * g, 2 * g + 1] for g in range(8)], bf)
    mask = np.where(np.arange(P)[None, :] > np.arange(P)[:, None], -1e10, 0.0)
    h.add("mask", mask.astype(bf))
    h.add("mask_t", np.ascontiguousarray(mask.T).astype(bf))

    f, h = stage("a3")
    f.add("q", a["L3_attn_Wq"])
    f.add("k", a["L3_attn_Wk"])
    swap = np.arange(P) ^ 1
    f.add("q_sw", a["L3_attn_Wq"][:, swap])
    f.add("k_sw", a["L3_attn_Wk"][:, swap])
    f.add("v", a["L3_attn_Wv"])
    f.add("out", a["L3_attn_Wo"])
    attn_common(f, h, 4, 32, [[2 * (4 * (g % 4) + j) + g // 4 for j in range(4)] for g in range(8)], bf)
    pos = np.arange(T, dtype=np.float32)[:, None]
    freq = np.float32(1.0) / np.float32(0.0001) ** (np.float32(2.0) * np.arange(2, dtype=np.float32) / np.float32(4))
    ang = (pos * freq.astype(np.float32)).astype(np.float32)
    pair = (np.arange(P) % 4) // 2
    cos = np.cos(ang).astype(np.float32).T[pair]
    sin = np.sin(ang).astype(np.float32).T[pair] * np.where(np.arange(P) % 2 == 0, -1, 1)[:, None]
    f.add("cos", np.concatenate([cos * 0.5, cos], 1).astype(np.float32))
    f.add("sin", np.concatenate([sin * 0.5, sin], 1).astype(np.float32))
    f.add("lam_q", np.tile(np.concatenate([a["L3_attn_lambda_q1"], a["L3_attn_lambda_q2"]]), (P, 1)))
    f.add("lam_k", np.tile(np.concatenate([a["L3_attn_lambda_k1"], a["L3_attn_lambda_k2"]]), (P, 1)))
    f.add("subln", np.tile(a["L3_attn_subln_g"], 16)[:, None])
    f.add("eps", np.full((P, 1), 1e-5, np.float32))
    mean8 = np.kron(np.eye(16, dtype=np.float32), np.full((8, 8), 1 / 8, np.float32))
    f.add("mean8", mean8)
    rest_layout(a, bf, stage)


def rest_layout(a, bf, stage):
    f, h = stage("a2")
    for name, w in (("q", "W_q"), ("k", "W_k"), ("v", "W_v")):
        f.add(name, a[f"L2_attn_{w}"].T)
    f.add("ones", np.ones((P, 1), np.float32))

    f, h = stage("f3")
    wqkv = a["L3_ffn_wqkv"]
    swap = np.arange(512) // 64 * 64 + (np.arange(512) % 64 + 32) % 64
    swap64 = (np.arange(64) + 32) % 64
    for l in range(2):
        q, k, v = wqkv[l][:, :512], wqkv[l][:, 512:1024], wqkv[l][:, 1024:]
        f.add(f"qk{l}", np.concatenate([q, k], 1))
        f.add(f"qk_sw{l}", np.concatenate([q[:, swap], k[:, swap]], 1))
        f.add(f"v{l}", v)
        for name, key in (("q_scale", "L3_ffn_q_scale"), ("k_scale", "L3_ffn_k_scale")):
            sc = a[key][l]
            f.add(f"{name}{l}", np.stack([np.tile(sc, 2), np.tile(sc[swap64], 2)], 1))
        f.add(f"wo{l}", tiles_of(a["L3_ffn_wo"][l], 4))
        f.add(f"ln_g{l}", a["L3_ffn_ln_g"][l][:, None])
        f.add(f"ln_b{l}", a["L3_ffn_ln_b"][l][:, None])
        hid = a["L3_ffn_w2"].shape[1]
        w1, b1 = a["L3_ffn_w1"][l], a["L3_ffn_b1"][l][None]
        f.add(f"w1a{l}", padded(w1[:, :hid], 3 * P))
        f.add(f"w1g{l}", padded(w1[:, hid:], 3 * P))
        f.add(f"b1a{l}", padded(b1[:, :hid], 3 * P).reshape(3, P).T)
        f.add(f"b1g{l}", padded(b1[:, hid:], 3 * P).reshape(3, P).T)
        f.add(f"w2{l}", tiles_of(a["L3_ffn_w2"][l], 3))
        f.add(f"b2{l}", a["L3_ffn_b2"][l][:, None])
    head_sum, head_bc = np.zeros((P, 8, 16), np.float32), np.zeros((16, 8, P), np.float32)
    for i in range(8):
        for c in range(P):
            head_sum[c, i, 2 * i + c // 64] = 1
            head_bc[2 * i + c // 64, i, c] = 1
    f.add("head_sum", head_sum.reshape(P, -1))
    f.add("head_bc", head_bc.reshape(16, -1))
    half = np.arange(0, 64, 2, dtype=np.float32)
    inv = (np.float32(1.0) / np.float32(10000.0) ** (half / np.float32(64))).astype(np.float32)
    t = np.arange(T, dtype=np.float32)
    fr = (t[:, None] * inv[None]).astype(np.float32)
    base = ((half + np.float32(0.4 * 64)) / np.float32(1.4 * 64)).astype(np.float32)
    power = ((t - T // 2) / np.float32(32)).astype(np.float32)
    sc = (base[None] ** power[:, None]).astype(np.float32)
    row = np.arange(P) % 32
    sign = np.where(np.arange(P) % 64 < 32, -1, 1)[:, None].astype(np.float32)
    cos, sin, sc = np.cos(fr).T[row], np.sin(fr).T[row] * sign, sc.T[row]
    f.add("cos", np.concatenate([cos * sc, cos / sc], 1).astype(np.float32))
    f.add("sin", np.concatenate([sin * sc, sin / sc], 1).astype(np.float32))
    j = np.arange(2 * P)[None, :] - P
    i = np.arange(P)[:, None]
    h.add("mask", np.where((i < j) | (i > j + 64), -BIG, 0.0).astype(bf))
    first_layout(a, bf, stage)


def first_layout(a, bf, stage):
    f, h = stage("a0")
    f.add("disp", a["L0_attn_W_disp"])
    f.add("val", a["L0_attn_W_val"])

    def blocks(w):
        out = np.zeros((8, 16, 8, 16), np.float32)
        for i in range(8):
            out[i, :, i, :] = w
        return out.reshape(P, P)

    f.add("strain", blocks(a["L0_attn_W_strain"]))
    f.add("dmg", blocks(a["L0_attn_W_dmg"]))
    f.add("w_pos", np.tile(a["L0_attn_W_pos"], (1, 8)))
    f.add("rel", a["L0_attn_rel_pos_emb"].T)
    f.add("b_dmg", np.tile(a["L0_attn_b_dmg"], 8)[:, None])
    f.add("b_out", np.tile(a["L0_attn_b_dmg_out"], P)[:, None])
    for name, key in (("w_bond", "L0_attn_W_bond"), ("w_dmg_out", "L0_attn_W_dmg_out")):
        out = np.zeros((8, 16, 4, 4, 8), np.float32)
        for k in range(4):
            for i in range(8):
                out[i, :, k, k, i] = a[key][:, 0]
        f.add(name, out.reshape(P, P))
    f.add("c_proj", a["L0_attn_W_cproj"])
    d = (np.arange(T) // 8)[None, :]
    m = np.where(np.arange(P)[:, None] - 63 + d < 0, -BIG, 0.0).astype(np.float32)
    f.add("mask", np.concatenate([m, m], 1))


def build(nc, x_d, out_d, f_d, b_d, fs, bs, stages):
    Stage.CLEARED = []
    with ExitStack() as top:
        X = top.enter_context(nc.sbuf_tensor("X", [P, NB, T], F32))
        Y = top.enter_context(nc.sbuf_tensor("Y", [P, NB, T], F32))
        PS = top.enter_context(nc.psum_tensor("PS", [P, NB, T], F32))
        x_loaded = top.enter_context(nc.semaphore("x_loaded"))
        stored = top.enter_context(nc.semaphore("stored"))

        def load(eng, name):
            wf, wb, sem, _ = bufs[name]
            eng.dma_start(wf[:, :], f_d[name]).then_inc(sem, 16)
            if name in b_d:
                eng.dma_start(wb[:, :], b_d[name]).then_inc(sem, 16)

        def weights(eng, name):
            eng.wait_ge(bufs[name][2], 32 if name in b_d else 16)

        def hold(ctx, name):
            wf = ctx.enter_context(nc.sbuf_tensor(f"w_{name}", [P, fs[name].cols], F32))
            wb = ctx.enter_context(nc.sbuf_tensor(f"wb_{name}", [P, max(bs[name].cols, 1)], BF16))
            sem = top.enter_context(nc.semaphore(f"{name}_weights"))
            views = {k: wf[0:v.shape[0], at:at + v.shape[1]] for k, v, at in fs[name].items}
            views |= {k: wb[0:v.shape[0], at:at + v.shape[1]] for k, v, at in bs[name].items}
            bufs[name] = (wf, wb, sem, views)
            return views

        scratch = nc.dram_tensor("scratch", (TT * 16 * 2 * 64 * P,), F32, kind="Internal").ap()
        first, last = stages
        bufs = {}
        C = dict(hold(top, "const"), weights=weights, load=load)

        with ExitStack() as ctx:
            block = ctx.enter_context(nc.Block())

            @block.sync
            def _(sp):
                sp.dma_start(X[:, :, :], x_d.rearrange("p (b t) -> p b t", b=NB)).then_inc(x_loaded, 16)
                load(sp, "const")
                sp.wait_ge(x_loaded, 16)
                weights(sp, "const")

        stage_of = [
            ("a0", lambda w: attn0(nc, "a0", X, Y, PS, C, w, scratch)),
            ("m0", lambda w: moe(nc, "m0", X, Y, PS, C, w, "top_softmax", 8, 2, 5)),
            ("a1", lambda w: attn(nc, "a1", X, Y, PS, C, w, True)),
            ("m1", lambda w: moe(nc, "m1", X, Y, PS, C, w, "softmax_top", 8, 2, 14)),
            ("a2", lambda w: attn2(nc, "a2", X, Y, PS, C, w)),
            ("m2", lambda w: moe(nc, "m2", X, Y, PS, C, w, "sigmoid_top", 32, 4, 24)),
            ("a3", lambda w: attn(nc, "a3", X, Y, PS, C, w, False)),
            ("f3", lambda w: local_ffn(nc, "f3", X, Y, PS, C, w)),
        ]
        for n, (name, emit) in enumerate(stage_of):
            if first <= n <= last:
                with ExitStack() as ctx:
                    emit(hold(ctx, name))
                layernorm(nc, f"ln{n}", X, Y, PS, C)
        with ExitStack() as ctx:
            block = ctx.enter_context(nc.Block())

            @block.sync
            def _(sp):
                sp.dma_start(out_d.rearrange("p (b t) -> p b t", b=NB), X[:, :, :]).then_inc(stored, 16)
                sp.wait_ge(stored, 16)


def kernel(**inputs):
    import ml_dtypes
    import concourse.bacc as bacc
    from concourse.bass_utils import run_bass_kernel_spmd

    bf = ml_dtypes.bfloat16
    a = {k: np.asarray(v) for k, v in inputs.items()}
    x = np.ascontiguousarray(a["L0_attn_x"].reshape(NB * T, P).T)
    fs, bs = lay_out(a, bf)
    nc = bacc.Bacc("TRN2", target_bir_lowering=False, num_devices=1)
    arrays = {"x_dram": x}
    f_d, b_d = {}, {}
    x_d = nc.dram_tensor("x_dram", x.shape, F32, kind="ExternalInput").ap()
    for name in fs:
        arrays[f"{name}_f_dram"] = fs[name].data(np.float32)
        f_d[name] = nc.dram_tensor(f"{name}_f_dram", (P, fs[name].cols), F32, kind="ExternalInput").ap()
        if bs[name].cols:
            arrays[f"{name}_b_dram"] = bs[name].data(bf)
            b_d[name] = nc.dram_tensor(f"{name}_b_dram", (P, bs[name].cols), BF16, kind="ExternalInput").ap()
    out_d = nc.dram_tensor("out_dram", (P, NB * T), F32, kind="ExternalOutput").ap()
    build(nc, x_d, out_d, f_d, b_d, fs, bs, STAGES)
    r = run_bass_kernel_spmd(nc, [arrays], core_ids=[0])
    return np.ascontiguousarray(r.results[0]["out_dram"].T).reshape(NB, T, P)
```

```python
import math
from contextlib import ExitStack

import numpy as np

import concourse.bass as bass
from concourse import mybir

F32 = mybir.dt.float32
BF16 = mybir.dt.bfloat16
ALU = mybir.AluOpType
ACT = mybir.ActivationFunctionType
AX = mybir.AxisListType.X

P = 128
NB = 8
T = 512
TT = T // P
NTOK = NB * T // P
BIG = 1e30
LAMBDA_INIT = 0.8 - 0.6 * math.exp(-0.3 * 12)

STAGES = (0, 7)


class Signals:

    def __init__(self, sem, per, ahead=0):
        self.sem, self.per, self.ahead = sem, per, ahead

    def at(self, turn, n):
        return turn * self.per + n + self.ahead


class Stage:

    def __init__(self, nc, ctx):
        self.nc, self.ctx, self.sems = nc, ctx, []
        ctx.callback(self.clear)

    CLEARED = []

    def clear(self):
        for sem in Stage.CLEARED:
            self.nc.release_semaphore(sem)
        Stage.CLEARED = list(self.sems)
        for sem in self.sems:
            self.nc.gpsimd.sem_clear(sem)

    def sb(self, name, shape, dt=F32):
        return self.ctx.enter_context(self.nc.sbuf_tensor(name, shape, dt))

    def sem(self, name):
        self.sems.append(self.nc.alloc_semaphore(name))
        return self.sems[-1]

    def sig(self, name, per, ahead=0):
        return Signals(self.sem(name), per, ahead)


def layernorm(nc, tag, X, Y, PS, C, following):
    with ExitStack() as ctx:
        s = Stage(nc, ctx)
        LEAD = 4
        std = s.sb(f"{tag}_std", [P, NTOK])
        rstd = s.sb(f"{tag}_rstd", [P, NTOK])
        mean_ready = s.sem(f"{tag}_mean_ready")
        centred = s.sem(f"{tag}_centred")
        squared = s.sem(f"{tag}_squared")
        var_ready = s.sem(f"{tag}_var_ready")
        eps_added = s.sem(f"{tag}_eps_added")
        std_ready = s.sem(f"{tag}_std_ready")
        rstd_ready = s.sem(f"{tag}_rstd_ready")
        spread = s.sem(f"{tag}_spread")
        block = ctx.enter_context(nc.Block())

        @block.sync
        def _(sp):
            if following:
                C["load"](sp, following)

        @block.tensor
        def _(pe):
            def mean(b):
                pe.matmul(PS[:, b, :], C["inv_d"], Y[:, b, :], start=True, stop=True).then_inc(mean_ready, 1)

            def variance(b):
                pe.wait_ge(squared, b + 1)
                for tt in range(TT):
                    n = b * TT + tt
                    mm = pe.matmul(PS[:, 0, n:n + 1], X[:, b, bass.ts(tt, P)], C["inv_d"][:, 0:1],
                                   start=True, stop=True)
                if b == NB - 1:
                    mm.then_inc(var_ready, 1)

            for b in range(LEAD):
                mean(b)
            for b in range(LEAD, NB):
                mean(b)
                variance(b - LEAD)
            for b in range(NB - LEAD, NB):
                variance(b)
            pe.wait_ge(rstd_ready, 1)
            for n in range(NTOK):
                mm = pe.matmul(PS[:, n // TT, bass.ts(n % TT, P)], rstd[:, n:n + 1].to_broadcast([P, P]),
                               C["ident"], start=True, stop=True)
                if n % TT == TT - 1:
                    mm.then_inc(spread, 1)

        @block.vector
        def _(dve):
            with dve.Fori(0, NB) as b:
                dve.wait_ge(mean_ready, b + 1)
                dve.tensor_tensor(Y[:, b, :], Y[:, b, :], PS[:, b, :], ALU.subtract).then_inc(centred, 1)
            dve.wait_ge(var_ready, 1)
            dve.tensor_scalar(std[:, :], PS[:, 0, 0:NTOK], 1e-5, None, ALU.add).then_inc(eps_added, 1)
            dve.wait_ge(std_ready, 1)
            dve.reciprocal(rstd[:, :], std[:, :]).then_inc(rstd_ready, 1)
            with dve.Fori(0, NB) as b:
                dve.wait_ge(spread, b + 1)
                dve.tensor_tensor(X[:, b, :], Y[:, b, :], PS[:, b, :], ALU.mult)

        @block.scalar
        def _(act):
            with act.Fori(0, NB) as b:
                act.wait_ge(centred, b + 1)
                act.activation(X[:, b, :], Y[:, b, :], ACT.Square).then_inc(squared, 1)
            act.wait_ge(eps_added, 1)
            act.activation(std[:, :], std[:, :], ACT.Sqrt).then_inc(std_ready, 1)


def moe(nc, tag, X, Y, PS, C, W, kind, E, K, NT):
    EW = E + (1 if kind in ("top_softmax", "softmax_top") else 0)
    NV = E + 8 - K
    NR = W["router"].shape[1]
    SENT, PICKED = -3e38, 3e38
    with ExitStack() as ctx:
        s = Stage(nc, ctx)
        vals = s.sb(f"{tag}_vals", [P, NTOK, NV])
        top = s.sb(f"{tag}_top", [P, NTOK, 8])
        marked = s.sb(f"{tag}_marked", [P, NTOK, NV])
        score = s.sb(f"{tag}_score", [P, NTOK, NR])
        wt = s.sb(f"{tag}_wt", [P, NTOK, EW])
        tot = s.sb(f"{tag}_tot", [P, NTOK])
        rtot = s.sb(f"{tag}_rtot", [P, NTOK])
        parts = s.sb(f"{tag}_parts", [P, NTOK, 96], BF16)
        partsT = s.sb(f"{tag}_partsT", [96, NB, T], BF16)
        silu = s.sb(f"{tag}_silu", [P, 3, T])
        prod = s.sb(f"{tag}_prod", [P, T])
        hid = s.sb(f"{tag}_hid", [P, 3, T])
        logits_ready = s.sem(f"{tag}_logits_ready")
        step = s.sem(f"{tag}_router_step")
        exp_in = s.sem(f"{tag}_exp_in")
        exp_out = s.sem(f"{tag}_exp_out")
        cleared = s.sem(f"{tag}_cleared")
        parts_ready = s.sem(f"{tag}_parts_ready")
        turned = s.sem(f"{tag}_turned")
        turned_kept = s.sem(f"{tag}_turned_kept")
        gate_ready = s.sig(f"{tag}_gate_ready", NT)
        up_ready = s.sig(f"{tag}_up_ready", NT)
        silu_ready = s.sig(f"{tag}_silu_ready", NT)
        prod_ready = s.sig(f"{tag}_prod_ready", NT, ahead=1)
        hid_ready = s.sig(f"{tag}_hid_ready", NT, ahead=1)
        hid_used = s.sig(f"{tag}_hid_used", NT, ahead=1)
        out_kept = s.sig(f"{tag}_out_kept", 1, ahead=1)
        block = ctx.enter_context(nc.Block())
        LOG = PS[:, 0:2, :].rearrange("p a b -> p (a b)")[:, 0:NTOK * 32].rearrange("p (n e) -> p n e", e=32)

        @block.gpsimd
        def _(pool):
            pool.memset(parts[:, :, :], 0.0).then_inc(cleared, 1)
            pool.memset(vals[:, :, E:NV], SENT).then_inc(cleared, 1)

        @block.tensor
        def _(pe):
            pe.sem_inc(hid_used.sem, 1)
            C["weights"](pe, tag)
            for n in range(NTOK):
                mm = pe.matmul(LOG[:, n, 0:NR], X[:, n // TT, bass.ts(n % TT, P)], W["router"],
                               start=True, stop=True)
            mm.then_inc(logits_ready, 1)
            pe.wait_ge(parts_ready, 1)
            for b in range(NB):
                TP = PS[:, b, 0:T // 2].bitcast(BF16)
                for t in range(TT):
                    mm = pe.transpose(TP[0:96, bass.ts(t, P)], parts[:, b * TT + t, :], C["ident_bf"])
                mm.then_inc(turned, 1)
            pe.wait_ge(turned_kept, NB)

            def down(b, f):
                pe.wait_ge(hid_ready.sem, hid_ready.at(b, f + 1))
                if f == 0:
                    pe.wait_ge(out_kept.sem, out_kept.at(b, 0))
                pe.matmul(PS[:, 6, :], W["down"][:, bass.ts(f, P)], hid[:, f % 3, :],
                          start=(f == 0), stop=(f == NT - 1)).then_inc(hid_used.sem, 1)

            with pe.Fori(0, NB) as b:
                for f in range(NT):
                    if f >= 2:
                        pe.wait_ge(silu_ready.sem, silu_ready.at(b, f - 1))
                        pe.wait_ge(hid_ready.sem, hid_ready.at(b, f - 1))
                    else:
                        pe.wait_ge(hid_ready.sem, hid_ready.at(b, 0))
                    pe.matmul(PS[:, f % 2, :], W["gate"][:, bass.ts(f, P)], X[:, b, :],
                              start=True, stop=True).then_inc(gate_ready.sem, 1)
                    pe.matmul(PS[:, 2 + f % 2, :], W["up"][:, bass.ts(f, P)], X[:, b, :], start=True, stop=True)
                    pe.matmul(PS[:, 4 + f % 2, :], W["sel"][:, bass.ts(f, P)], partsT[:, b, :],
                              start=True, stop=True).then_inc(up_ready.sem, 1)
                    if f >= 2:
                        down(b, f - 2)
                down(b, NT - 2)
                down(b, NT - 1)

        @block.scalar
        def _(act):
            if kind == "top_softmax":
                act.wait_ge(exp_in, 1)
                act.activation(score[:, :, :], score[:, :, :], ACT.Exp).then_inc(exp_out, 1)
            elif kind == "softmax_top":
                act.wait_ge(exp_in, 1)
                act.activation(score[:, :, :], score[:, :, :], ACT.Exp).then_inc(exp_out, 1)
            else:
                act.wait_ge(logits_ready, 1)
                act.activation(score[:, 0:NTOK // 2, :], LOG[:, 0:NTOK // 2, 0:NR], ACT.Sigmoid)
                act.activation(score[:, NTOK // 2:, :], LOG[:, NTOK // 2:, 0:NR], ACT.Sigmoid).then_inc(exp_out, 1)
            with act.Fori(0, NB) as b:
                for f in range(NT):
                    act.wait_ge(gate_ready.sem, gate_ready.at(b, f + 1))
                    if f >= 3:
                        act.wait_ge(prod_ready.sem, prod_ready.at(b, f - 2))
                    else:
                        act.wait_ge(prod_ready.sem, prod_ready.at(b, 0))
                    act.activation(silu[:, f % 3, :], PS[:, f % 2, :], ACT.Silu).then_inc(silu_ready.sem, 1)

        @block.vector
        def _(dve):
            dve.sem_inc(prod_ready.sem, 1)
            dve.sem_inc(hid_ready.sem, 1)
            dve.sem_inc(out_kept.sem, 1)
            chain = [0]

            def then(ins):
                chain[0] += 1
                ins.then_inc(step, 1)
                dve.wait_ge(step, chain[0])

            def over(a, n):
                return a.rearrange("p (n o) -> p n o", o=1).to_broadcast([P, NTOK, n])

            C["weights"](dve, tag)
            dve.wait_ge(logits_ready, 1)
            if kind == "top_softmax":
                bias = W["bias"].rearrange("p (o e) -> p o e", o=1).to_broadcast([P, NTOK, E])
                dve.wait_ge(cleared, 2)
                then(dve.tensor_tensor(vals[:, :, 0:E], LOG[:, :, 0:E], bias, ALU.add))
                pick_from = vals
            elif kind == "softmax_top":
                then(dve.tensor_reduce(tot[:, :], LOG[:, :, 0:E], AX, ALU.max))
                then(dve.tensor_tensor(score[:, :, 0:E], LOG[:, :, 0:E], over(tot[:, :], E), ALU.subtract))
                dve.tensor_scalar(score[:, :, E:E + 1], LOG[:, :, E:E + 1], -1.0, None, ALU.mult).then_inc(exp_in, 1)
                dve.wait_ge(exp_out, 1)
                then(dve.tensor_reduce(tot[:, :], score[:, :, 0:E], AX, ALU.add))
                then(dve.reciprocal(rtot[:, :], tot[:, :]))
                dve.wait_ge(cleared, 2)
                then(dve.tensor_tensor(vals[:, :, 0:E], score[:, :, 0:E], over(rtot[:, :], E), ALU.mult))
            else:
                bias = W["bias"].rearrange("p (o e) -> p o e", o=1).to_broadcast([P, NTOK, E])
                dve.wait_ge(exp_out, 1)
                dve.wait_ge(cleared, 2)
                then(dve.tensor_tensor(vals[:, :, 0:E], score[:, :, 0:E], bias, ALU.add))
            for n in range(NTOK):
                m = dve.max(top[:, n, :], vals[:, n, 0:E])
            then(m)
            then(dve.memset(top[:, :, K:8], SENT))
            for n in range(NTOK):
                m = dve.match_replace(marked[:, n, :], top[:, n, :], vals[:, n, :], PICKED)
            then(m)
            then(dve.tensor_scalar(marked[:, :, 0:E], marked[:, :, 0:E], 1e38, None, ALU.is_ge))
            if kind == "top_softmax":
                best = top[:, :, 0:1].to_broadcast([P, NTOK, E])
                dve.tensor_tensor(score[:, :, :], vals[:, :, 0:E], best, ALU.subtract).then_inc(exp_in, 1)
                dve.wait_ge(exp_out, 1)
                source = score
            elif kind == "softmax_top":
                source = vals
            else:
                source = score
            then(dve.tensor_tensor(wt[:, :, 0:E], source[:, :, 0:E], marked[:, :, 0:E], ALU.mult))
            if kind != "softmax_top":
                then(dve.tensor_reduce(tot[:, :], wt[:, :, 0:E], AX, ALU.add))
                then(dve.reciprocal(rtot[:, :], tot[:, :]))
                then(dve.tensor_tensor(wt[:, :, 0:E], wt[:, :, 0:E], over(rtot[:, :], E), ALU.mult))
            if kind == "top_softmax":
                then(dve.memset(wt[:, :, E:EW], 1.0))
            elif kind == "softmax_top":
                then(dve.tensor_scalar(score[:, :, E:EW], score[:, :, E:EW], 1.0, None, ALU.add))
                then(dve.reciprocal(wt[:, :, E:EW], score[:, :, E:EW]))
            then(dve.tensor_copy(parts[:, :, 0:EW], wt[:, :, :]))
            then(dve.tensor_tensor(wt[:, :, :], wt[:, :, :], parts[:, :, 0:EW], ALU.subtract))
            then(dve.tensor_copy(parts[:, :, 32:32 + EW], wt[:, :, :]))
            then(dve.tensor_tensor(wt[:, :, :], wt[:, :, :], parts[:, :, 32:32 + EW], ALU.subtract))
            dve.tensor_copy(parts[:, :, 64:64 + EW], wt[:, :, :]).then_inc(parts_ready, 1)
            for b in range(NB):
                dve.wait_ge(turned, b + 1)
                dve.tensor_copy(partsT[:, b, :], PS[:, b, 0:T // 2].bitcast(BF16)[0:96, :]).then_inc(turned_kept, 1)

            with dve.Fori(0, NB) as b:
                for f in range(NT):
                    dve.wait_ge(silu_ready.sem, silu_ready.at(b, f + 1))
                    dve.wait_ge(up_ready.sem, up_ready.at(b, f + 1))
                    if f >= 1:
                        dve.wait_ge(hid_ready.sem, hid_ready.at(b, f))
                    else:
                        dve.wait_ge(hid_ready.sem, hid_ready.at(b, 0))
                    dve.tensor_tensor(prod[:, :], silu[:, f % 3, :], PS[:, 2 + f % 2, :], ALU.mult)\
                       .then_inc(prod_ready.sem, 1)
                    dve.wait_ge(prod_ready.sem, prod_ready.at(b, f + 1))
                    if f >= 3:
                        dve.wait_ge(hid_used.sem, hid_used.at(b, f - 2))
                    else:
                        dve.wait_ge(hid_used.sem, hid_used.at(b, 0))
                    dve.tensor_tensor(hid[:, f % 3, :], prod[:, :], PS[:, 4 + f % 2, :], ALU.mult)\
                       .then_inc(hid_ready.sem, 1)
                dve.wait_ge(hid_used.sem, hid_used.at(b, NT))
                dve.tensor_tensor(Y[:, b, :], X[:, b, :], PS[:, 6, :], ALU.add).then_inc(out_kept.sem, 1)


TERMS = [(0, 0), (0, 1), (1, 0), (0, 2), (2, 0), (1, 1)]


def attn(nc, tag, X, Y, PS, C, W, causal):
    D = 8 if causal else 4
    SW = 64 if causal else 32
    HG = P // SW
    NG = 8
    NO = NG * HG // 4
    MR = 6 * D
    NU = TT * HG
    NPR = HG // 2
    STEPS = NG * TT
    EARLY = 2
    STRIPS_AFTER = {0: (2,), 1: (3,), 2: (4,), 3: (5,), 4: (6,), 5: (7,)}
    FIRST_FILL = 2
    NP = 1 if causal else 2
    with ExitStack() as ctx:
        s = Stage(nc, ctx)
        xs = s.sb(f"{tag}_xs", [P, T])
        qk = s.sb(f"{tag}_qk", [P, 2, T])
        rot = s.sb(f"{tag}_rot", [P, 2, T])
        qk_parts = s.sb(f"{tag}_qk_parts", [P, 3, 2, T], BF16)
        q_str = s.sb(f"{tag}_q_str", [P, NG, T], BF16)
        k_str = s.sb(f"{tag}_k_str", [P, NG, HG, T], BF16)
        q_max = s.sb(f"{tag}_q_max", [P, 2, T], BF16)
        v_aug = s.sb(f"{tag}_v_aug", [P, TT, 16, 32])
        mx = s.sb(f"{tag}_mx", [P, 2, TT, HG])
        mx_rest = s.sb(f"{tag}_mx_rest", [P, TT, HG])
        neg_max = s.sb(f"{tag}_neg_max", [P, 2, TT, P], BF16)
        probs = s.sb(f"{tag}_probs", [P, 3, HG, T])
        o_raw = s.sb(f"{tag}_o_raw", [P, NO, T])
        rsum = s.sb(f"{tag}_rsum", [P, 2, T])
        oc = s.sb(f"{tag}_oc", [P, 2, T])
        sq = s.sb(f"{tag}_sq", [P, T])
        lam = s.sb(f"{tag}_lam", [P, 8])
        set_up = s.sem(f"{tag}_set_up")
        lam_in = s.sem(f"{tag}_lam_in")
        lam_exp = s.sem(f"{tag}_lam_exp")
        lam_step = s.sem(f"{tag}_lam_step")
        xs_ready = s.sig(f"{tag}_xs_ready", 1)
        qk_ready = s.sig(f"{tag}_qk_ready", NP)
        v_ready = s.sig(f"{tag}_v_ready", 1)
        v_kept = s.sig(f"{tag}_v_kept", 1)
        split_step = s.sig(f"{tag}_split_step", 8 if not causal else 5)
        parts_ready = s.sig(f"{tag}_parts_ready", 1)
        spread = s.sig(f"{tag}_spread", 2 * NG)
        q_early = s.sig(f"{tag}_q_early", EARLY)
        q_kept = s.sig(f"{tag}_q_kept", NG - EARLY)
        k_kept = s.sig(f"{tag}_k_kept", NG * HG)
        scored = s.sig(f"{tag}_scored", NG * NU)
        maxed = s.sig(f"{tag}_maxed", NG * NU)
        max_step = s.sig(f"{tag}_max_step", 3 * NG)
        neg_ready = s.sig(f"{tag}_neg_ready", NG)
        neg_turned = s.sig(f"{tag}_neg_turned", NG)
        q_max_ready = s.sig(f"{tag}_q_max_ready", NG)
        shifted = s.sig(f"{tag}_shifted", STEPS * NPR)
        exped = s.sig(f"{tag}_exped", STEPS * NPR)
        pv_done = s.sig(f"{tag}_pv_done", STEPS)
        o_kept = s.sig(f"{tag}_o_kept", NO)
        gathered = s.sig(f"{tag}_gathered", NO // 2)
        post = s.sig(f"{tag}_post", 1 if causal else 7)
        squares = s.sig(f"{tag}_squares", 1)
        ms_ready = s.sig(f"{tag}_ms_ready", 1)
        rms_ready = s.sig(f"{tag}_rms_ready", 1)
        o_ready = s.sig(f"{tag}_o_ready", 1)
        projected = s.sig(f"{tag}_projected", 1)
        done = s.sig(f"{tag}_done", 1, ahead=1)
        block = ctx.enter_context(nc.Block())
        NEGT = PS[:, 7, 0:T // 2].bitcast(BF16)

        def o_tile(g):
            return (g // 2, (g % 2) * 2) if causal else (g, 0)

        def head_v(g, j):
            return 2 * g + j if causal else 4 * (g % 4) + j

        def keys(tt):
            return (tt + 1) * P if causal else T

        def first_query(st):
            return st * P if causal else 0

        def keep_o(act, b, g):
            o, slot = o_tile(g)
            if slot + HG == 4:
                act.wait_ge(pv_done.sem, pv_done.at(b, (g + 1) * TT))
                act.activation(o_raw[:, o, :], PS[:, 6, :], ACT.Copy).then_inc(o_kept.sem, 1)

        def batches(eng, body):
            body(0, None, 1)
            with eng.Fori(1, NB - 1) as b:
                body(b, b - 1, b + 1)
            body(NB - 1, NB - 2, None)

        @block.gpsimd
        def _(pool):
            pool.memset(neg_max[:, :, :, :], 0.0).then_inc(set_up, 1)
            pool.memset(v_aug[:, :, :, :], 0.0).then_inc(set_up, 1)
            pool.wait_ge(set_up, 2)
            pool.memset(v_aug[:, :, :, 8:9], 1.0).then_inc(set_up, 1)

        @block.tensor
        def _(pe):
            C["weights"](pe, tag)

            def pass1(b, g, tt, heads=range(HG)):
                for j in heads:
                    u = g * NU + tt * HG + j
                    if u >= 2:
                        pe.wait_ge(maxed.sem, maxed.at(b, u - 1))
                    n = keys(tt)
                    mm = pe.matmul(PS[:, u % 2, 0:n], q_str[:, g, bass.ts(tt, P)], k_str[:, g, j, 0:n],
                                   start=True, stop=not causal)
                    if causal:
                        mm = pe.matmul(PS[:, u % 2, tt * P:n], C["ident_bf"], W["mask"],
                                       start=False, stop=True)
                    mm.then_inc(scored.sem, 1)

            def pass2(b, g, st, pr):
                if st == 0 and pr == 0:
                    pe.wait_ge(q_max_ready.sem, q_max_ready.at(b, g + 1))
                t0 = first_query(st)
                v = (g * TT + st) * NPR + pr
                if v >= 2:
                    pe.wait_ge(exped.sem, exped.at(b, v - 1))
                for j in (2 * pr, 2 * pr + 1):
                    bank = 2 + 2 * (v % 2) + j % 2
                    mm = pe.matmul(PS[:, bank, 0:T - t0], k_str[:, g, j, bass.ts(st, P)],
                                   q_max[:, g % 2, t0:T], start=True, stop=not causal)
                    if causal:
                        mm = pe.matmul(PS[:, bank, 0:P], C["ident_bf"], W["mask_t"], start=False, stop=True)
                mm.then_inc(shifted.sem, 1)

            def pv(b, g, st):
                o, slot = o_tile(g)
                pe.wait_ge(exped.sem, exped.at(b, (g * TT + st + 1) * NPR))
                if st == 0 and slot == 0 and o > 0:
                    pe.wait_ge(o_kept.sem, o_kept.at(b, o))
                t0 = first_query(st)
                for j in range(HG):
                    at = 32 * (slot + j)
                    mm = pe.matmul(PS[at:at + 32, 6, t0:T], v_aug[:, st, head_v(g, j), :],
                                   probs[:, (g * TT + st) % 3, j, 0:T - t0], start=(st == 0), stop=(st == TT - 1))
                mm.then_inc(pv_done.sem, 1)

            def turn_max(b, g):
                pe.wait_ge(neg_ready.sem, neg_ready.at(b, g + 1))
                if g >= 1:
                    pe.wait_ge(q_max_ready.sem, q_max_ready.at(b, g))
                for tt in range(TT):
                    mm = pe.transpose(NEGT[:, bass.ts(tt, P)], neg_max[:, g % 2, tt, :], C["ident_bf"])
                mm.then_inc(neg_turned.sem, 1)

            def project(b, n):
                for i, name in enumerate(["q", "k"] if causal else [("q", "q_sw"), ("k", "k_sw")][n]):
                    mm = pe.matmul(PS[:, i, :], W[name], X[:, b, :], start=True, stop=True)
                mm.then_inc(qk_ready.sem, 1)

            def fill_strips(b, g):
                bank = 0 if g < EARLY else 6
                pe.wait_ge(parts_ready.sem, parts_ready.at(b, 1))
                if g == EARLY:
                    pe.wait_ge(v_kept.sem, v_kept.at(b, 1))
                elif g >= 1:
                    if g < EARLY:
                        pe.wait_ge(q_early.sem, q_early.at(b, g))
                    else:
                        pe.wait_ge(q_kept.sem, q_kept.at(b, g - EARLY))
                    pe.wait_ge(k_kept.sem, k_kept.at(b, g * HG))
                for n in range(2):
                    for i in range(3):
                        at = ((n * 3 + i) * NG + g) * P
                        mm = pe.matmul(PS[:, bank + n, :], W["strips"][:, at:at + P], qk_parts[:, i, n, :],
                                       start=(i == 0), stop=(i == 2))
                    mm.then_inc(spread.sem, 1)

            def gather(par, n):
                for i in range(4):
                    mm = pe.matmul(PS[32 * i:32 * i + 32, 2 + 2 * par + n, :], W[("pick_o", "pick_sum")[n]],
                                   o_raw[:, 4 * par + i, :], start=True, stop=True)
                mm.then_inc(gathered.sem, 1)

            def mean_squares(b):
                pe.wait_ge(squares.sem, squares.at(b, 1))
                pe.matmul(PS[:, 2, :], W["mean8"], sq[:, :], start=True, stop=True).then_inc(ms_ready.sem, 1)

            def project_out(b):
                pe.wait_ge(o_ready.sem, o_ready.at(b, 1))
                pe.matmul(PS[:, 3, :], W["out"], oc[:, 0, :], start=True, stop=True).then_inc(projected.sem, 1)

            def body(b, before, after):
                pe.wait_ge(xs_ready.sem, xs_ready.at(b, 1))
                for st in range(TT):
                    mm = pe.matmul(PS[:, 7, bass.ts(st, P)], xs[:, bass.ts(st, P)], W["v"], start=True, stop=True)
                mm.then_inc(v_ready.sem, 1)
                pe.wait_ge(q_early.sem, q_early.at(b, EARLY))
                pe.wait_ge(k_kept.sem, k_kept.at(b, EARLY * HG))
                for i in range(2 * TT):
                    for j in range(HG):
                        pass1(b, i // TT, i % TT, (j,))
                        if i == 0 and before is not None:
                            if j == 0:
                                pe.wait_ge(o_kept.sem, o_kept.at(before, NO))
                            gather(j // 2, j % 2)
                    if i == 3 and before is not None and not causal:
                        mean_squares(before)
                    for g in STRIPS_AFTER.get(i, ()):
                        fill_strips(b, g)
                    if i == 6 and before is not None:
                        project_out(before)
                pe.wait_ge(q_kept.sem, q_kept.at(b, NG - EARLY))
                pe.wait_ge(k_kept.sem, k_kept.at(b, NG * HG))
                turn_max(b, 0)
                if before is not None:
                    pe.wait_ge(done.sem, done.at(before, 1))
                for g in range(NG):
                    for st in range(TT):
                        ahead = g + 2 < NG
                        for pr in range(NPR):
                            if ahead:
                                pass1(b, g + 2, st, (pr,))
                            pass2(b, g, st, pr)
                        for j in range(NPR, HG - 1):
                            if ahead:
                                pass1(b, g + 2, st, (j,))
                        if (g, st) > (0, 0):
                            pv(b, *((g, st - 1) if st else (g - 1, TT - 1)))
                        if ahead:
                            pass1(b, g + 2, st, (HG - 1,))
                        if st == 1 and g + 1 < NG:
                            turn_max(b, g + 1)
                        if after is not None:
                            if (g, st) == (6, 0):
                                pe.wait_ge(maxed.sem, maxed.at(b, NG * NU))
                                project(after, 0)
                            if (g, st) == (6, 1) and not causal:
                                pe.wait_ge(split_step.sem, split_step.at(after, 2))
                                project(after, 1)
                            if g == 7 and 0 <= st - FIRST_FILL < EARLY:
                                fill_strips(after, st - FIRST_FILL)
                pv(b, NG - 1, TT - 1)

            for n in range(NP):
                if n == 1:
                    pe.wait_ge(split_step.sem, split_step.at(0, 2))
                project(0, n)
            for g in range(EARLY):
                fill_strips(0, g)
            batches(pe, body)
            last = NB - 1
            pe.wait_ge(o_kept.sem, o_kept.at(last, NO))
            for par in range(NO // 4):
                for n in range(2):
                    gather(par, n)
            if not causal:
                mean_squares(last)
            project_out(last)

        @block.scalar
        def _(act):
            C["weights"](act, tag)
            if not causal:
                act.wait_ge(lam_in, 1)
                act.activation(lam[:, 2:4], lam[:, 0:2], ACT.Exp).then_inc(lam_exp, 1)
            def copy_x(b):
                act.activation(xs[:, :], X[:, b, :], ACT.Copy).then_inc(xs_ready.sem, 1)

            def keep_strips(b, g):
                bank = 0 if g < EARLY else 6
                if g >= EARLY:
                    act.wait_ge(spread.sem, spread.at(b, 2 * g + 1))
                    act.activation(q_str[:, g, :], PS[:, bank, :], ACT.Copy).then_inc(q_kept.sem, 1)
                act.wait_ge(spread.sem, spread.at(b, 2 * g + 2))
                for j in range(HG):
                    act.activation(k_str[:, g, j, :], PS[:, bank + 1, :], ACT.Identity,
                                   bias=W["ones_rows"][:, j:j + 1], scale=W["strip_rows"][:, j:j + 1])\
                       .then_inc(k_kept.sem, 1)

            def rms(b):
                act.wait_ge(post.sem, post.at(b, 5))
                act.activation(sq[:, :], oc[:, 0, :], ACT.Square).then_inc(squares.sem, 1)
                act.wait_ge(ms_ready.sem, ms_ready.at(b, 1))
                act.activation(rsum[:, 0, :], PS[:, 2, :], ACT.Sqrt, bias=W["eps"]).then_inc(rms_ready.sem, 1)

            def body(b, before, after):
                for g in range(EARLY, NG):
                    if g == 5 and before is not None and not causal:
                        rms(before)
                    keep_strips(b, g)
                for g in range(NG):
                    for st in range(TT):
                        n = T - first_query(st)
                        step = g * TT + st
                        if step >= 3:
                            act.wait_ge(pv_done.sem, pv_done.at(b, step - 2))
                        for pr in range(NPR):
                            v = step * NPR + pr
                            act.wait_ge(shifted.sem, shifted.at(b, v + 1))
                            bank = 2 + 2 * (v % 2)
                            act.activation(probs[:, step % 3, 2 * pr:2 * pr + 2, 0:n], PS[:, bank:bank + 2, 0:n],
                                           ACT.Exp).then_inc(exped.sem, 1)
                        if st == 0 and g > 0:
                            keep_o(act, b, g - 1)
                        if after is not None:
                            if (g, st) == (6, 0):
                                act.wait_ge(v_ready.sem, v_ready.at(b, 1))
                                copy_x(after)
                            if g == 7 and 0 <= st - FIRST_FILL < EARLY:
                                keep_strips(after, st - FIRST_FILL)
                keep_o(act, b, NG - 1)

            copy_x(0)
            for g in range(EARLY):
                keep_strips(0, g)
            batches(act, body)
            if not causal:
                rms(NB - 1)

        @block.vector
        def _(dve):
            dve.sem_inc(done.sem, 1)
            C["weights"](dve, tag)
            if not causal:
                for n in range(2):
                    dve.tensor_tensor(sq[:, 4 * n:4 * n + 4], W["lam_q"][:, 4 * n:4 * n + 4],
                                      W["lam_k"][:, 4 * n:4 * n + 4], ALU.mult).then_inc(lam_step, 1)
                dve.wait_ge(lam_step, 2)
                dve.tensor_reduce(lam[:, 0:2], sq[:, 0:8].rearrange("p (n e) -> p n e", e=4), AX, ALU.add)\
                   .then_inc(lam_in, 1)
                dve.wait_ge(lam_exp, 1)
                dve.tensor_tensor(lam[:, 4:5], lam[:, 3:4], lam[:, 2:3], ALU.subtract).then_inc(lam_step, 1)
                dve.wait_ge(lam_step, 3)
                dve.tensor_scalar(lam[:, 5:6], lam[:, 4:5], -LAMBDA_INIT, None, ALU.add).then_inc(lam_step, 1)
                dve.wait_ge(lam_step, 4)
            dve.wait_ge(set_up, 3)

            def maxima(b, g, tt, before=None):
                for j in range(HG):
                    u = g * NU + tt * HG + j
                    dve.wait_ge(scored.sem, scored.at(b, u + 1))
                    if tt == 0 and j == 0 and g >= 2:
                        dve.wait_ge(max_step.sem, max_step.at(b, 3 * (g - 1)))
                    elif tt == 0 and j == 0 and before is not None:
                        dve.wait_ge(max_step.sem, max_step.at(before, 3 * (NG - 1 + g)))
                    dve.tensor_reduce(mx[:, g % 2, tt, j:j + 1], PS[:, u % 2, 0:keys(tt)], AX, ALU.max)\
                       .then_inc(maxed.sem, 1)

            def negate(b, g, before=None):
                rows = neg_max[:, g % 2, :, :].rearrange("p t (j w) -> p t j w", w=SW)
                dve.wait_ge(maxed.sem, maxed.at(b, (g + 1) * NU))
                if g >= 2:
                    dve.wait_ge(neg_turned.sem, neg_turned.at(b, g - 1))
                elif before is not None:
                    dve.wait_ge(neg_turned.sem, neg_turned.at(before, NG - 1 + g))
                m = mx[:, g % 2, :, :]
                dve.tensor_scalar(rows[:, :, :, MR], m, -1.0, None, ALU.mult).then_inc(max_step.sem, 1)
                dve.wait_ge(max_step.sem, max_step.at(b, 3 * g + 1))
                if g >= 1:
                    dve.wait_ge(neg_ready.sem, neg_ready.at(b, g))
                elif before is not None:
                    dve.wait_ge(neg_ready.sem, neg_ready.at(before, NG))
                dve.scalar_tensor_tensor(mx_rest[:, :, :], m, -1.0, rows[:, :, :, MR], ALU.mult, ALU.subtract)\
                   .then_inc(max_step.sem, 1)
                dve.wait_ge(max_step.sem, max_step.at(b, 3 * g + 2))
                dve.tensor_copy(rows[:, :, :, MR + 1], mx_rest[:, :, :]).then_inc(max_step.sem, 1)
                dve.wait_ge(max_step.sem, max_step.at(b, 3 * g + 3))
                dve.tensor_tensor(rows[:, :, :, MR + 2], mx_rest[:, :, :], rows[:, :, :, MR + 1], ALU.subtract)\
                   .then_inc(neg_ready.sem, 1)

            def add_max(b, g):
                dve.wait_ge(neg_turned.sem, neg_turned.at(b, g + 1))
                if g >= 2:
                    dve.wait_ge(shifted.sem, shifted.at(b, (g - 1) * TT * NPR))
                dve.tensor_tensor(q_max[:, g % 2, :], q_str[:, g, :], NEGT, ALU.add).then_inc(q_max_ready.sem, 1)

            def make_qk(b, n, before):
                dve.wait_ge(qk_ready.sem, qk_ready.at(b, n + 1))
                if n == 0 and before is not None:
                    dve.wait_ge(parts_ready.sem, parts_ready.at(before, 1))
                if causal:
                    dve.tensor_scalar(qk[:, 0, :], PS[:, 0, :], float(D) ** -0.5, None, ALU.mult)\
                       .then_inc(split_step.sem, 1)
                    dve.tensor_copy(qk[:, 1, :], PS[:, 1, :]).then_inc(split_step.sem, 1)
                else:
                    tab = slice(n * T, (n + 1) * T)
                    dve.tensor_tensor(qk[:, n, :], PS[:, 0, :], W["cos"][:, tab], ALU.mult)\
                       .then_inc(split_step.sem, 1)
                    dve.tensor_tensor(rot[:, n, :], PS[:, 1, :], W["sin"][:, tab], ALU.mult)\
                       .then_inc(split_step.sem, 1)

            def split(b, before):
                n = 2 * NP
                dve.wait_ge(split_step.sem, split_step.at(b, n))
                if not causal:
                    dve.tensor_tensor(qk[:, :, :], qk[:, :, :], rot[:, :, :], ALU.add).then_inc(split_step.sem, 1)
                    n += 1
                    dve.wait_ge(split_step.sem, split_step.at(b, n))
                if before is not None:
                    dve.wait_ge(spread.sem, spread.at(before, 2 * NG))
                dve.tensor_copy(qk_parts[:, 0, :, :], qk[:, :, :]).then_inc(split_step.sem, 1)
                dve.wait_ge(split_step.sem, split_step.at(b, n + 1))
                dve.tensor_tensor(qk[:, :, :], qk[:, :, :], qk_parts[:, 0, :, :], ALU.subtract)\
                   .then_inc(split_step.sem, 1)
                dve.wait_ge(split_step.sem, split_step.at(b, n + 2))
                dve.tensor_copy(qk_parts[:, 1, :, :], qk[:, :, :]).then_inc(split_step.sem, 1)
                dve.wait_ge(split_step.sem, split_step.at(b, n + 3))
                dve.tensor_tensor(qk_parts[:, 2, :, :], qk[:, :, :], qk_parts[:, 1, :, :], ALU.subtract)\
                   .then_inc(parts_ready.sem, 1)

            def keep_early(b, g):
                dve.wait_ge(spread.sem, spread.at(b, 2 * g + 1))
                dve.tensor_copy(q_str[:, g, :], PS[:, 0, :]).then_inc(q_early.sem, 1)

            def invert_sums(b, par):
                dve.wait_ge(gathered.sem, gathered.at(b, 2 * par + 2))
                dve.wait_ge(done.sem, done.at(b, 0))
                dve.reciprocal(rsum[:, par, :], PS[:, 3 + 2 * par, :]).then_inc(post.sem, 1)

            def normalise(b):
                if causal:
                    dve.wait_ge(post.sem, post.at(b, 1))
                    dve.tensor_tensor(oc[:, 0, :], PS[:, 2, :], rsum[:, 0, :], ALU.mult).then_inc(o_ready.sem, 1)
                    return
                dve.wait_ge(post.sem, post.at(b, 2))
                for par in range(2):
                    dve.tensor_tensor(oc[:, par, :], PS[:, 2 + 2 * par, :], rsum[:, par, :], ALU.mult)\
                       .then_inc(post.sem, 1)
                dve.wait_ge(post.sem, post.at(b, 4))
                dve.scalar_tensor_tensor(oc[:, 0, :], oc[:, 1, :], lam[:, 5:6], oc[:, 0, :], ALU.mult, ALU.add)\
                   .then_inc(post.sem, 1)

            def rms_norm(b):
                dve.wait_ge(rms_ready.sem, rms_ready.at(b, 1))
                dve.reciprocal(rsum[:, 1, :], rsum[:, 0, :]).then_inc(post.sem, 1)
                dve.wait_ge(post.sem, post.at(b, 6))
                dve.tensor_tensor(oc[:, 1, :], oc[:, 0, :], rsum[:, 1, :], ALU.mult).then_inc(post.sem, 1)
                dve.wait_ge(post.sem, post.at(b, 7))
                dve.tensor_scalar(oc[:, 0, :], oc[:, 1, :], W["subln"], 1.0 - LAMBDA_INIT, ALU.mult, ALU.mult)\
                   .then_inc(o_ready.sem, 1)

            def add_x(b):
                dve.wait_ge(projected.sem, projected.at(b, 1))
                if causal:
                    y = dve.scalar_tensor_tensor(Y[:, b, :], PS[:, 3, :], W["b_out"], X[:, b, :], ALU.add, ALU.add)
                else:
                    y = dve.tensor_tensor(Y[:, b, :], PS[:, 3, :], X[:, b, :], ALU.add)
                y.then_inc(done.sem, 1)

            def body(b, before, after):
                for i in range(2 * TT):
                    maxima(b, i // TT, i % TT, before)
                    if i == 0:
                        dve.wait_ge(v_ready.sem, v_ready.at(b, 1))
                        dve.tensor_copy(v_aug[:, :, :, 0:8].rearrange("p s h e -> p (s h) e"),
                                        PS[:, 7, :].rearrange("p (sh e) -> p sh e", e=8)).then_inc(v_kept.sem, 1)
                    if before is not None:
                        if i < NO // 4:
                            invert_sums(before, i)
                        if i == 2:
                            normalise(before)
                        if i == 4 and not causal:
                            rms_norm(before)
                        if i == 6:
                            add_x(before)
                    if i % TT == TT - 1:
                        negate(b, i // TT, before)
                dve.wait_ge(q_kept.sem, q_kept.at(b, NG - EARLY))
                add_max(b, 0)
                for g in range(NG):
                    for st in range(TT):
                        if g + 2 < NG:
                            maxima(b, g + 2, st)
                        if st == 1 and g + 1 < NG:
                            add_max(b, g + 1)
                        if after is not None:
                            if (g, st) == (6, 0):
                                make_qk(after, 0, b)
                            if (g, st) == (6, 1):
                                if not causal:
                                    make_qk(after, 1, b)
                                split(after, b)
                            if g == 7 and 0 <= st - FIRST_FILL < EARLY:
                                keep_early(after, st - FIRST_FILL)
                    if g + 2 < NG:
                        negate(b, g + 2)

            for n in range(NP):
                make_qk(0, n, None)
            split(0, None)
            for g in range(EARLY):
                keep_early(0, g)
            batches(dve, body)
            last = NB - 1
            for par in range(NO // 4):
                invert_sums(last, par)
            normalise(last)
            if not causal:
                rms_norm(last)
            add_x(last)


def attn0(nc, tag, X, Y, PS, C, W, scratch):
    W1 = 63
    NQ, NK, H = 4, 4, 8
    NCH = 2 * NQ * NK
    RING = 3
    GATE = ACT.Gelu
    with ExitStack() as ctx:
        s = Stage(nc, ctx)
        disp = s.sb(f"{tag}_disp", [P, 2, T])
        a_pad = s.sb(f"{tag}_a_pad", [P, 2, 2, W1 + T])
        d_pad = s.sb(f"{tag}_d_pad", [P, 2, 2, W1 + T])
        x_pad = s.sb(f"{tag}_x_pad", [P, W1 + T + 1])
        v_tok = s.sb(f"{tag}_v_tok", [P, 2, 8, P])
        pos = s.sb(f"{tag}_pos", [P, 64])
        b_half = s.sb(f"{tag}_b_half", [P, 1])
        bond = s.sb(f"{tag}_bond", [P, RING, 4, T])
        dmg = s.sb(f"{tag}_dmg", [P, RING, 4, T])
        tanh = s.sb(f"{tag}_tanh", [P, 2, T])
        logit = s.sb(f"{tag}_logit", [P, 2, 8, T])
        probs = s.sb(f"{tag}_probs", [P, TT, 16, 64])
        masked = s.sb(f"{tag}_masked", [P, 2, T])
        mx = s.sb(f"{tag}_mx", [P, 16])
        tot = s.sb(f"{tag}_tot", [P, TT, 16])
        rtot = s.sb(f"{tag}_rtot", [P, TT, 16])
        band = s.sb(f"{tag}_band", [P, 2, 16, P])
        band_t = s.sb(f"{tag}_band_t", [P, 16, P])
        o_tok = s.sb(f"{tag}_o_tok", [P, TT, P])
        o_t = s.sb(f"{tag}_o_t", [P, T])
        set_up = s.sem(f"{tag}_set_up")
        zeroed = s.sem(f"{tag}_zeroed")
        pos_ready = s.sem(f"{tag}_pos_ready")
        pos_kept = s.sem(f"{tag}_pos_kept")
        x_kept = s.sig(f"{tag}_x_kept", 1)
        disp_ready = s.sig(f"{tag}_disp_ready", 1)
        disp_kept = s.sig(f"{tag}_disp_kept", 1)
        a_ready = s.sig(f"{tag}_a_ready", 1)
        a_kept = s.sig(f"{tag}_a_kept", 1)
        d_ready = s.sig(f"{tag}_d_ready", 1)
        d_kept = s.sig(f"{tag}_d_kept", 1)
        v_ready = s.sig(f"{tag}_v_ready", 1)
        v_kept = s.sig(f"{tag}_v_kept", 1)
        bond_in = s.sig(f"{tag}_bond_in", NCH)
        dmg_in_pool = s.sig(f"{tag}_dmg_in_pool", NCH - NCH // 8)
        dmg_in_dve = s.sig(f"{tag}_dmg_in_dve", NCH // 8)
        bond_gelu = s.sig(f"{tag}_bond_gelu", NCH)
        dmg_gelu = s.sig(f"{tag}_dmg_gelu", NCH)
        bond_used = s.sig(f"{tag}_bond_used", NCH)
        dmg_used = s.sig(f"{tag}_dmg_used", NCH)
        tanh_ready = s.sig(f"{tag}_tanh_ready", 8)
        logit_ready = s.sig(f"{tag}_logit_ready", 8)
        turned = s.sig(f"{tag}_turned", TT)
        masked_ready = s.sig(f"{tag}_masked_ready", 1)
        maxed = s.sig(f"{tag}_maxed", TT)
        centred = s.sig(f"{tag}_centred", TT)
        exped = s.sig(f"{tag}_exped", TT)
        summed = s.sig(f"{tag}_summed", TT)
        inverted = s.sig(f"{tag}_inverted", 1)
        skewed = [s.sig(f"{tag}_skewed{i}", 32) for i in range(TT)]
        banded = [s.sig(f"{tag}_banded{i}", 16) for i in range(TT)]
        band_turned = s.sig(f"{tag}_band_turned", 2 * TT)
        band_kept = s.sig(f"{tag}_band_kept", 2 * TT)
        pv_done = s.sig(f"{tag}_pv_done", TT)
        o_scaled = s.sig(f"{tag}_o_scaled", TT)
        o_turned = s.sig(f"{tag}_o_turned", 1)
        o_kept = s.sig(f"{tag}_o_kept", 1)
        projected = s.sig(f"{tag}_projected", 1)
        y_done = s.sig(f"{tag}_y_done", 1)
        block = ctx.enter_context(nc.Block())

        TILE = 16 * 2 * 64 * P

        def chunk(n):
            return n // 16, (n // 4) % 4, n % 4

        def batches(eng, body, tail):
            body(0, 0, None, 1)
            body(1, 1, 0, 2)
            with eng.Fori(1, NB // 2 - 1) as i:
                body(i * 2, 0, i * 2 - 1, i * 2 + 1)
                body(i * 2 + 1, 1, i * 2, i * 2 + 2)
            body(NB - 2, 0, NB - 3, NB - 1)
            body(NB - 1, 1, NB - 2, None)
            tail(NB - 1, 1)

        SOFTEN_PE = {5: (0, 1), 9: (2,), 10: (3,)}
        SOFTEN_DVE = {8: 0, 9: 1, 12: 2, 13: 3}
        EXP = 14
        SUMS = {18: 0, 19: 1, 20: 2, 21: 3}
        TURN = {17 + i: i for i in range(2 * TT)}
        PV = {19 + 2 * i: i for i in range(TT)}
        SCALE = {23: 0, 25: 1, 27: 2, 28: 3}

        def by_dve(n):
            return n % 8 == 7

        def damage(eng, par, n):
            g, q, k = chunk(n)
            d0 = 16 * q + k
            row = d_pad[:, par, g, :]
            part = [row.ap[0][0], row.ap[0][1]]
            later = bass.AP(tensor=row.tensor, offset=row.offset + d0, ap=[part, [4, 4], [1, T]])
            own = bass.AP(tensor=row.tensor, offset=row.offset + W1, ap=[part, [0, 4], [1, T]])
            return eng.tensor_tensor(dmg[:, n % RING, :, :], later, own, ALU.subtract)

        @block.sync
        def _(sp):
            sp.wait_ge(set_up, 5)
            for i in range(TT):
                for part in range(2):
                    base = (2 * i + part) * P * 16 * 64
                    sp.dma_start(scratch[base:base + P * 16 * 64].rearrange("(p c) -> p c", p=P),
                                 probs[:, 0, :, :].rearrange("p h d -> p (h d)")).then_inc(zeroed, 16)
            sp.wait_ge(zeroed, 16 * 2 * TT)

            def write(b, tt):
                base = tt * TILE
                sp.wait_ge(exped.sem, exped.at(b, tt + 1))
                sp.wait_ge(banded[tt].sem, banded[tt].at(b, 0))
                for half in range(2):
                    dst = bass.AP(tensor=scratch.tensor, offset=scratch.offset + base + half * 64 * P,
                                  ap=[[P + 1, 64], [2 * 64 * P, 16], [1, 64]])
                    sp.dma_start(dst, probs[64 * half:64 * half + 64, tt, :, :]).then_inc(skewed[tt].sem, 16)

            def read(b, tt):
                sp.wait_ge(skewed[tt].sem, skewed[tt].at(b, 32))
                if tt >= 2:
                    sp.wait_ge(band_turned.sem, band_turned.at(b, 2 * (tt - 1)))
                else:
                    sp.wait_ge(band_turned.sem, band_turned.at(b, 0))
                src = bass.AP(tensor=scratch.tensor, offset=scratch.offset + tt * TILE,
                              ap=[[P, P], [2 * 64 * P, 16], [1, P]])
                sp.dma_start(band[:, tt % 2, :, :], src).then_inc(banded[tt].sem, 16)

            def skew(b):
                write(b, 0)
                write(b, 1)
                read(b, 0)
                write(b, 2)
                read(b, 1)
                write(b, 3)
                read(b, 2)
                read(b, 3)

            for b in range(NB):
                skew(b)

        @block.gpsimd
        def _(pool):
            pool.memset(a_pad[:, :, :, 0:W1], 0.0).then_inc(set_up, 1)
            pool.memset(d_pad[:, :, :, 0:W1], 0.0).then_inc(set_up, 1)
            pool.memset(x_pad[:, 0:W1], 0.0).then_inc(set_up, 1)
            pool.memset(x_pad[:, W1 + T:W1 + T + 1], 0.0).then_inc(set_up, 1)
            pool.memset(probs[:, 0, :, :], 0.0).then_inc(set_up, 1)
            pool.wait_ge(set_up, 5)

            def body(b, par, before, after):
                pool.wait_ge(d_kept.sem, d_kept.at(b, 1))
                for n in range(NCH):
                    g, q, k = chunk(n)
                    if by_dve(n):
                        continue
                    if n >= RING:
                        pool.wait_ge(dmg_used.sem, dmg_used.at(b, n - RING + 1))
                    elif before is not None:
                        pool.wait_ge(dmg_used.sem, dmg_used.at(before, min(NCH, NCH - 1 + n)))
                    damage(pool, par, n).then_inc(dmg_in_pool.sem, 1)

            batches(pool, body, lambda b, par: None)

        @block.tensor
        def _(pe):
            C["weights"](pe, tag)
            pe.matmul(PS[:, 0, 0:64], W["w_pos"], W["rel"], start=True, stop=True).then_inc(pos_ready, 1)
            pe.wait_ge(pos_kept, 1)

            def project_disp(b):
                for g in range(2):
                    mm = pe.matmul(PS[:, 4 + g, :], W["disp"][:, bass.ts(g, P)], X[:, b, :], start=True, stop=True)
                mm.then_inc(disp_ready.sem, 1)

            def project_ad(b):
                pe.wait_ge(disp_kept.sem, disp_kept.at(b, 1))
                for g in range(2):
                    mm = pe.matmul(PS[:, 6 + g, :], W["strain"], disp[:, g, :], start=True, stop=True)
                mm.then_inc(a_ready.sem, 1)
                for g in range(2):
                    mm = pe.matmul(PS[:, 4 + g, :], W["dmg"], disp[:, g, :], start=True, stop=True)
                mm.then_inc(d_ready.sem, 1)

            def project_v(b):
                pe.wait_ge(x_kept.sem, x_kept.at(b, 1))
                pe.wait_ge(a_kept.sem, a_kept.at(b, 1))
                for j in range(8):
                    mm = pe.matmul(PS[:, 6 + j // 4, bass.ts(j % 4, P)], x_pad[:, 64 * j:64 * j + P], W["val"],
                                   start=True, stop=True)
                mm.then_inc(v_ready.sem, 1)

            def soften(b, par, tt):
                pe.wait_ge(logit_ready.sem, logit_ready.at(b, 8))
                if tt >= 2:
                    pe.wait_ge(centred.sem, centred.at(b, tt - 1))
                for g in range(2):
                    for q in range(NQ):
                        mm = pe.transpose(PS[:, 4 + 2 * (tt % 2) + g, bass.ts(q, P)],
                                          logit[:, par, 4 * g + q, bass.ts(tt, P)], C["ident"])
                mm.then_inc(turned.sem, 1)

            def turn_bands(b, i):
                tt, half = i // 2, i % 2
                if half == 0:
                    pe.wait_ge(banded[tt].sem, banded[tt].at(b, 16))
                if i == 0:
                    pe.wait_ge(centred.sem, centred.at(b, TT))
                else:
                    pe.wait_ge(band_kept.sem, band_kept.at(b, i))
                for hh in range(8):
                    mm = pe.transpose(PS[:, 6 + hh // 4, bass.ts(hh % 4, P)], band[:, tt % 2, 8 * half + hh, :],
                                      C["ident"])
                mm.then_inc(band_turned.sem, 1)

            def products(b, par, tt):
                pe.wait_ge(band_kept.sem, band_kept.at(b, 2 * tt + 2))
                if tt >= 2:
                    pe.wait_ge(o_scaled.sem, o_scaled.at(b, tt - 1))
                else:
                    pe.wait_ge(centred.sem, centred.at(b, TT))
                for h in range(16):
                    for half in range(2):
                        rows = slice(64 * half, 64 * half + 64)
                        mm = pe.matmul(PS[rows, 4 + tt % 2, 8 * h:8 * h + 8], band_t[:, h, rows],
                                       v_tok[:, par, 2 * tt + half, 8 * h:8 * h + 8], start=True, stop=True)
                mm.then_inc(pv_done.sem, 1)

            def turn_o(b):
                pe.wait_ge(o_scaled.sem, o_scaled.at(b, TT))
                for tt in range(TT):
                    mm = pe.transpose(PS[:, 5, bass.ts(tt, P)], o_tok[:, tt, :], C["ident"])
                mm.then_inc(o_turned.sem, 1)

            def finish(b):
                pe.wait_ge(o_kept.sem, o_kept.at(b, 1))
                pe.matmul(PS[:, 4, :], W["c_proj"], o_t[:, :], start=True, stop=True).then_inc(projected.sem, 1)

            def body(b, par, before, after):
                for n in range(NCH):
                    g, q, k = chunk(n)
                    gq = n // 4
                    if k == 0:
                        if gq >= 2:
                            pe.wait_ge(tanh_ready.sem, tanh_ready.at(b, gq - 1))
                            pe.wait_ge(logit_ready.sem, logit_ready.at(b, gq - 1))
                        elif before is not None:
                            pe.wait_ge(tanh_ready.sem, tanh_ready.at(before, 7 + gq))
                            pe.wait_ge(logit_ready.sem, logit_ready.at(before, 7 + gq))
                    for bank, data, ready, used, wname in ((gq % 2, bond, bond_gelu, bond_used, "w_bond"),
                                                           (2 + gq % 2, dmg, dmg_gelu, dmg_used, "w_dmg_out")):
                        pe.wait_ge(ready.sem, ready.at(b, n + 1))
                        for c in range(4):
                            mm = pe.matmul(PS[32 * c:32 * c + 32, bank, :], W[wname][:, 32 * k:32 * k + 32],
                                           data[:, n % RING, c, :], start=(k == 0), stop=(k == 3))
                        mm.then_inc(used.sem, 1)
                    if n == 0:
                        if before is not None:
                            pe.wait_ge(y_done.sem, y_done.at(before, 0))
                        if after is not None:
                            project_disp(after)
                    if n == 2:
                        pe.wait_ge(v_kept.sem, v_kept.at(b, 1))
                        if after is not None:
                            project_ad(after)
                    if before is not None:
                        for tt in SOFTEN_PE.get(n, ()):
                            if tt < 2 and after is not None:
                                kept = a_kept if tt else d_kept
                                pe.wait_ge(kept.sem, kept.at(after, 1))
                            soften(before, 1 - par, tt)
                        if n in PV:
                            products(before, 1 - par, PV[n])
                        if n in TURN:
                            turn_bands(before, TURN[n])
                        if n == 28:
                            turn_o(before)
                        if n == 29:
                            finish(before)
                    if n == 30 and after is not None:
                        if before is not None:
                            pe.wait_ge(band_kept.sem, band_kept.at(before, 2 * TT))
                        project_v(after)

            def tail(b, par):
                for tt in range(TT):
                    soften(b, par, tt)
                turn_bands(b, 0)
                turn_bands(b, 1)
                for tt in range(TT):
                    if tt + 1 < TT:
                        turn_bands(b, 2 * tt + 2)
                    products(b, par, tt)
                    if tt + 1 < TT:
                        turn_bands(b, 2 * tt + 3)
                turn_o(b)
                finish(b)

            project_disp(0)
            project_ad(0)
            project_v(0)
            batches(pe, body, tail)

        @block.scalar
        def _(act):
            C["weights"](act, tag)
            act.wait_ge(set_up, 5)
            act.wait_ge(pos_kept, 2)

            def keep_x_disp(b, first=False):
                if not first:
                    act.wait_ge(v_ready.sem, v_ready.at(b, 0))
                    act.wait_ge(d_ready.sem, d_ready.at(b, 0))
                act.activation(x_pad[:, W1:W1 + T], X[:, b, :], ACT.Copy).then_inc(x_kept.sem, 1)
                act.wait_ge(disp_ready.sem, disp_ready.at(b, 1))
                act.activation(disp[:, :, :], PS[:, 4:6, :], ACT.Copy).then_inc(disp_kept.sem, 1)

            def keep_v(b, par):
                act.wait_ge(v_ready.sem, v_ready.at(b, 1))
                act.activation(v_tok[:, par, :, :].rearrange("p j c -> p (j c)"),
                               PS[:, 6:8, :].rearrange("p a c -> p (a c)"), ACT.Copy).then_inc(v_kept.sem, 1)

            def exps(b):
                act.wait_ge(centred.sem, centred.at(b, TT))
                act.activation(probs[:, :, :, :], probs[:, :, :, :], ACT.Exp).then_inc(exped.sem, TT)

            def keep_bands(b, i):
                tt, half = i // 2, i % 2
                act.wait_ge(band_turned.sem, band_turned.at(b, i + 1))
                act.wait_ge(pv_done.sem, pv_done.at(b, tt))
                act.activation(band_t[:, 8 * half:8 * half + 8, :],
                               PS[:, 6:8, :].rearrange("p a (h t) -> p (a h) t", h=4), ACT.Copy)\
                   .then_inc(band_kept.sem, 1)

            def keep_o(b):
                act.wait_ge(projected.sem, projected.at(b, 0))
                act.wait_ge(o_turned.sem, o_turned.at(b, 1))
                act.activation(o_t[:, :], PS[:, 5, :], ACT.Copy).then_inc(o_kept.sem, 1)

            def to_tanh(b, gq, before):
                act.wait_ge(dmg_used.sem, dmg_used.at(b, 4 * gq + 4))
                if gq >= 2:
                    act.wait_ge(logit_ready.sem, logit_ready.at(b, gq - 1))
                elif before is not None:
                    act.wait_ge(logit_ready.sem, logit_ready.at(before, 7 + gq))
                act.activation(tanh[:, gq % 2, :], PS[:, 2 + gq % 2, :], ACT.Tanh, bias=b_half[:, :], scale=0.5)\
                   .then_inc(tanh_ready.sem, 1)

            def body(b, par, before, after):
                for n in range(NCH):
                    g, q, k = chunk(n)
                    act.wait_ge(bond_in.sem, bond_in.at(b, n + 1))
                    act.activation(bond[:, n % RING, :, :], bond[:, n % RING, :, :], GATE).then_inc(bond_gelu.sem, 1)
                    if by_dve(n):
                        act.wait_ge(dmg_in_dve.sem, dmg_in_dve.at(b, n // 8 + 1))
                    else:
                        act.wait_ge(dmg_in_pool.sem, dmg_in_pool.at(b, n + 1 - n // 8))
                    act.activation(dmg[:, n % RING, :, :], dmg[:, n % RING, :, :], GATE, bias=W["b_dmg"])\
                       .then_inc(dmg_gelu.sem, 1)
                    if n == 0 and before is not None:
                        to_tanh(before, 7, None)
                    elif k == 0 and n > 0:
                        to_tanh(b, n // 4 - 1, before)
                    if n == 1 and after is not None:
                        keep_x_disp(after)
                    if before is not None:
                        if n == EXP:
                            exps(before)
                        if n - 1 in TURN:
                            keep_bands(before, TURN[n - 1])
                        if n == 29:
                            keep_o(before)
                    if n == 31 and after is not None:
                        if before is not None:
                            act.wait_ge(pv_done.sem, pv_done.at(before, TT))
                        keep_v(after, 1 - par)

            def tail(b, par):
                to_tanh(b, 7, None)
                for tt in range(TT):
                    act.wait_ge(centred.sem, centred.at(b, tt + 1))
                    act.activation(probs[:, tt, :, :], probs[:, tt, :, :], ACT.Exp).then_inc(exped.sem, 1)
                for i in range(2 * TT):
                    keep_bands(b, i)
                keep_o(b)

            keep_x_disp(0, first=True)
            keep_v(0, 0)
            batches(act, body, tail)

        @block.vector
        def _(dve):
            C["weights"](dve, tag)
            dve.wait_ge(set_up, 5)
            dve.wait_ge(pos_ready, 1)
            dve.tensor_copy(pos[:, :], PS[:, 0, 0:64]).then_inc(pos_kept, 1)
            dve.tensor_scalar(b_half[:, :], W["b_out"], 0.5, None, ALU.mult).then_inc(pos_kept, 1)
            dve.wait_ge(pos_kept, 2)
            dve.wait_ge(zeroed, 16 * 2 * TT)

            def project(b, par):
                dve.wait_ge(a_ready.sem, a_ready.at(b, 1))
                dve.tensor_copy(a_pad[:, par, :, W1:W1 + T], PS[:, 6:8, :]).then_inc(a_kept.sem, 1)
                dve.wait_ge(d_ready.sem, d_ready.at(b, 1))
                dve.tensor_copy(d_pad[:, par, :, W1:W1 + T], PS[:, 4:6, :]).then_inc(d_kept.sem, 1)

            def soften(b, tt):
                dve.wait_ge(turned.sem, turned.at(b, tt + 1))
                dve.wait_ge(skewed[tt].sem, skewed[tt].at(b, 0))
                src = PS[:, 4 + 2 * (tt % 2):6 + 2 * (tt % 2), :]
                if tt == 0:
                    dve.tensor_tensor(masked[:, :, :], src, W["mask"].rearrange("p (g c) -> p g c", g=2), ALU.add)\
                       .then_inc(masked_ready.sem, 1)
                    dve.wait_ge(masked_ready.sem, masked_ready.at(b, 1))
                    dve.wait_ge(summed.sem, summed.at(b, 0))
                    src = masked[:, :, :]
                if tt >= 1:
                    dve.wait_ge(centred.sem, centred.at(b, tt))
                by_head = src.rearrange("p g (d h) -> p g h d", h=H)
                dve.tensor_reduce(mx[:, :].rearrange("p (g h) -> p g h", g=2), by_head, AX, ALU.max)\
                   .then_inc(maxed.sem, 1)
                dve.wait_ge(maxed.sem, maxed.at(b, tt + 1))
                for g in range(2):
                    m = dve.tensor_tensor(probs[:, tt, 8 * g:8 * g + 8, :],
                                          src[:, g, :].rearrange("p (d h) -> p h d", h=H),
                                          mx[:, 8 * g:8 * g + 8].rearrange("p (h o) -> p h o", o=1)
                                          .to_broadcast([P, H, 64]), ALU.subtract)
                m.then_inc(centred.sem, 1)

            def sums(b, tt):
                dve.wait_ge(exped.sem, exped.at(b, TT))
                if tt == 0:
                    dve.wait_ge(inverted.sem, inverted.at(b, 0))
                dve.tensor_reduce(tot[:, tt, :], probs[:, tt, :, :], AX, ALU.add).then_inc(summed.sem, 1)

            def invert(b):
                dve.wait_ge(summed.sem, summed.at(b, TT))
                dve.wait_ge(o_scaled.sem, o_scaled.at(b, 0))
                dve.reciprocal(rtot[:, :, :], tot[:, :, :]).then_inc(inverted.sem, 1)

            def scale(b, tt):
                dve.wait_ge(pv_done.sem, pv_done.at(b, tt + 1))
                if tt == 0:
                    dve.wait_ge(inverted.sem, inverted.at(b, 1))
                    dve.wait_ge(o_turned.sem, o_turned.at(b, 0))
                dve.tensor_tensor(o_tok[:, tt, :].rearrange("p (h e) -> p h e", e=8),
                                  PS[:, 4 + tt % 2, 0:P].rearrange("p (h e) -> p h e", e=8),
                                  rtot[:, tt, :].rearrange("p (h o) -> p h o", o=1).to_broadcast([P, 16, 8]),
                                  ALU.mult).then_inc(o_scaled.sem, 1)

            def finish(b):
                dve.wait_ge(projected.sem, projected.at(b, 1))
                dve.tensor_tensor(Y[:, b, :], X[:, b, :], PS[:, 4, :], ALU.add).then_inc(y_done.sem, 1)

            def to_logit(b, par, gq):
                dve.wait_ge(bond_used.sem, bond_used.at(b, 4 * gq + 4))
                dve.wait_ge(tanh_ready.sem, tanh_ready.at(b, gq + 1))
                dve.scalar_tensor_tensor(logit[:, par, gq, :], tanh[:, gq % 2, :], -5.0, PS[:, gq % 2, :],
                                         ALU.mult, ALU.add).then_inc(logit_ready.sem, 1)

            def body(b, par, before, after):
                dve.wait_ge(a_kept.sem, a_kept.at(b, 1))
                dve.wait_ge(d_kept.sem, d_kept.at(b, 1))
                for n in range(NCH):
                    g, q, k = chunk(n)
                    if n >= RING:
                        dve.wait_ge(bond_used.sem, bond_used.at(b, n - RING + 1))
                    elif before is not None:
                        dve.wait_ge(bond_used.sem, bond_used.at(before, min(NCH, NCH - 1 + n)))
                    for c in range(4):
                        d = 16 * q + 4 * c + k
                        m = dve.scalar_tensor_tensor(bond[:, n % RING, c, :], a_pad[:, par, g, d:d + T],
                                                     pos[:, d:d + 1], a_pad[:, par, g, W1:W1 + T],
                                                     ALU.add, ALU.subtract)
                    m.then_inc(bond_in.sem, 1)
                    if by_dve(n):
                        dve.wait_ge(dmg_used.sem, dmg_used.at(b, n - RING + 1))
                        damage(dve, par, n).then_inc(dmg_in_dve.sem, 1)
                    if n == 3 and before is not None:
                        to_logit(before, 1 - par, 7)
                    elif k == 3 and n > 3:
                        to_logit(b, par, n // 4 - 1)
                    if n == 4 and after is not None:
                        project(after, 1 - par)
                    if before is not None:
                        if n in SOFTEN_DVE:
                            soften(before, SOFTEN_DVE[n])
                        if n in SUMS:
                            sums(before, SUMS[n])
                        if n == 22:
                            invert(before)
                        if n in SCALE:
                            scale(before, SCALE[n])
                        if n == 31:
                            finish(before)

            def tail(b, par):
                to_logit(b, par, 7)
                for tt in range(TT):
                    soften(b, tt)
                for tt in range(TT):
                    sums(b, tt)
                invert(b)
                for tt in range(TT):
                    scale(b, tt)
                finish(b)

            project(0, 0)
            batches(dve, body, tail)


def attn2(nc, tag, X, Y, PS, C, W):
    with ExitStack() as ctx:
        s = Stage(nc, ctx)
        q_sb = s.sb(f"{tag}_q", [P, T])
        v_sb = s.sb(f"{tag}_v", [P, T])
        sq = s.sb(f"{tag}_sq", [P, 2, T])
        kv = s.sb(f"{tag}_kv", [P, T])
        scaled = s.sb(f"{tag}_scaled", [P, T])
        norm = s.sb(f"{tag}_norm", [P, 8])
        rnorm = s.sb(f"{tag}_rnorm", [P, 8])
        feat = s.sb(f"{tag}_feat", [P, 1])
        projected = s.sig(f"{tag}_projected", 1)
        squared = s.sig(f"{tag}_squared", 2)
        copied = s.sig(f"{tag}_copied", 2)
        summed = s.sig(f"{tag}_summed", 1)
        norm_ready = s.sig(f"{tag}_norm_ready", 1)
        clipped = s.sig(f"{tag}_clipped", 1)
        rnorm_ready = s.sig(f"{tag}_rnorm_ready", 1)
        spread = s.sig(f"{tag}_spread", 1)
        kv_ready = s.sig(f"{tag}_kv_ready", 1)
        feat_ready = s.sig(f"{tag}_feat_ready", 1)
        scaled_ready = s.sig(f"{tag}_scaled_ready", 1, ahead=1)
        done = s.sig(f"{tag}_done", 1, ahead=1)
        block = ctx.enter_context(nc.Block())

        @block.tensor
        def _(pe):
            C["weights"](pe, tag)
            with pe.Fori(0, NB) as b:
                pe.wait_ge(done.sem, done.at(b, 0))
                for n, name in enumerate(("q", "k", "v")):
                    mm = pe.matmul(PS[:, n, :], W[name], X[:, b, :], start=True, stop=True)
                mm.then_inc(projected.sem, 1)
                for n in range(2):
                    pe.wait_ge(squared.sem, squared.at(b, n + 1))
                    for t in range(TT):
                        mm = pe.matmul(PS[:, 3, 4 * n + t:4 * n + t + 1], sq[:, n, bass.ts(t, P)],
                                       W["ones"][:, 0:1], start=True, stop=True)
                mm.then_inc(summed.sem, 1)
                pe.wait_ge(rnorm_ready.sem, rnorm_ready.at(b, 1))
                for n in range(2):
                    for t in range(TT):
                        col = 4 * n + t
                        mm = pe.matmul(PS[:, 4 + n, bass.ts(t, P)], rnorm[:, col:col + 1].to_broadcast([P, P]),
                                       C["ident"], start=True, stop=True)
                mm.then_inc(spread.sem, 1)

        @block.scalar
        def _(act):
            with act.Fori(0, NB) as b:
                act.wait_ge(done.sem, done.at(b, 0))
                act.wait_ge(projected.sem, projected.at(b, 1))
                for n in range(2):
                    act.activation(sq[:, n, :], PS[:, n, :], ACT.Square).then_inc(squared.sem, 1)
                act.activation(v_sb[:, :], PS[:, 2, :], ACT.Copy).then_inc(copied.sem, 1)
                act.activation(q_sb[:, :], PS[:, 0, :], ACT.Copy).then_inc(copied.sem, 1)
                act.wait_ge(summed.sem, summed.at(b, 1))
                act.activation(norm[:, :], PS[:, 3, 0:8], ACT.Sqrt).then_inc(norm_ready.sem, 1)

        @block.vector
        def _(dve):
            dve.sem_inc(scaled_ready.sem, 1)
            dve.sem_inc(done.sem, 1)
            with dve.Fori(0, NB) as b:
                dve.wait_ge(projected.sem, projected.at(b, 1))
                dve.wait_ge(copied.sem, copied.at(b, 1))
                dve.wait_ge(squared.sem, squared.at(b, 2))
                dve.tensor_tensor(kv[:, :], PS[:, 1, :], v_sb[:, :], ALU.mult).then_inc(kv_ready.sem, 1)
                dve.wait_ge(norm_ready.sem, norm_ready.at(b, 1))
                dve.tensor_scalar(norm[:, :], norm[:, :], 1e-12, None, ALU.max).then_inc(clipped.sem, 1)
                dve.wait_ge(clipped.sem, clipped.at(b, 1))
                dve.reciprocal(rnorm[:, :], norm[:, :]).then_inc(rnorm_ready.sem, 1)
                dve.wait_ge(spread.sem, spread.at(b, 1))
                dve.wait_ge(kv_ready.sem, kv_ready.at(b, 1))
                dve.wait_ge(scaled_ready.sem, scaled_ready.at(b, 0))
                dve.wait_ge(done.sem, done.at(b, 0))
                dve.scalar_tensor_tensor(scaled[:, :], kv[:, :], 1.0 / T, PS[:, 5, :], ALU.mult, ALU.mult,
                                         accum_out=feat[:, :]).then_inc(feat_ready.sem, 1)
                dve.wait_ge(feat_ready.sem, feat_ready.at(b, 1))
                dve.wait_ge(copied.sem, copied.at(b, 2))
                dve.scalar_tensor_tensor(scaled[:, :], q_sb[:, :], feat[:, 0:1], PS[:, 4, :], ALU.mult, ALU.mult)\
                   .then_inc(scaled_ready.sem, 1)
                dve.wait_ge(scaled_ready.sem, scaled_ready.at(b, 1))
                dve.tensor_tensor(Y[:, b, :], scaled[:, :], X[:, b, :], ALU.add).then_inc(done.sem, 1)


def local_ffn(nc, tag, X, Y, PS, C, W):
    HID_T = 3
    HALVES = 2 * TT
    LANES = 2
    with ExitStack() as ctx:
        s = Stage(nc, ctx)

        def bufs(name, shape):
            return [s.sb(f"{tag}_{name}{g}", shape) for g in range(LANES)]

        def sigs(name, per):
            return [s.sig(f"{tag}_{name}{g}", per) for g in range(LANES)]

        z = bufs("z", [P, T])
        h = bufs("h", [P, T])
        v = bufs("v", [P, TT, T])
        qk = bufs("qk", [P, 8, T])
        norm = bufs("norm", [P, TT * 16])
        rnorm = bufs("rnorm", [P, TT * 16])
        rnorm8 = bufs("rnorm8", [P, TT * 16])
        rnorm_t = bufs("rnorm_t", [16, T])
        mx = bufs("mx", [P, 4])
        nmx = bufs("nmx", [P, 4])
        tot = bufs("tot", [P, 2, 4])
        rtot = bufs("rtot", [P, 4])
        probs = bufs("probs", [P, 8, 2 * P])
        probs_t = bufs("probs_t", [P, 4, 2, P])
        o = bufs("o", [P, 4, T])
        std = bufs("std", [P, TT])
        rstd = bufs("rstd", [P, TT])
        hn = bufs("hn", [P, T])
        rot = [o[g][:, 0:2, :] for g in range(LANES)]
        sq = [o[g][:, 2:4, :] for g in range(LANES)]
        gated = [qk[g][:, 0:HID_T, :] for g in range(LANES)]
        gelu = [qk[g][:, 4:4 + HID_T, :] for g in range(LANES)]
        set_up = s.sem(f"{tag}_set_up")
        shifted = sigs("shifted", 2)
        v_ready = sigs("v_ready", TT)
        v_kept = sigs("v_kept", TT)
        proj_ready = sigs("proj_ready", 8)
        squared = sigs("squared", 8)
        sq_used = sigs("sq_used", 2)
        rot1 = sigs("rot1", 8)
        rot2 = sigs("rot2", 8)
        rotated = sigs("rotated", 8)
        norm_ready = sigs("norm_ready", 1)
        norm_turned = sigs("norm_turned", 1)
        clipped = sigs("clipped", 1)
        rnorm_ready = sigs("rnorm_ready", 1)
        rnorm8_ready = sigs("rnorm8_ready", 1)
        rnorm_turned = sigs("rnorm_turned", 1)
        rnorm_t_kept = sigs("rnorm_t_kept", 1)
        rnorm_spread = sigs("rnorm_spread", 4)
        k_ready = sigs("k_ready", 4)
        scored = sigs("scored", HALVES)
        maxed = sigs("maxed", HALVES)
        negated = sigs("negated", HALVES)
        exped = sigs("exped", HALVES)
        inverted = sigs("inverted", HALVES)
        probs_ready = sigs("probs_ready", HALVES)
        turned = sigs("turned", HALVES)
        turned_kept = sigs("turned_kept", HALVES)
        pv_done = sigs("pv_done", HALVES)
        o_kept = sigs("o_kept", HALVES)
        attn_out = sigs("attn_out", 1)
        z_mid = sigs("z_mid", 1)
        shifted_mid = sigs("shifted_mid", 2)
        mean_ready = sigs("mean_ready", 1)
        centred = sigs("centred", 1)
        sq_mid = sigs("sq_mid", 1)
        var_ready = sigs("var_ready", 1)
        eps_added = sigs("eps_added", 1)
        std_ready = sigs("std_ready", 1)
        rstd_ready = sigs("rstd_ready", 1)
        rstd_spread = sigs("rstd_spread", 1)
        scaled = sigs("scaled", 1)
        hn_ready = sigs("hn_ready", 1)
        hidden = sigs("hidden", HID_T)
        gelu_ready = sigs("gelu_ready", HID_T)
        gated_ready = sigs("gated_ready", HID_T)
        ffn_out = sigs("ffn_out", 1)
        done = [s.sig(f"{tag}_done{g}", 1, ahead=1) for g in range(LANES)]
        summed = sigs("summed", 1)
        block = ctx.enter_context(nc.Block())

        def w(l, name):
            return W[f"{name}{l}"]

        def head(n, sl):
            return 4 * (n % 2) + 2 * (sl % 2) + sl // 2

        def keys(tt):
            return (slice(0, P), slice(P, 2 * P)) if tt == 0 else (slice(tt * P - 64, (tt + 1) * P), slice(64, 2 * P))

        def square_of(g, i):
            if i % 4 < 2:
                return sq[g][:, i % 4, :]
            a = i % 4 - 2
            return probs_t[g][:, 2 * a:2 * a + 2, :, :].rearrange("p h k i -> p (h k i)")

        def probs_of(g, n):
            return probs[g][:, 4 * (n % 2):4 * (n % 2) + 4, :]

        @block.gpsimd
        def _(pool):
            for g in range(LANES):
                pool.memset(h[g][64:P, 0:1], 0.0).then_inc(set_up, 1)
                pool.wait_ge(set_up, 2 * g + 1)
                pool.memset(probs[g][:, :, 0:64], 0.0).then_inc(set_up, 1)
                pool.wait_ge(set_up, 2 * g + 2)
            with pool.Fori(0, NB // LANES) as c:
                for l in range(2):
                    t = c * 2 + l
                    for i in range(8):
                        for g in range(LANES):
                            pool.wait_ge(rot1[g].sem, rot1[g].at(t, i + 1))
                            pool.wait_ge(rot2[g].sem, rot2[g].at(t, i + 1))
                            pool.tensor_tensor(qk[g][:, i, :], rot[g][:, 0, :], rot[g][:, 1, :], ALU.add)\
                                .then_inc(rotated[g].sem, 1)

        @block.tensor
        def _(pe):
            C["weights"](pe, tag)

            def bank(g, n):
                return PS[:, 4 * g + n, :]

            def norm_sums(g, t, n):
                pe.wait_ge(squared[g].sem, squared[g].at(t, 4 * n + 4))
                for i in range(4):
                    mm = pe.matmul(PS[32 * i:32 * i + 32, 4 * g + 2, :], W["head_sum"][:, bass.ts(n, 32)],
                                   square_of(g, 4 * n + i), start=(n == 0), stop=(n == 1))
                mm.then_inc(sq_used[g].sem, 1)

            def scores(g, t, n):
                tt = n // 2
                js, cols = keys(tt)
                if n == 0:
                    pe.wait_ge(k_ready[g].sem, k_ready[g].at(t, 4))
                    pe.wait_ge(rotated[g].sem, rotated[g].at(t, 8))
                else:
                    pe.wait_ge(exped[g].sem, exped[g].at(t, n))
                for sl in range(4):
                    hd = head(n, sl)
                    strip = slice(64 * (hd % 2), 64 * (hd % 2) + 64)
                    out = bank(g, sl // 2)[:, (sl % 2) * 256:(sl % 2) * 256 + 256][:, cols]
                    pe.matmul(out, qk[g][strip, hd // 2, bass.ts(tt, P)], qk[g][strip, 4 + hd // 2, js],
                              start=True, stop=False)
                    mm = pe.matmul(out, C["ident_bf"], W["mask"][:, cols], start=False, stop=True)
                mm.then_inc(scored[g].sem, 1)

            def turn(g, t, n):
                pe.wait_ge(probs_ready[g].sem, probs_ready[g].at(t, n + 1))
                if n >= 1:
                    pe.wait_ge(o_kept[g].sem, o_kept[g].at(t, n))
                for hd in range(4):
                    for kt in range(0 if n >= 2 else 1, 2):
                        at = (hd * 2 + kt) * P
                        mm = pe.transpose(bank(g, 2 + at // T)[:, at % T:at % T + P],
                                          probs_of(g, n)[:, hd, bass.ts(kt, P)], C["ident"])
                mm.then_inc(turned[g].sem, 1)

            def pv(g, t, n):
                tt = n // 2
                pe.wait_ge(turned_kept[g].sem, turned_kept[g].at(t, n + 1))
                kts = range(0 if tt else 1, 2)
                for sl in range(4):
                    hd = head(n, sl)
                    rows = slice(64 * (hd % 2), 64 * (hd % 2) + 64)
                    for kt in kts:
                        mm = pe.matmul(PS[rows, 4 * g + 2, bass.ts(hd // 2 % 2, P)],
                                       v[g][:, tt - 1 + kt, bass.ts(hd, 64)], probs_t[g][:, sl, kt, :],
                                       start=(kt == kts[0]), stop=(kt == 1))
                mm.then_inc(pv_done[g].sem, 1)

            def ffn_down(g, t, l, i):
                pe.wait_ge(gated_ready[g].sem, gated_ready[g].at(t, i + 1))
                mm = pe.matmul(bank(g, 2), w(l, "w2")[:, bass.ts(i, P)], gated[g][:, i, :],
                               start=(i == 0), stop=(i == HID_T - 1))
                if i == HID_T - 1:
                    mm.then_inc(ffn_out[g].sem, 1)

            lanes = range(LANES)
            with pe.Fori(0, NB // LANES) as c:
                for l in range(2):
                    t = c * 2 + l
                    for st in range(TT):
                        for g in lanes:
                            if st == 0:
                                pe.wait_ge(shifted[g].sem, shifted[g].at(t, 2))
                            if st == 1:
                                pe.wait_ge(done[g].sem, done[g].at(t, 0))
                            if st >= 2:
                                pe.wait_ge(v_kept[g].sem, v_kept[g].at(t, st - 1))
                            pe.matmul(bank(g, 3 - st % 2), h[g][:, bass.ts(st, P)], w(l, "v"), start=True, stop=True)\
                              .then_inc(v_ready[g].sem, 1)
                    for i in range(8):
                        if i == 4:
                            for g in lanes:
                                pe.wait_ge(v_kept[g].sem, v_kept[g].at(t, TT))
                                norm_sums(g, t, 0)
                        for g in lanes:
                            if i >= 1:
                                pe.wait_ge(rot1[g].sem, rot1[g].at(t, i))
                                pe.wait_ge(rot2[g].sem, rot2[g].at(t, i))
                                pe.wait_ge(squared[g].sem, squared[g].at(t, i))
                            pe.matmul(bank(g, 0), w(l, "qk")[:, bass.ts(i, P)], h[g][:, :], start=True, stop=True)
                            pe.matmul(bank(g, 1), w(l, "qk_sw")[:, bass.ts(i, P)], h[g][:, :], start=True, stop=True)\
                              .then_inc(proj_ready[g].sem, 1)
                    for g in lanes:
                        norm_sums(g, t, 1)
                    for g in lanes:
                        pe.wait_ge(norm_ready[g].sem, norm_ready[g].at(t, 1))
                        for tt in range(TT):
                            mm = pe.transpose(bank(g, 3)[:, bass.ts(tt, P)], hn[g][:, bass.ts(tt, P)], C["ident"])
                        mm.then_inc(norm_turned[g].sem, 1)
                    for g in lanes:
                        pe.wait_ge(rnorm_ready[g].sem, rnorm_ready[g].at(t, 1))
                        for tt in range(TT):
                            mm = pe.transpose(bank(g, 3)[0:16, bass.ts(tt, P)], rnorm[g][:, bass.ts(tt, 16)], C["ident"])
                        mm.then_inc(rnorm_turned[g].sem, 1)
                    for i in range(4):
                        for g in lanes:
                            if i == 0:
                                pe.wait_ge(rnorm_t_kept[g].sem, rnorm_t_kept[g].at(t, 1))
                                pe.wait_ge(rot1[g].sem, rot1[g].at(t, 8))
                                pe.wait_ge(rot2[g].sem, rot2[g].at(t, 8))
                            if i >= 2:
                                pe.wait_ge(k_ready[g].sem, k_ready[g].at(t, i - 1))
                            pe.matmul(bank(g, i % 2), W["head_bc"][:, bass.ts(i, P)], rnorm_t[g][:, :],
                                      start=True, stop=True).then_inc(rnorm_spread[g].sem, 1)
                    for g in lanes:
                        scores(g, t, 0)
                    for n in range(HALVES):
                        if n + 1 < HALVES:
                            for g in lanes:
                                scores(g, t, n + 1)
                        for g in lanes:
                            turn(g, t, n)
                        for g in lanes:
                            pv(g, t, n)
                    for g in lanes:
                        pe.wait_ge(o_kept[g].sem, o_kept[g].at(t, HALVES))
                        for i in range(4):
                            mm = pe.matmul(bank(g, 0), w(l, "wo")[:, bass.ts(i, P)], o[g][:, i, :],
                                           start=(i == 0), stop=(i == 3))
                        mm.then_inc(attn_out[g].sem, 1)
                    for g in lanes:
                        pe.wait_ge(shifted_mid[g].sem, shifted_mid[g].at(t, 2))
                        pe.matmul(bank(g, 1), C["inv_d"], h[g][:, :], start=True, stop=True).then_inc(mean_ready[g].sem, 1)
                    for g in lanes:
                        pe.wait_ge(sq_mid[g].sem, sq_mid[g].at(t, 1))
                        for tt in range(TT):
                            mm = pe.matmul(bank(g, 2)[:, tt:tt + 1], sq[g][:, 0, bass.ts(tt, P)], C["inv_d"][:, 0:1],
                                           start=True, stop=True)
                        mm.then_inc(var_ready[g].sem, 1)
                    for g in lanes:
                        pe.wait_ge(rstd_ready[g].sem, rstd_ready[g].at(t, 1))
                        for tt in range(TT):
                            mm = pe.matmul(bank(g, 3)[:, bass.ts(tt, P)], rstd[g][:, tt:tt + 1].to_broadcast([P, P]),
                                           C["ident"], start=True, stop=True)
                        mm.then_inc(rstd_spread[g].sem, 1)
                    for i in range(HID_T):
                        for g in lanes:
                            if i == 0:
                                pe.wait_ge(hn_ready[g].sem, hn_ready[g].at(t, 1))
                            else:
                                pe.wait_ge(gated_ready[g].sem, gated_ready[g].at(t, i))
                            pe.matmul(bank(g, 0), w(l, "w1a")[:, bass.ts(i, P)], hn[g][:, :], start=True, stop=True)
                            pe.matmul(bank(g, 1), w(l, "w1g")[:, bass.ts(i, P)], hn[g][:, :],
                                      start=True, stop=True).then_inc(hidden[g].sem, 1)
                        if i >= 1:
                            for g in lanes:
                                ffn_down(g, t, l, i - 1)
                    for g in lanes:
                        ffn_down(g, t, l, HID_T - 1)

        @block.scalar
        def _(act):
            C["weights"](act, tag)

            def bank(g, n):
                return PS[:, 4 * g + n, :]

            def exps(g, t, n):
                tt = n // 2
                js, cols = keys(tt)
                act.wait_ge(negated[g].sem, negated[g].at(t, n + 1))
                if n >= 2:
                    act.wait_ge(turned[g].sem, turned[g].at(t, n - 1))
                for sl in range(4):
                    hd = tt * 16 + head(n, sl) // 2 * 4 + head(n, sl) % 2
                    a = act.activation(probs_of(g, n)[:, sl, cols],
                                       bank(g, sl // 2)[:, (sl % 2) * 256:(sl % 2) * 256 + 256][:, cols], ACT.Exp,
                                       bias=nmx[g][:, sl:sl + 1], scale=rnorm8[g][:, hd:hd + 1],
                                       accum_out=tot[g][:, n % 2, sl:sl + 1])
                a.then_inc(exped[g].sem, 1)

            lanes = range(LANES)
            with act.Fori(0, NB // LANES) as c:
                for l in range(2):
                    t = c * 2 + l
                    for st in range(TT):
                        for g in lanes:
                            act.wait_ge(v_ready[g].sem, v_ready[g].at(t, st + 1))
                            act.activation(v[g][:, st, :], bank(g, 3 - st % 2), ACT.Copy).then_inc(v_kept[g].sem, 1)
                    for i in range(8):
                        for g in lanes:
                            act.wait_ge(proj_ready[g].sem, proj_ready[g].at(t, i + 1))
                            if i == 4:
                                act.wait_ge(sq_used[g].sem, sq_used[g].at(t, 1))
                            act.activation(square_of(g, i), bank(g, 0), ACT.Square).then_inc(squared[g].sem, 1)
                    for g in lanes:
                        act.wait_ge(sq_used[g].sem, sq_used[g].at(t, 2))
                        act.activation(hn[g][:, :], bank(g, 2), ACT.Sqrt).then_inc(norm_ready[g].sem, 1)
                    for g in lanes:
                        act.wait_ge(rnorm_turned[g].sem, rnorm_turned[g].at(t, 1))
                        act.activation(rnorm_t[g][:, :], bank(g, 3)[0:16, :], ACT.Copy).then_inc(rnorm_t_kept[g].sem, 1)
                    for g in lanes:
                        exps(g, t, 0)
                    for n in range(1, HALVES):
                        for g in lanes:
                            exps(g, t, n)
                    for g in lanes:
                        act.wait_ge(centred[g].sem, centred[g].at(t, 1))
                        act.activation(sq[g][:, 0, :], hn[g][:, :], ACT.Square).then_inc(sq_mid[g].sem, 1)
                    for g in lanes:
                        act.wait_ge(eps_added[g].sem, eps_added[g].at(t, 1))
                        act.activation(std[g][:, :], std[g][:, :], ACT.Sqrt).then_inc(std_ready[g].sem, 1)
                    for i in range(HID_T):
                        for g in lanes:
                            act.wait_ge(hidden[g].sem, hidden[g].at(t, i + 1))
                            act.activation(gelu[g][:, i, :], bank(g, 1), ACT.Gelu,
                                           bias=w(l, "b1g")[:, i:i + 1]).then_inc(gelu_ready[g].sem, 1)

        @block.vector
        def _(dve):
            C["weights"](dve, tag)
            for g in range(LANES):
                dve.sem_inc(done[g].sem, 1)
            dve.wait_ge(set_up, 2 * LANES)
            cos, sin = W["cos"], W["sin"]

            def bank(g, n):
                return PS[:, 4 * g + n, :]

            def shift(g, src, sig):
                dve.tensor_copy(h[g][0:64, :], src[0:64, :]).then_inc(sig[g].sem, 1)
                dve.tensor_copy(h[g][64:P, 1:T], src[64:P, 0:T - 1]).then_inc(sig[g].sem, 1)

            def maxima(g, t, n):
                tt = n // 2
                js, cols = keys(tt)
                dve.wait_ge(scored[g].sem, scored[g].at(t, n + 1))
                src = PS[:, 4 * g:4 * g + 2, :].rearrange("p a (h j) -> p (a h) j", j=256)[:, :, cols]
                dve.tensor_reduce(mx[g][:, :], src, AX, ALU.max).then_inc(maxed[g].sem, 1)
                dve.wait_ge(maxed[g].sem, maxed[g].at(t, n + 1))
                at = tt * 16 + 8 * (n % 2)
                rn = rnorm8[g][:, at:at + 8].rearrange("p (y w) -> p w y", w=4)[:, 0:2, :]
                dve.scalar_tensor_tensor(nmx[g][:, :].rearrange("p (x y) -> p x y", x=2),
                                         mx[g][:, :].rearrange("p (x y) -> p x y", x=2), -1.0, rn,
                                         ALU.mult, ALU.mult).then_inc(negated[g].sem, 1)

            def normalise(g, t, n):
                js, cols = keys(n // 2)
                dve.wait_ge(exped[g].sem, exped[g].at(t, n + 1))
                dve.reciprocal(rtot[g][:, :], tot[g][:, n % 2, :]).then_inc(inverted[g].sem, 1)
                dve.wait_ge(inverted[g].sem, inverted[g].at(t, n + 1))
                pr = probs_of(g, n)[:, :, cols]
                dve.tensor_tensor(pr, pr, rtot[g][:, :].rearrange("p (h o) -> p h o", o=1)
                                  .to_broadcast([P, 4, cols.stop - cols.start]), ALU.mult)\
                   .then_inc(probs_ready[g].sem, 1)

            def keep_turned(g, t, n):
                dve.wait_ge(turned[g].sem, turned[g].at(t, n + 1))
                if n >= 1:
                    dve.wait_ge(pv_done[g].sem, pv_done[g].at(t, n))
                src = PS[:, 4 * g + 2:4 * g + 4, :].rearrange("p a (h k i) -> p (a h) k i", k=2, i=P)
                lo = 0 if n >= 2 else 1
                dve.tensor_copy(probs_t[g][:, :, lo:2, :], src[:, :, lo:2, :]).then_inc(turned_kept[g].sem, 1)

            def keep_o(g, t, n):
                dve.wait_ge(pv_done[g].sem, pv_done[g].at(t, n + 1))
                dve.tensor_copy(o[g][:, 2 * (n % 2):2 * (n % 2) + 2, bass.ts(n // 2, P)],
                                bank(g, 2)[:, 0:2 * P].rearrange("p (i q) -> p i q", i=2)).then_inc(o_kept[g].sem, 1)

            lanes = range(LANES)
            def body(c, last=False):
                for l in range(2):
                    t = c * 2 + l
                    if l == 1:
                        for g in lanes:
                            dve.wait_ge(done[g].sem, done[g].at(t, 0))
                            shift(g, z[g], shifted)
                    for i in range(8):
                        for g in lanes:
                            dve.wait_ge(proj_ready[g].sem, proj_ready[g].at(t, i + 1))
                            if i >= 1:
                                dve.wait_ge(rotated[g].sem, rotated[g].at(t, i))
                            qs = w(l, "q_scale") if i < 4 else w(l, "k_scale")
                            tab = slice(0, T) if i < 4 else slice(T, 2 * T)
                            dve.scalar_tensor_tensor(rot[g][:, 1, :], bank(g, 1), qs[:, 1:2], sin[:, tab],
                                                     ALU.mult, ALU.mult).then_inc(rot2[g].sem, 1)
                            dve.wait_ge(squared[g].sem, squared[g].at(t, i + 1))
                            dve.scalar_tensor_tensor(rot[g][:, 0, :], bank(g, 0), qs[:, 0:1], cos[:, tab],
                                                     ALU.mult, ALU.mult).then_inc(rot1[g].sem, 1)
                    for g in lanes:
                        dve.wait_ge(norm_turned[g].sem, norm_turned[g].at(t, 1))
                        dve.tensor_scalar(norm[g][:, :].rearrange("p (tc w) -> p tc w", w=4),
                                          bank(g, 3).rearrange("p (tc w) -> p tc w", w=32)[:, :, 0:4],
                                          1e-12, None, ALU.max).then_inc(clipped[g].sem, 1)
                        dve.wait_ge(clipped[g].sem, clipped[g].at(t, 1))
                        dve.reciprocal(rnorm[g][:, :], norm[g][:, :]).then_inc(rnorm_ready[g].sem, 1)
                        dve.wait_ge(rnorm_ready[g].sem, rnorm_ready[g].at(t, 1))
                        dve.tensor_scalar(rnorm8[g][:, :], rnorm[g][:, :], 8.0, None, ALU.mult)\
                           .then_inc(rnorm8_ready[g].sem, 1)
                    for i in range(4):
                        for g in lanes:
                            if i == 0:
                                dve.wait_ge(rotated[g].sem, rotated[g].at(t, 8))
                            dve.wait_ge(rnorm_spread[g].sem, rnorm_spread[g].at(t, i + 1))
                            dve.tensor_tensor(qk[g][:, 4 + i, :], qk[g][:, 4 + i, :], bank(g, i % 2), ALU.mult)\
                               .then_inc(k_ready[g].sem, 1)
                    for g in lanes:
                        dve.wait_ge(rnorm8_ready[g].sem, rnorm8_ready[g].at(t, 1))
                        maxima(g, t, 0)
                    for g in lanes:
                        normalise(g, t, 0)
                    for n in range(HALVES):
                        if n + 1 < HALVES:
                            for g in lanes:
                                maxima(g, t, n + 1)
                        for g in lanes:
                            keep_turned(g, t, n)
                        if n + 1 < HALVES:
                            for g in lanes:
                                normalise(g, t, n + 1)
                        for g in lanes:
                            keep_o(g, t, n)
                    for g in lanes:
                        dve.wait_ge(attn_out[g].sem, attn_out[g].at(t, 1))
                        before = z[g] if l else X[:, c * 2 + g, :]
                        dve.tensor_tensor(z[g][:, :], before[:, :], bank(g, 0), ALU.add).then_inc(z_mid[g].sem, 1)
                        dve.wait_ge(z_mid[g].sem, z_mid[g].at(t, 1))
                        shift(g, z[g], shifted_mid)
                    for g in lanes:
                        dve.wait_ge(mean_ready[g].sem, mean_ready[g].at(t, 1))
                        dve.wait_ge(shifted_mid[g].sem, shifted_mid[g].at(t, 2))
                        dve.tensor_tensor(hn[g][:, :], h[g][:, :], bank(g, 1), ALU.subtract).then_inc(centred[g].sem, 1)
                    for g in lanes:
                        dve.wait_ge(var_ready[g].sem, var_ready[g].at(t, 1))
                        dve.tensor_scalar(std[g][:, :], bank(g, 2)[:, 0:TT], 1e-5, None, ALU.add)\
                           .then_inc(eps_added[g].sem, 1)
                    for g in lanes:
                        dve.wait_ge(std_ready[g].sem, std_ready[g].at(t, 1))
                        dve.reciprocal(rstd[g][:, :], std[g][:, :]).then_inc(rstd_ready[g].sem, 1)
                    for g in lanes:
                        dve.wait_ge(rstd_spread[g].sem, rstd_spread[g].at(t, 1))
                        dve.wait_ge(sq_mid[g].sem, sq_mid[g].at(t, 1))
                        dve.scalar_tensor_tensor(hn[g][:, :], hn[g][:, :], w(l, "ln_g"), bank(g, 3), ALU.mult, ALU.mult)\
                           .then_inc(scaled[g].sem, 1)
                        dve.wait_ge(scaled[g].sem, scaled[g].at(t, 1))
                        dve.tensor_scalar(hn[g][:, :], hn[g][:, :], w(l, "ln_b"), None, ALU.add)\
                           .then_inc(hn_ready[g].sem, 1)
                    if l == 1 and not last:
                        for g in lanes:
                            dve.wait_ge(mean_ready[g].sem, mean_ready[g].at(t, 1))
                            dve.wait_ge(centred[g].sem, centred[g].at(t, 1))
                            shift(g, X[:, c * 2 + LANES + g, :], shifted)
                    for i in range(HID_T):
                        for g in lanes:
                            dve.wait_ge(gelu_ready[g].sem, gelu_ready[g].at(t, i + 1))
                            dve.scalar_tensor_tensor(gated[g][:, i, :], bank(g, 0), w(l, "b1a")[:, i:i + 1],
                                                     gelu[g][:, i, :], ALU.add, ALU.mult).then_inc(gated_ready[g].sem, 1)
                    for g in lanes:
                        dve.wait_ge(ffn_out[g].sem, ffn_out[g].at(t, 1))
                        dve.scalar_tensor_tensor(z[g][:, :], bank(g, 2), w(l, "b2"), z[g][:, :], ALU.add, ALU.add)\
                           .then_inc(done[g].sem, 1)
                    if l == 1:
                        for g in lanes:
                            dve.wait_ge(done[g].sem, done[g].at(t, 1))
                            dve.tensor_tensor(Y[:, c * 2 + g, :], X[:, c * 2 + g, :], z[g][:, :], ALU.add)\
                               .then_inc(summed[g].sem, 1)
                            dve.wait_ge(summed[g].sem, summed[g].at(c, 1))

            for g in lanes:
                shift(g, X[:, g, :], shifted)
            with dve.Fori(0, NB // LANES - 1) as c:
                body(c)
            body(NB // LANES - 1, last=True)




class Pack:

    def __init__(self):
        self.items, self.cols = [], 0

    def add(self, name, array):
        self.items.append((name, array, self.cols))
        self.cols += array.shape[1]

    def data(self, dtype):
        out = np.zeros((P, self.cols), dtype)
        for _, a, at in self.items:
            out[:a.shape[0], at:at + a.shape[1]] = a
        return out


def moe_sel(sizes, dtype):
    units = np.concatenate([np.full(n, e) for e, n in enumerate(sizes)])
    nt = -(-len(units) // P)
    sel = np.zeros((96, nt * P), dtype)
    for part in range(3):
        sel[32 * part + units, np.arange(len(units))] = 1
    return sel


def tiles_of(w, nt):
    out = np.zeros((nt * P, w.shape[1]), w.dtype)
    out[:w.shape[0]] = w
    return out.reshape(nt, P, w.shape[1]).transpose(1, 0, 2).reshape(P, -1)


def padded(w, cols):
    out = np.zeros((w.shape[0], cols), w.dtype)
    out[:, :w.shape[1]] = w
    return out


def lay_out(a, bf):
    fs, bs = {}, {}

    def stage(name):
        fs[name], bs[name] = Pack(), Pack()
        return fs[name], bs[name]

    f, h = stage("const")
    f.add("inv_d", np.full((P, P), 1.0 / P, np.float32))
    f.add("ident", np.eye(P, dtype=np.float32))
    h.add("ident_bf", np.eye(P).astype(bf))

    f, h = stage("m0")
    E, D, F = a["L0_ffn_Wg"].shape
    nt = (E * F + 128) // P
    f.add("router", a["L0_ffn_Wr"])
    f.add("bias", np.tile(a["L0_ffn_expert_bias"], (P, 1)))
    f.add("gate", np.concatenate([a["L0_ffn_Wg"].transpose(1, 0, 2).reshape(D, -1), a["L0_ffn_Sg"]], 1))
    f.add("up", np.concatenate([a["L0_ffn_Wu"].transpose(1, 0, 2).reshape(D, -1), a["L0_ffn_Su"]], 1))
    f.add("down", tiles_of(np.concatenate([a["L0_ffn_Wd"].reshape(-1, D), a["L0_ffn_Sd"]], 0), nt))
    h.add("sel", moe_sel([F] * E + [128], bf))

    f, h = stage("m1")
    gu = a["L1_ffn_experts_gate_up"]
    E, I = gu.shape[0], gu.shape[1] // 2
    SI = a["L1_ffn_shared_gate_w"].shape[0]
    nt = -(-(E * I + SI) // P)
    f.add("router", np.concatenate([a["L1_ffn_gate_w"], a["L1_ffn_shared_expert_gate_w"]], 0).T)
    f.add("gate", padded(np.concatenate([gu[:, :I].reshape(-1, P), a["L1_ffn_shared_gate_w"]], 0).T, nt * P))
    f.add("up", padded(np.concatenate([gu[:, I:].reshape(-1, P), a["L1_ffn_shared_up_w"]], 0).T, nt * P))
    f.add("down", tiles_of(np.concatenate([a["L1_ffn_experts_down"].transpose(0, 2, 1).reshape(-1, P),
                                           a["L1_ffn_shared_down_w"].T], 0), nt))
    h.add("sel", moe_sel([I] * E + [SI], bf))

    f, h = stage("m2")
    E, D, I = a["L2_ffn_w1"].shape
    nt = E * I // P
    f.add("router", a["L2_ffn_gate_w"].T)
    f.add("bias", np.tile(a["L2_ffn_e_bias"], (P, 1)))
    f.add("gate", a["L2_ffn_w1"].transpose(1, 0, 2).reshape(D, -1))
    f.add("up", a["L2_ffn_w3"].transpose(1, 0, 2).reshape(D, -1))
    f.add("down", tiles_of(a["L2_ffn_w2"].reshape(-1, D), nt))
    h.add("sel", moe_sel([I] * E, bf))
    more_layout(a, bf, stage)
    return fs, bs


def strips(heads, D, SW, bf):
    out = np.zeros((P, 2, 3, len(heads), P), bf)
    for g, hs in enumerate(heads):
        for j, h in enumerate(hs):
            for term, parts in enumerate(TERMS):
                for e in range(D):
                    for n in range(2):
                        out[h * D + e, n, parts[n], g, j * SW + term * D + e] = 1
    return out.reshape(P, -1)


def attn_common(f, h, D, SW, heads, bf):
    ones, strip = np.zeros((2, P, P // SW), np.float32)
    for j in range(P // SW):
        ones[j * SW + 6 * D:j * SW + 6 * D + 3, j] = 1
        strip[j * SW:(j + 1) * SW, j] = 1
    f.add("ones_rows", ones)
    f.add("strip_rows", strip)
    h.add("strips", strips(heads, D, SW, bf))
    pick_o, pick_sum = np.zeros((P, 32), np.float32), np.zeros((P, 32), np.float32)
    for j in range(4):
        for e in range(8):
            pick_o[32 * j + e, 8 * j + e] = 1
            pick_sum[32 * j + 8, 8 * j + e] = 1
    f.add("pick_o", pick_o)
    f.add("pick_sum", pick_sum)


def more_layout(a, bf, stage):
    f, h = stage("a1")
    w = a["L1_attn_w_qkv"]
    f.add("q", w[:, :P])
    f.add("k", w[:, P:2 * P])
    f.add("v", w[:, 2 * P:])
    f.add("out", a["L1_attn_w_out"])
    f.add("b_out", a["L1_attn_b_out"][:, None])
    attn_common(f, h, 8, 64, [[2 * g, 2 * g + 1] for g in range(8)], bf)
    mask = np.where(np.arange(P)[None, :] > np.arange(P)[:, None], -1e10, 0.0)
    h.add("mask", mask.astype(bf))
    h.add("mask_t", np.ascontiguousarray(mask.T).astype(bf))

    f, h = stage("a3")
    f.add("q", a["L3_attn_Wq"])
    f.add("k", a["L3_attn_Wk"])
    swap = np.arange(P) ^ 1
    f.add("q_sw", a["L3_attn_Wq"][:, swap])
    f.add("k_sw", a["L3_attn_Wk"][:, swap])
    f.add("v", a["L3_attn_Wv"])
    f.add("out", a["L3_attn_Wo"])
    attn_common(f, h, 4, 32, [[2 * (4 * (g % 4) + j) + g // 4 for j in range(4)] for g in range(8)], bf)
    pos = np.arange(T, dtype=np.float32)[:, None]
    freq = np.float32(1.0) / np.float32(0.0001) ** (np.float32(2.0) * np.arange(2, dtype=np.float32) / np.float32(4))
    ang = (pos * freq.astype(np.float32)).astype(np.float32)
    pair = (np.arange(P) % 4) // 2
    cos = np.cos(ang).astype(np.float32).T[pair]
    sin = np.sin(ang).astype(np.float32).T[pair] * np.where(np.arange(P) % 2 == 0, -1, 1)[:, None]
    f.add("cos", np.concatenate([cos * 0.5, cos], 1).astype(np.float32))
    f.add("sin", np.concatenate([sin * 0.5, sin], 1).astype(np.float32))
    f.add("lam_q", np.tile(np.concatenate([a["L3_attn_lambda_q1"], a["L3_attn_lambda_q2"]]), (P, 1)))
    f.add("lam_k", np.tile(np.concatenate([a["L3_attn_lambda_k1"], a["L3_attn_lambda_k2"]]), (P, 1)))
    f.add("subln", np.tile(a["L3_attn_subln_g"], 16)[:, None])
    f.add("eps", np.full((P, 1), 1e-5, np.float32))
    mean8 = np.kron(np.eye(16, dtype=np.float32), np.full((8, 8), 1 / 8, np.float32))
    f.add("mean8", mean8)
    rest_layout(a, bf, stage)


def rest_layout(a, bf, stage):
    f, h = stage("a2")
    for name, w in (("q", "W_q"), ("k", "W_k"), ("v", "W_v")):
        f.add(name, a[f"L2_attn_{w}"].T)
    f.add("ones", np.ones((P, 1), np.float32))

    f, h = stage("f3")
    wqkv = a["L3_ffn_wqkv"]
    swap = np.arange(512) // 64 * 64 + (np.arange(512) % 64 + 32) % 64
    swap64 = (np.arange(64) + 32) % 64
    for l in range(2):
        q, k, v = wqkv[l][:, :512], wqkv[l][:, 512:1024], wqkv[l][:, 1024:]
        f.add(f"qk{l}", np.concatenate([q, k], 1))
        f.add(f"qk_sw{l}", np.concatenate([q[:, swap], k[:, swap]], 1))
        f.add(f"v{l}", v)
        for name, key in (("q_scale", "L3_ffn_q_scale"), ("k_scale", "L3_ffn_k_scale")):
            sc = a[key][l]
            f.add(f"{name}{l}", np.stack([np.tile(sc, 2), np.tile(sc[swap64], 2)], 1))
        f.add(f"wo{l}", tiles_of(a["L3_ffn_wo"][l], 4))
        f.add(f"ln_g{l}", a["L3_ffn_ln_g"][l][:, None])
        f.add(f"ln_b{l}", a["L3_ffn_ln_b"][l][:, None])
        hid = a["L3_ffn_w2"].shape[1]
        w1, b1 = a["L3_ffn_w1"][l], a["L3_ffn_b1"][l][None]
        f.add(f"w1a{l}", padded(w1[:, :hid], 3 * P))
        f.add(f"w1g{l}", padded(w1[:, hid:], 3 * P))
        f.add(f"b1a{l}", padded(b1[:, :hid], 3 * P).reshape(3, P).T)
        f.add(f"b1g{l}", padded(b1[:, hid:], 3 * P).reshape(3, P).T)
        f.add(f"w2{l}", tiles_of(a["L3_ffn_w2"][l], 3))
        f.add(f"b2{l}", a["L3_ffn_b2"][l][:, None])
    head_sum, head_bc = np.zeros((P, 2, 32), np.float32), np.zeros((16, 4, P), np.float32)
    for c in range(P):
        for n in range(2):
            head_sum[c, n, 2 * n + c // 64] = 1
        for i in range(4):
            head_bc[4 * i + 2 + c // 64, i, c] = 1
    f.add("head_sum", head_sum.reshape(P, -1))
    f.add("head_bc", head_bc.reshape(16, -1))
    half = np.arange(0, 64, 2, dtype=np.float32)
    inv = (np.float32(1.0) / np.float32(10000.0) ** (half / np.float32(64))).astype(np.float32)
    t = np.arange(T, dtype=np.float32)
    fr = (t[:, None] * inv[None]).astype(np.float32)
    base = ((half + np.float32(0.4 * 64)) / np.float32(1.4 * 64)).astype(np.float32)
    power = ((t - T // 2) / np.float32(32)).astype(np.float32)
    sc = (base[None] ** power[:, None]).astype(np.float32)
    row = np.arange(P) % 32
    sign = np.where(np.arange(P) % 64 < 32, -1, 1)[:, None].astype(np.float32)
    cos, sin, sc = np.cos(fr).T[row], np.sin(fr).T[row] * sign, sc.T[row]
    f.add("cos", np.concatenate([cos * sc, cos / sc], 1).astype(np.float32))
    f.add("sin", np.concatenate([sin * sc, sin / sc], 1).astype(np.float32))
    j = np.arange(2 * P)[None, :] - P
    i = np.arange(P)[:, None]
    h.add("mask", np.where((i < j) | (i > j + 64), -BIG, 0.0).astype(bf))
    first_layout(a, bf, stage)


def first_layout(a, bf, stage):
    f, h = stage("a0")
    f.add("disp", a["L0_attn_W_disp"])
    f.add("val", a["L0_attn_W_val"])

    def blocks(w):
        out = np.zeros((8, 16, 8, 16), np.float32)
        for i in range(8):
            out[i, :, i, :] = w
        return out.reshape(P, P)

    f.add("strain", blocks(a["L0_attn_W_strain"]))
    f.add("dmg", blocks(a["L0_attn_W_dmg"]))
    f.add("w_pos", np.tile(a["L0_attn_W_pos"], (1, 8)))
    f.add("rel", a["L0_attn_rel_pos_emb"].T)
    f.add("b_dmg", np.tile(a["L0_attn_b_dmg"], 8)[:, None])
    f.add("b_out", np.tile(a["L0_attn_b_dmg_out"], P)[:, None])
    for name, key in (("w_bond", "L0_attn_W_bond"), ("w_dmg_out", "L0_attn_W_dmg_out")):
        out = np.zeros((8, 16, 4, 4, 8), np.float32)
        for k in range(4):
            for i in range(8):
                out[i, :, k, k, i] = a[key][:, 0]
        f.add(name, out.reshape(P, P))
    f.add("c_proj", a["L0_attn_W_cproj"])
    d = (np.arange(T) // 8)[None, :]
    m = np.where(np.arange(P)[:, None] - 63 + d < 0, -BIG, 0.0).astype(np.float32)
    f.add("mask", np.concatenate([m, m], 1))


def build(nc, x_d, out_d, f_d, b_d, fs, bs, stages):
    Stage.CLEARED = []
    with ExitStack() as top:
        X = top.enter_context(nc.sbuf_tensor("X", [P, NB, T], F32))
        Y = top.enter_context(nc.sbuf_tensor("Y", [P, NB, T], F32))
        PS = top.enter_context(nc.psum_tensor("PS", [P, NB, T], F32))
        x_loaded = top.enter_context(nc.semaphore("x_loaded"))
        stored = top.enter_context(nc.semaphore("stored"))

        def load(eng, name):
            wf, wb, sem, _ = bufs[name]
            eng.dma_start(wf[:, :], f_d[name]).then_inc(sem, 16)
            if name in b_d:
                eng.dma_start(wb[:, :], b_d[name]).then_inc(sem, 16)

        def weights(eng, name):
            eng.wait_ge(bufs[name][2], 32 if name in b_d else 16)

        def hold(ctx, name):
            wf = ctx.enter_context(nc.sbuf_tensor(f"w_{name}", [P, fs[name].cols], F32))
            wb = ctx.enter_context(nc.sbuf_tensor(f"wb_{name}", [P, max(bs[name].cols, 1)], BF16))
            sem = top.enter_context(nc.semaphore(f"{name}_weights"))
            views = {k: wf[0:v.shape[0], at:at + v.shape[1]] for k, v, at in fs[name].items}
            views |= {k: wb[0:v.shape[0], at:at + v.shape[1]] for k, v, at in bs[name].items}
            bufs[name] = (wf, wb, sem, views)
            return views

        scratch = nc.dram_tensor("scratch", (TT * 16 * 2 * 64 * P,), F32, kind="Internal").ap()
        first, last = stages
        bufs = {}
        C = dict(hold(top, "const"), weights=weights, load=load)

        names = ("a0", "m0", "a1", "m1", "a2", "m2", "a3", "f3")
        held = ExitStack()
        views = hold(held, names[first])

        with ExitStack() as ctx:
            block = ctx.enter_context(nc.Block())

            @block.sync
            def _(sp):
                sp.dma_start(X[:, :, :], x_d.rearrange("p (b t) -> p b t", b=NB)).then_inc(x_loaded, 16)
                load(sp, "const")
                load(sp, names[first])
                sp.wait_ge(x_loaded, 16)
                weights(sp, "const")

        stage_of = {
            "a0": lambda w: attn0(nc, "a0", X, Y, PS, C, w, scratch),
            "m0": lambda w: moe(nc, "m0", X, Y, PS, C, w, "top_softmax", 8, 2, 5),
            "a1": lambda w: attn(nc, "a1", X, Y, PS, C, w, True),
            "m1": lambda w: moe(nc, "m1", X, Y, PS, C, w, "softmax_top", 8, 2, 14),
            "a2": lambda w: attn2(nc, "a2", X, Y, PS, C, w),
            "m2": lambda w: moe(nc, "m2", X, Y, PS, C, w, "sigmoid_top", 32, 4, 24),
            "a3": lambda w: attn(nc, "a3", X, Y, PS, C, w, False),
            "f3": lambda w: local_ffn(nc, "f3", X, Y, PS, C, w),
        }
        for n in range(first, last + 1):
            stage_of[names[n]](views)
            held.close()
            following = names[n + 1] if n < last else None
            if following:
                views = hold(held, following)
            layernorm(nc, f"ln{n}", X, Y, PS, C, following)
        with ExitStack() as ctx:
            block = ctx.enter_context(nc.Block())

            @block.sync
            def _(sp):
                sp.dma_start(out_d.rearrange("p (b t) -> p b t", b=NB), X[:, :, :]).then_inc(stored, 16)
                sp.wait_ge(stored, 16)


def kernel(**inputs):
    import ml_dtypes
    import concourse.bacc as bacc
    from concourse.bass_utils import run_bass_kernel_spmd

    bf = ml_dtypes.bfloat16
    a = {k: np.asarray(v) for k, v in inputs.items()}
    x = np.ascontiguousarray(a["L0_attn_x"].reshape(NB * T, P).T)
    fs, bs = lay_out(a, bf)
    nc = bacc.Bacc("TRN2", target_bir_lowering=False, num_devices=1)
    arrays = {"x_dram": x}
    f_d, b_d = {}, {}
    x_d = nc.dram_tensor("x_dram", x.shape, F32, kind="ExternalInput").ap()
    for name in fs:
        arrays[f"{name}_f_dram"] = fs[name].data(np.float32)
        f_d[name] = nc.dram_tensor(f"{name}_f_dram", (P, fs[name].cols), F32, kind="ExternalInput").ap()
        if bs[name].cols:
            arrays[f"{name}_b_dram"] = bs[name].data(bf)
            b_d[name] = nc.dram_tensor(f"{name}_b_dram", (P, bs[name].cols), BF16, kind="ExternalInput").ap()
    out_d = nc.dram_tensor("out_dram", (P, NB * T), F32, kind="ExternalOutput").ap()
    build(nc, x_d, out_d, f_d, b_d, fs, bs, STAGES)
    r = run_bass_kernel_spmd(nc, [arrays], core_ids=[0])
    return np.ascontiguousarray(r.results[0]["out_dram"].T).reshape(NB, T, P)
```
